# Optimizing a Trainium2 kernel written in Bass

```python
import numpy as np
import jax
import jax.numpy as jnp

def _softmax(x, axis=-1):
    return jax.nn.softmax(x, axis=axis)

def _gelu(x):
    return jax.nn.gelu(x, approximate=True)

def _silu(x):
    return jax.nn.silu(x)

def _sigmoid(x):
    return jax.nn.sigmoid(x)

def _layernorm(x, axis=-1, eps=1e-05):
    m = jnp.mean(x, axis=axis, keepdims=True)
    v = jnp.var(x, axis=axis, keepdims=True)
    return (x - m) / jnp.sqrt(v + eps)

def _scatter_add(tgt, idx, src, axis=0):
    return tgt.at[idx].add(src)

def _segment_sum(src, seg, n):
    return jax.ops.segment_sum(src, seg, n)
kernel_name = 'mk_audio_tower_d1_tok_audfeat768_r4_2f3e78'

def setup_inputs(seed: int=0):
    np.random.seed(seed)
    _w = jnp.asarray

    def _rec_inputs():
        import jax
        import jax.numpy as jnp
        _rk = jax.random.key(seed)
        x = -0.000183583 + 0.999963 * jax.random.normal(jax.random.fold_in(_rk, 1), (4, 750, 192), jnp.float32)
        return x
    x = _rec_inputs()

    def _L0_tok_setup():
        import jax, jax.numpy as jnp
        import numpy as np
        KEEP_RATIO = 0.7
        LN_EPS = 1e-05
        key = jax.random.key(seed)
        k1, k2 = jax.random.split(key)
        B, N, D = (16, 2048, 192)
        x = jax.random.normal(k1, (B, N, D), dtype=jnp.float32)
        gamma = jnp.ones((D,), dtype=jnp.float32)
        beta = jnp.zeros((D,), dtype=jnp.float32)
        w = jax.random.normal(k2, (D,), dtype=jnp.float32) * (1.0 / np.sqrt(D))
        b = jnp.zeros((1,), dtype=jnp.float32)
        return {'x': x, 'gamma': gamma, 'beta': beta, 'w': w, 'b': b}
    _L0_tok_all = _L0_tok_setup()
    _L0_tok_in = {k: v for k, v in _L0_tok_all.items() if k in ('gamma', 'beta', 'w', 'b')}
    del _L0_tok_all

    def _L0_attn_setup():
        import math
        import jax, jax.numpy as jnp
        import numpy as np
        D_MODEL = 192
        N_HEAD = 12
        HEAD_DIM = D_MODEL // N_HEAD
        ROPE_BASE = 10000.0
        EPS = 1e-06

        def rotary_cache(seq_len, head_dim, base=ROPE_BASE):
            half = head_dim // 2
            freq = 1.0 / base ** (jnp.arange(half, dtype=jnp.float32) / half)
            freqs = jnp.arange(seq_len, dtype=jnp.float32)[:, None] * freq[None, :]
            return (jnp.cos(freqs), jnp.sin(freqs))

        def apply_rope(x, cos, sin):
            cos = cos.astype(x.dtype)
            sin = sin.astype(x.dtype)
            x1 = x[..., ::2]
            x2 = x[..., 1::2]
            out = jnp.stack((x1 * cos - x2 * sin, x1 * sin + x2 * cos), axis=-1)
            return out.reshape(x.shape)
        key = jax.random.key(seed)
        kx, kq, kk, kv, kp = jax.random.split(key, 5)
        B, S, D = (2, 512, D_MODEL)
        x = jax.random.normal(kx, (B, S, D), dtype=jnp.float32)
        scale = 0.02
        Wq = jax.random.normal(kq, (D, D), dtype=jnp.float32) * scale
        Wk = jax.random.normal(kk, (D, D), dtype=jnp.float32) * scale
        Wv = jax.random.normal(kv, (D, D), dtype=jnp.float32) * scale
        Wproj = jax.random.normal(kp, (D, D), dtype=jnp.float32) * scale
        return {'x': x, 'Wq': Wq, 'Wk': Wk, 'Wv': Wv, 'Wproj': Wproj}
    _L0_attn_all = _L0_attn_setup()
    _L0_attn_in = {k: v for k, v in _L0_attn_all.items() if k in ('Wq', 'Wk', 'Wv', 'Wproj')}
    del _L0_attn_all

    def _L0_ffn_setup():
        import jax, jax.numpy as jnp
        import numpy as np
        B, T, DM, DF, E, K = (4, 256, 192, 768, 8, 2)
        key = jax.random.key(seed)
        k0, k1, k2, k3 = jax.random.split(key, 4)
        x = jax.random.normal(k0, (B, T, DM), jnp.float32)
        Wg = jax.random.normal(k1, (DM, E), jnp.float32) * 0.02
        W1 = jax.random.normal(k2, (E, DM, DF), jnp.float32) * 0.02
        b1 = jnp.zeros((E, DF), jnp.float32)
        W2 = jax.random.normal(k3, (E, DF, DM), jnp.float32) * 0.02
        b2 = jnp.zeros((E, DM), jnp.float32)
        return {'x': x, 'Wg': Wg, 'W1': W1, 'b1': b1, 'W2': W2, 'b2': b2}
    _L0_ffn_all = _L0_ffn_setup()
    _L0_ffn_in = {k: v for k, v in _L0_ffn_all.items() if k in ('Wg', 'W1', 'b1', 'W2', 'b2')}
    del _L0_ffn_all
    return {'x': x, 'L0_tok_gamma': _L0_tok_in['gamma'], 'L0_tok_beta': _L0_tok_in['beta'], 'L0_tok_w': _L0_tok_in['w'], 'L0_tok_b': _L0_tok_in['b'], 'L0_attn_Wq': _L0_attn_in['Wq'], 'L0_attn_Wk': _L0_attn_in['Wk'], 'L0_attn_Wv': _L0_attn_in['Wv'], 'L0_attn_Wproj': _L0_attn_in['Wproj'], 'L0_ffn_Wg': _L0_ffn_in['Wg'], 'L0_ffn_W1': _L0_ffn_in['W1'], 'L0_ffn_b1': _L0_ffn_in['b1'], 'L0_ffn_W2': _L0_ffn_in['W2'], 'L0_ffn_b2': _L0_ffn_in['b2']}

def reference(x, L0_tok_gamma, L0_tok_beta, L0_tok_w, L0_tok_b, L0_attn_Wq, L0_attn_Wk, L0_attn_Wv, L0_attn_Wproj, L0_ffn_Wg, L0_ffn_W1, L0_ffn_b1, L0_ffn_W2, L0_ffn_b2):
    import jax
    import jax.numpy as jnp

    def _L0_tok_ref(x, gamma, beta, w, b):
        import jax, jax.numpy as jnp
        import numpy as np
        KEEP_RATIO = 0.7
        LN_EPS = 1e-05
        B, N, D = x.shape
        mu = jnp.mean(x, axis=-1, keepdims=True)
        var = jnp.mean(jnp.square(x - mu), axis=-1, keepdims=True)
        xn = (x - mu) * jax.lax.rsqrt(var + LN_EPS) * gamma + beta
        scores = jnp.einsum('bnd,d->bn', xn, w) + b[0]
        k = int(N * KEEP_RATIO)
        _, idx = jax.lax.top_k(scores, k)
        x_kept = jnp.take_along_axis(x, idx[..., None], axis=1)
        return x_kept

    def _L0_attn_ref(x, Wq, Wk, Wv, Wproj):
        import math
        import jax, jax.numpy as jnp
        import numpy as np
        D_MODEL = 192
        N_HEAD = 12
        HEAD_DIM = D_MODEL // N_HEAD
        ROPE_BASE = 10000.0
        EPS = 1e-06

        def rotary_cache(seq_len, head_dim, base=ROPE_BASE):
            half = head_dim // 2
            freq = 1.0 / base ** (jnp.arange(half, dtype=jnp.float32) / half)
            freqs = jnp.arange(seq_len, dtype=jnp.float32)[:, None] * freq[None, :]
            return (jnp.cos(freqs), jnp.sin(freqs))

        def apply_rope(x, cos, sin):
            cos = cos.astype(x.dtype)
            sin = sin.astype(x.dtype)
            x1 = x[..., ::2]
            x2 = x[..., 1::2]
            out = jnp.stack((x1 * cos - x2 * sin, x1 * sin + x2 * cos), axis=-1)
            return out.reshape(x.shape)
        B, S, D = x.shape
        H, hd = (N_HEAD, HEAD_DIM)

        def heads(W):
            return (x @ W.T).reshape(B, S, H, hd).transpose(0, 2, 1, 3)
        q, k, v = (heads(Wq), heads(Wk), heads(Wv))
        cos, sin = rotary_cache(S, hd)
        cos = cos[None, None]
        sin = sin[None, None]
        q = apply_rope(q, cos, sin)
        k = apply_rope(k, cos, sin)
        scores = jnp.einsum('bhsd,bhtd->bhst', q.astype(jnp.float32), k.astype(jnp.float32))
        scores = scores / math.sqrt(hd)
        weights = jax.lax.erf(scores) + 1.0
        mask = jnp.tril(jnp.ones((S, S), dtype=bool))[None, None]
        weights = jnp.where(mask, weights, 0.0)
        denom = jnp.maximum(weights.sum(axis=-1, keepdims=True), EPS)
        y = jnp.einsum('bhst,bhtd->bhsd', weights, v.astype(jnp.float32)) / denom
        y = y.astype(v.dtype)
        y = y.transpose(0, 2, 1, 3).reshape(B, S, D)
        return y @ Wproj.T

    def _L0_ffn_ref(x, Wg, W1, b1, W2, b2):
        import jax, jax.numpy as jnp
        import numpy as np
        B, T, DM, DF, E, K = (4, 256, 192, 768, 8, 2)
        m = x.shape[-1]
        xs = x.reshape(-1, m)
        S = xs.shape[0]
        n_exp = W1.shape[0]
        logits = xs @ Wg
        probs = jax.nn.softmax(logits, axis=-1)
        topv, topi = jax.lax.top_k(probs, K)
        cw = topv / jnp.sum(topv, axis=-1, keepdims=True)
        combine_weights = cw.T
        eid_flat = topi.T.reshape(-1)
        dispatch_mask = jnp.argsort(eid_flat)
        e_sorted = eid_flat[dispatch_mask]
        dispatched = xs[dispatch_mask % S]
        expert_outputs = jnp.zeros_like(dispatched)
        for e in range(n_exp):
            sel = (e_sorted == e)[:, None].astype(dispatched.dtype)
            h = jax.nn.relu(dispatched @ W1[e] + b1[e])
            expert_outputs = expert_outputs + sel * (h @ W2[e] + b2[e])
        rerouted = jnp.zeros((S * K, m), expert_outputs.dtype).at[dispatch_mask].set(expert_outputs)
        rerouted = rerouted.reshape(K, S, m)
        combined = jnp.einsum('ks,ksm->sm', combine_weights, rerouted)
        return combined.reshape(x.shape).astype(x.dtype)
    h = _L0_tok_ref(x, L0_tok_gamma, L0_tok_beta, L0_tok_w, L0_tok_b)
    h = h + _L0_attn_ref(_layernorm(h, axis=-1), L0_attn_Wq, L0_attn_Wk, L0_attn_Wv, L0_attn_Wproj)
    h = h + _L0_ffn_ref(_layernorm(h, axis=-1), L0_ffn_Wg, L0_ffn_W1, L0_ffn_b1, L0_ffn_W2, L0_ffn_b2)
    return h

_drawn_inputs = setup_inputs


def setup_inputs(seed=0):
    import zlib

    import numpy as np

    out = dict(_drawn_inputs(seed))
    spreads = {'L0_tok_gamma': (1.0, 0.2),
     'L0_tok_beta': (0.0, 0.1),
     'L0_ffn_b1': (0.0, 0.298),
     'L0_ffn_b2': (0.0, 0.1)}
    factors = {'L0_attn_Wq': 8.0, 'L0_attn_Wk': 8.0, 'L0_attn_Wv': 3.789, 'L0_attn_Wproj': 3.858}
    for name, (base, spread) in spreads.items():
        noise = np.random.default_rng([zlib.crc32(name.encode()), seed]).standard_normal(out[name].shape)
        drawn = base * np.exp(spread * noise) if base else spread * noise
        out[name] = jnp.asarray(drawn.astype(out[name].dtype))
    for name, factor in factors.items():
        out[name] = (out[name] * factor).astype(out[name].dtype)
    return out
```

```python
from contextlib import ExitStack

import numpy as np

import concourse.bass as bass
from concourse import mybir

F32 = mybir.dt.float32
BF16 = mybir.dt.bfloat16
I32 = mybir.dt.int32
U32 = mybir.dt.uint32
ALU = mybir.AluOpType
ACT = mybir.ActivationFunctionType
AX = mybir.AxisListType

B, N, D = 4, 750, 192
KEEP = int(N * 0.7)
HEADS, HD = 12, 16
E, F = 8, 768
TIN, NIN = 125, 6
TOK, NT = 105, 5
C = D // 2
HALF = HD // 2
P = 128
NTA = B * NT
ROWS = B * KEEP
TILES = (2 * ROWS + E * (P - 1)) // P
LN_EPS = 1e-5
DEN_EPS = 1e-6

S0 = 115
PIECES = [(0, S0, KEEP - S0, 0), (1, 128, KEEP - 128, 410), (0, 0, S0, 807),
          (2, 256, KEEP - 256, 922), (3, 384, KEEP - 384, 1191)]
RUN = 1332
RUN0 = 512 - (KEEP - S0)
TAIL = KEEP - 512

D1, D2, D3 = 0.10836966378404583, -0.0026960067293568426, 4.653028531935965e-05
K0, K1 = 1.01124489655701, 1.274538823519078
MIX0 = 0.555126294782942
MIX1 = 1.0 - MIX0
SCORE_SCALE = 1.0 / HD ** 0.5

Q_BLOCKS = [0, 0, 0, 1, 1, 1, 2, 2]
K_BLOCKS = [0, 1, 2, 0, 1, 2, 0, 1]


def build_plan():
    plan = [("rank", b) for b in range(B)]
    plan += [("xT", 0), ("q", 0), ("k", 0), ("hi", 0), ("hi", 1), ("mid", 0), ("mid", 1), ("v", 0), ("tail", 0)]
    for b in range(B):
        for h in range(HEADS):
            plan.append(("head", b, h))
            if b and h == 1:
                plan += [("av", 3 * b - 1), ("v", b), ("tail", b), ("oT", 3 * b - 1)]
            if b and h == 2:
                plan.append(("yT", b - 1))
            if b and h == 3:
                plan += [("proj", b - 1), ("zT", b - 1)]
            if b and h == 4:
                plan.append(("logit", b - 1))
            if h == 5:
                plan.append(("av", 3 * b))
            if h == 6:
                plan.append(("oT", 3 * b))
                if b + 1 < B:
                    plan += [("xT", b + 1), ("q", b + 1)]
            if h == 7 and b + 1 < B:
                plan += [("k", b + 1), ("hi", 2 * b + 2)]
            if h == 8 and b + 1 < B:
                plan += [("mid", 2 * b + 2), ("hi", 2 * b + 3)]
            if h == 9:
                plan.append(("av", 3 * b + 1))
                if b + 1 < B:
                    plan.append(("mid", 2 * b + 3))
            if h == 10:
                plan.append(("oT", 3 * b + 1))
    b = B - 1
    plan += [("flush",), ("av", 3 * b + 2), ("oT", 3 * b + 2), ("yT", b), ("proj", b), ("zT", b), ("logit", b)]
    return plan


SLOTTED = ("rank", "xT", "q", "k", "v", "tail", "head", "oT", "yT", "proj", "zT", "logit")


def build_program(nc, x, gamma, beta, w, b_score, wqT, wkT, wvT, wpT, wg, w1, b1, w2, b2,
                  rope_cos, rope_sin, count, out):
    plan = build_plan()
    unit_of = {}
    for u in plan:
        if u[0] in SLOTTED:
            unit_of[u] = len(unit_of)
    nonlinear_of = {}
    for u in plan:
        if u[0] in ("tail", "head"):
            nonlinear_of[u] = len(nonlinear_of)

    ctx = ExitStack()
    with ctx:
        def sb(name, shape, dt=F32):
            return ctx.enter_context(nc.sbuf_tensor(name, shape, dt))

        def dram(name, shape, dt=F32):
            return nc.dram_tensor(name, shape, dt, kind="Internal").ap()

        def sem(name):
            return ctx.enter_context(nc.semaphore(name))

        sorted_d = dram("sorted_d", [B * N, 2 * D])
        parts_d = dram("parts_d", [B, 2, 6 * C, KEEP], BF16)
        disp_d = dram("disp_d", [TILES * P, D])
        res_d = dram("res_d", [TILES * P, D])

        arena = sb("arena", [P, 21504])
        g_area = sb("g_area", [P, 8 * RUN])
        hres = sb("hres", [TOK, NTA, D])
        z = sb("z", [TOK, NTA, D])
        x_sorted = sb("x_sorted", [TOK, NT, D])
        sq = sb("sq", [P, 2, RUN])
        cub = sb("cub", [P, 2, RUN])
        v_mix = sb("v_mix", [P, 2, NT, HEADS * (HD + 1)])
        v_mix5 = v_mix[:, :, :, :].rearrange("p m t (h d) -> p m t h d", h=HEADS)
        g_tail = sb("g_tail", [TAIL, 2, HEADS, TAIL])
        o_sb = sb("o_sb", [P, 2, KEEP])
        y_sb = sb("y_sb", [TOK, NT, D])
        yT = sb("yT", [C, 2, KEEP])
        wp_sb = sb("wp_sb", [C, 2, D])
        wg_sb = sb("wg_sb", [C, 2, E])
        ident = sb("ident", [P, P])
        later = sb("later", [TIN, TIN])
        before = sb("before", [TOK, TOK])
        ones = sb("ones", [P, P])
        count_sb = sb("count_sb", [P, TILES])
        small = sb("small", [P, 640])

        stack_w = HEADS * KEEP // 2
        def stack(par, qk):
            at = par * 12288 + qk * stack_w
            return arena[:, at:at + stack_w].bitcast(BF16)
        rot_c = arena[0:C, 6300:7350].rearrange("p (a s) -> p a s", a=2)
        rot_s = arena[0:C, 7350:8400].rearrange("p (a s) -> p a s", a=2)
        rot = arena[0:C, 8400:9450].rearrange("p (a s) -> p a s", a=2)
        parts = arena[0:C, 9450:11025].bitcast(BF16).rearrange("p (a b s) -> p a b s", a=3, b=2)
        xT = arena[0:C, 11025:12075].rearrange("p (c s) -> p c s", c=2)
        w1_sb = arena[:, 0:12288]
        cos_sb = arena[0:C, 18588:19113]
        sin_sb = arena[0:C, 19113:19638]
        wqk_sb = arena[0:C, 19638:20406].rearrange("p (q c t m) -> p q c t m", q=2, c=2, t=2)
        wv_sb = arena[0:C, 20406:20790].rearrange("p (c o) -> p c o", c=2)
        w2_sb = arena[:, 12288:21504]
        y1_g = arena[0:TOK, 0:NTA * D].rearrange("p (t d) -> p t d", t=NTA)
        y2_g = arena[0:TOK, 4096:4096 + NTA * D].rearrange("p (t d) -> p t d", t=NTA)

        xn = g_area[0:TIN, 0:24 * 384].rearrange("p (t d) -> p t d", t=B * NIN)
        zeros = g_area[:, 9216:9216 + 1280]
        sig = g_area[:, :].rearrange("p (h m s) -> p h m s", h=4, m=2)
        b2_bc = g_area[:, 0:1536]
        x_tile = g_area[:, 1536:2112].rearrange("p (r d) -> p r d", r=3)
        x_tT = g_area[0:C + 1, 2112:2624].rearrange("p (r c t) -> p r c t", r=2, c=2)
        hid = g_area[:, 2624:4160].rearrange("p (r f) -> p r f", r=2)
        hidT = g_area[:, 4160:5696].rearrange("p (r k t) -> p r k t", r=2, k=6)
        y_tile = g_area[:, 5696:6080].rearrange("p (r d) -> p r d", r=2)

        used = [0]

        def tiny(parts_, *dims, dt=F32):
            n = int(np.prod(dims))
            v = small[0:parts_, used[0]:used[0] + n]
            used[0] += n
            assert used[0] <= 640
            if dt is not F32:
                v = v.bitcast(dt)
            if len(dims) == 2:
                v = v.rearrange("p (a b) -> p a b", a=dims[0])
            return v

        stats = tiny(P, 6)
        mv = tiny(P, B * NIN, 2)
        var_e = tiny(P, B * NIN)
        rs = tiny(P, B * NIN)
        rs_t = tiny(P, B * NIN)
        score = tiny(P, B * NIN)
        cnt = tiny(P, B * NIN, 4)
        idx = tiny(P, B * NIN, dt=U32)
        konst = tiny(P, 2)
        den = tiny(P, NT, 4)
        mv2 = tiny(P, NTA, 2)
        logits = tiny(P, NTA, E)
        front = cub[0:TIN, 0, :]
        gw = front[:, 0:D]
        gam_bc = front[:, D:2 * D]
        bet_bc = front[:, 2 * D:3 * D]
        w_bc = front[:, 3 * D:4 * D]
        junk = front[:, 4 * D:5 * D]
        sdiag = cub[0:TIN, 1, 0:NIN * TIN].rearrange("p (t j) -> p t j", t=NIN)
        cmp_junk = sq[0:TIN, 0, 0:N]

        rused = [0]

        def late(*dims, dt=F32):
            n = int(np.prod(dims))
            v = sq[0:TOK, 0, :][:, rused[0]:rused[0] + n] if rused[0] + n <= RUN else None
            rused[0] += n
            if dt is not F32:
                v = v.bitcast(dt)
            if len(dims) == 2:
                v = v.rearrange("p (a b) -> p a b", a=dims[0])
            return v

        prob = late(NTA, E)
        cand = late(NTA, E)
        hot1 = late(NTA, E)
        hot2 = late(NTA, E)
        both = late(NTA, E)
        totals = late(E, NTA)
        run_tot = late(E, NTA)
        r20 = cub[0:TOK, 0, :]
        top1, top2, ind, sums, cw1, cw2 = (r20[:, 32 * i:32 * i + NTA] for i in range(6))
        pos1, pos2 = (r20[:, 192 + 32 * i:192 + 32 * i + NTA].bitcast(U32) for i in range(2))
        carry = r20[:, 256:256 + E * NTA].rearrange("p (e t) -> p e t", e=E)
        n_tiles = r20[:, 448:448 + E]
        n_int = r20[:, 464:464 + E].bitcast(I32)
        ends = r20[:, 480:480 + E]
        base = r20[:, 496:496 + E]
        tile_cmp = r20[:, 512:512 + TILES * E].rearrange("p (t e) -> p t e", e=E)
        eid_f = r20[:, 832:832 + TILES]
        eid = r20[:, 880:880 + TILES].bitcast(I32)
        posf = late(NTA, E)

        slots = [ctx.enter_context(nc.psum_tensor(f"slot{i}", [P, 1536], F32)) for i in range(2)]
        o_ps = ctx.enter_context(nc.psum_tensor("o_ps", [P, 1024], F32))

        def slot(u):
            return slots[unit_of[u] % 2]

        x_in = [sem(f"x_in{b}") for b in range(B)]
        row_in, w_in, zero_set, zero_out = sem("row_in"), sem("w_in"), sem("zero_set"), sem("zero_out")
        const_set, vec_step = sem("const_set"), sem("vec_step")
        diag_ready, idx_ready = sem("diag_ready"), sem("idx_ready")
        scattered = [sem(f"scattered{b}") for b in range(B)]
        x_loaded, h_loaded = ([sem(f"{n}{b}") for b in range(B)] for n in ("x_loaded", "h_loaded"))
        psum_full, slot_free = sem("psum_full"), [sem("slot_free0"), sem("slot_free1")]
        xT_ready, rope_mul, rotated, hi_ready, rest_ready, mid_ready, parts_ready = (
            sem("xT_ready"), sem("rope_mul"), sem("rotated"), sem("hi_ready"), sem("rest_ready"),
            sem("mid_ready"), sem("parts_ready"))
        parts_out, stack_in = sem("parts_out"), [sem("stack_in0"), sem("stack_in1")]
        v_ready, sq_ready, cub_ready, masked, sig_ready = (
            sem("v_ready"), sem("sq_ready"), sem("cub_ready"), sem("masked"), sem("sig_ready"))
        sq_used = sem("sq_used")
        pool_step = sem("pool_step")
        av_done, o_ready, y_ready, yT_ready, z_ready, zT_ready = (
            sem("av_done"), sem("o_ready"), sem("y_ready"), sem("yT_ready"), sem("z_ready"), sem("zT_ready"))
        w1_in, w2_in, b2_in = sem("w1_in"), sem("w2_in"), sem("b2_in")
        hot_ready, prefix_ready, pos_ready, dispatched = (
            sem("hot_ready"), sem("prefix_ready"), sem("pos_ready"), sem("dispatched"))
        ones_row = sem("ones_row")
        tile_in = [sem(f"tile_in{i}") for i in range(2)]
        tT_full, tT_ready, hid_full, hid_a, hid_b = (
            sem("tT_full"), sem("tT_ready"), sem("hid_full"), sem("hid_a"), sem("hid_b"))
        hT_full, hT_a, hT_b, y_full, y_out_ready = (
            sem("hT_full"), sem("hT_a"), sem("hT_b"), sem("y_full"), sem("y_out_ready"))
        y_out = [sem(f"y_out{i}") for i in range(2)]
        gathered, out_ready, out_done = sem("gathered"), sem("out_ready"), sem("out_done")

        def free_before(u):
            n = unit_of[u]
            return n % 2, n // 2

        def take_slot(eng, u):
            s, k = free_before(u)
            if k:
                eng.wait_ge(slot_free[s], k)

        def full(eng, u):
            eng.wait_ge(psum_full, unit_of[u] + 1)

        block = ctx.enter_context(nc.Block())

        @block.sync
        def _(sp):
            for b in range(B):
                sp.dma_start(xn[:, NIN * b:NIN * (b + 1), 0:D],
                             x[b].rearrange("(t p) d -> p t d", p=TIN)).then_inc(x_in[b], 16)
                if b == 0:
                    for dst, src in ((gam_bc, gamma), (bet_bc, beta), (w_bc, w)):
                        sp.dma_start(dst, src.rearrange("(a d) -> a d", a=1).broadcast_to([TIN, D])).then_inc(row_in, 16)
                    sp.dma_start(konst[0:TIN, 1:2], b_score.rearrange("(a d) -> a d", a=1).broadcast_to([TIN, 1])).then_inc(row_in, 16)
            for dst, src in ((wqk_sb[:, 0], wqT), (wqk_sb[:, 1], wkT), (wv_sb, wvT), (wp_sb[:, :, :], wpT),
                             (wg_sb[:, :, :], wg.rearrange("(c p) e -> p c e", c=2)), (cos_sb, rope_cos),
                             (sin_sb, rope_sin), (count_sb[:, :], count.rearrange("(a d) -> a d", a=1).broadcast_to([P, TILES]))):
                sp.dma_start(dst, src).then_inc(w_in, 16)
            sp.wait_ge(zero_set, 1)
            disp_flat = disp_d.rearrange("(p r) d -> p (r d)", p=P)
            for i in range(TILES * D // 1280):
                sp.dma_start(disp_flat[:, 1280 * i:1280 * (i + 1)], zeros).then_inc(zero_out, 16)

            def load_sorted(b):
                sp.wait_ge(scattered[b], 16 * NIN)
                rows = sorted_d[N * b:N * b + KEEP, :].rearrange("(t p) d -> p t d", p=TOK)
                if b:
                    sp.wait_ge(psum_full, unit_of[("xT", b - 1)] + 1)
                sp.dma_start(x_sorted[:, :, :], rows[:, :, D:2 * D]).then_inc(x_loaded[b], 16)
                sp.dma_start(hres[:, NT * b:NT * (b + 1), :], rows[:, :, 0:D]).then_inc(h_loaded[b], 16)

            def stack_parts(m):
                b, qk = m // 2, m % 2
                sp.wait_ge(parts_ready, m + 1)
                sp.dma_start(parts_d[b, qk].rearrange("(a m) s -> m a s", a=6),
                             parts.rearrange("p a b s -> p (a b) s")).then_inc(parts_out, 16)
                sp.wait_ge(parts_out, 16 * (m + 1))
                if b >= 2 and qk == 0:
                    sp.wait_ge(psum_full, unit_of[("head", b - 2, HEADS - 1)] + 1)
                rows = parts_d[b, qk].rearrange("m s -> (m s)").rearrange("(r x) -> r x", r=3 * HD)
                st = stack(b % 2, qk)
                for i, part in enumerate((Q_BLOCKS, K_BLOCKS)[qk]):
                    sp.dma_start(st[HD * i:HD * (i + 1), :], rows[HD * part:HD * (part + 1), :]).then_inc(stack_in[b % 2], 16)

            load_sorted(0)
            stack_parts(0)
            stack_parts(1)
            for b in range(1, B):
                load_sorted(b)
                stack_parts(2 * b)
                stack_parts(2 * b + 1)
            sp.wait_ge(psum_full, unit_of[("v", B - 1)] + 1)
            sp.dma_start(w1_sb[0:C, :].rearrange("p (e c f) -> p e c f", e=E, c=2)[:, :, 0], w1.rearrange("e (c p) f -> c p e f", c=2)[0]).then_inc(w1_in, 16)
            sp.dma_start(w1_sb[0:C, :].rearrange("p (e c f) -> p e c f", e=E, c=2)[:, :, 1], w1.rearrange("e (c p) f -> c p e f", c=2)[1]).then_inc(w1_in, 16)
            sp.dma_start(w1_sb[C:C + 1, :].rearrange("p (e c f) -> p e c f", e=E, c=2)[:, :, 1], b1.rearrange("(a e) f -> a e f", a=1)).then_inc(w1_in, 16)
            sp.wait_ge(psum_full, unit_of[("head", B - 1, HEADS - 1)] + 1)
            for e in range(E):
                sp.dma_start(w2_sb.rearrange("p (e k d) -> p e k d", e=E, k=6)[:, e],
                             w2[e].rearrange("(k p) d -> p k d", k=6)).then_inc(w2_in, 16)
            sp.wait_ge(av_done, 3 * B)
            sp.dma_start(b2_bc, b2.rearrange("(a e) d -> a (e d)", a=1).broadcast_to([P, E * D])).then_inc(b2_in, 16)
            sp.wait_ge(dispatched, 16 * 2 * NTA)

            def load_tile(par, row):
                sp.dma_start(x_tile[:, par, :], disp_d[bass.ds(row, P), :]).then_inc(tile_in[par], 16)

            for par in range(2):
                sp.sem_inc(y_out[par], 16)
            load_tile(0, 0)
            load_tile(1, P)
            with sp.Fori(0, TILES // 2 - 1) as j:
                for par in range(2):
                    sp.wait_ge(tT_full, 2 * j + par + 1)
                    load_tile(par, (2 * j + par + 2) * P)
                    sp.wait_ge(y_out_ready, 2 * j + par + 2)
                    sp.dma_start(res_d[bass.ds((2 * j + par) * P, P), :], y_tile[:, par, :]).then_inc(y_out[par], 16)
            for par in range(2):
                sp.wait_ge(y_out_ready, TILES + par)
                sp.dma_start(res_d[(TILES - 2 + par) * P:(TILES - 1 + par) * P, :], y_tile[:, par, :]).then_inc(y_out[par], 16)
            for b in range(B):
                sp.wait_ge(out_ready, b + 1)
                sp.dma_start(out[b].rearrange("(t p) d -> p t d", p=TOK), z[:, NT * b:NT * (b + 1), :]).then_inc(out_done, 16)
            sp.wait_ge(out_done, 16 * B)

        @block.gpsimd
        def _(g):
            step = [0]

            def link(ins):
                ins.then_inc(pool_step, 1)
                step[0] += 1
                g.wait_ge(pool_step, step[0])

            g.memset(zeros, 0.0).then_inc(zero_set, 1)
            g.memset(ones[:, :], 1.0)
            g.memset(ident[:, :], 0.0)
            g.memset(later[:, :], 1.0)
            link(g.memset(before[:, :], 1.0))
            g.affine_select(out=ident[:, :], in_=ident[:, :], compare_op=ALU.not_equal, fill=1.0, base=0,
                            pattern=[[-1, P]], channel_multiplier=1)
            g.affine_select(out=later[:, :], in_=later[:, :], compare_op=ALU.is_gt, fill=0.0, base=0,
                            pattern=[[-1, TIN]], channel_multiplier=1)
            link(g.affine_select(out=before[:, :], in_=before[:, :], compare_op=ALU.is_gt, fill=0.0, base=0,
                                 pattern=[[1, TOK]], channel_multiplier=-1))
            g.sem_inc(const_set, 1)
            for b in range(B):
                g.wait_ge(idx_ready, b + 1)
                for t in range(NIN * b, NIN * (b + 1)):
                    g.indirect_dma_start(sorted_d, bass.IndirectOffsetOnAxis(idx[0:TIN, t:t + 1], 0),
                                         xn[:, t, :], None).then_inc(scattered[b], 16)

            def rotate(m):
                g.wait_ge(rope_mul, m + 1)
                if m:
                    g.wait_ge(parts_out, 16 * m)
                g.tensor_tensor(rot[:, 0, :], rot_c[:, 0, :], rot_s[:, 1, :], ALU.subtract)
                g.tensor_tensor(rot[:, 1, :], rot_s[:, 0, :], rot_c[:, 1, :], ALU.add).then_inc(rotated, 1)

            def rest(m):
                g.wait_ge(hi_ready, m + 1)
                g.tensor_tensor(rot, rot, parts[:, 0], ALU.subtract).then_inc(rest_ready, 1)

            def low(m):
                g.wait_ge(mid_ready, m + 1)
                g.wait_ge(rest_ready, m + 1)
                g.tensor_tensor(parts[:, 2], rot, parts[:, 1], ALU.subtract).then_inc(parts_ready, 1)

            def mask(ap, first, groups=None, stride=1):
                pat = ([groups] if groups else []) + [[1, ap.shape[-1]]]
                return g.affine_select(out=ap, in_=ap, compare_op=ALU.is_ge, fill=-1e12, base=first,
                                       pattern=pat, channel_multiplier=-1)

            for u in plan:
                if u[0] in ("q", "k"):
                    m = 2 * u[1] + (u[0] == "k")
                    rotate(m)
                    rest(m)
                    low(m)
                elif u[0] in ("tail", "head"):
                    n = nonlinear_of[u]
                    g.wait_ge(cub_ready, n + 1)
                    c = cub[:, n % 2, :]
                    if u[0] == "tail":
                        mask(c[0:TAIL, 0:HEADS * TAIL].rearrange("p (h s) -> p h s", h=HEADS), 0, [0, HEADS]).then_inc(masked, 1)
                    else:
                        mask(c[:, 807:807 + S0], 0)
                        mask(c[:, 0:P - S0], S0)
                        mask(c[:, 410:410 + P], 0)
                        mask(c[:, 922:922 + P], 0)
                        mask(c[:, 1191:1191 + P], 0).then_inc(masked, 1)
            g.wait_ge(zero_out, 16 * (TILES * D // 1280))
            g.wait_ge(pos_ready, 1)
            for t in range(NTA):
                for pos in (pos1, pos2):
                    g.indirect_dma_start(disp_d, bass.IndirectOffsetOnAxis(pos[:, t:t + 1], 0),
                                         z[:, t, :], None).then_inc(dispatched, 16)
            for par in range(2):
                g.wait_ge(y_out[par], 16 * (TILES // 2 + 1))
            for t in range(NTA):
                for dst, pos in ((y1_g, pos1), (y2_g, pos2)):
                    g.indirect_dma_start(dst[:, t, :], None, res_d,
                                         bass.IndirectOffsetOnAxis(pos[:, t:t + 1], 0)).then_inc(gathered, 16)

        @block.scalar
        def _(act):
            def evacuate_T(u, dst, ready):
                full(act, u)
                s = slot(u)
                act.activation(dst[:, 0, 0:4 * TOK], s[0:C, 0:4 * TOK], ACT.Copy)
                act.activation(dst[:, 1, 0:4 * TOK], s[0:C, 512:512 + 4 * TOK], ACT.Copy)
                act.activation(dst[:, :, 4 * TOK:KEEP], s[0:C, 1024:1024 + 2 * TOK].rearrange("p (c s) -> p c s", c=2),
                               ACT.Copy).then_inc(ready, 1)
                act.wait_ge(ready, count_of[u[0]])
                act.sem_inc(slot_free[free_before(u)[0]], 1)

            count_of = {}
            pending = []

            def sigmoids():
                if not pending:
                    return
                u = pending.pop(0)
                n = nonlinear_of[u]
                act.wait_ge(masked, n + 1)
                c = cub[:, n % 2, :]
                b = u[1]
                if u[0] == "tail":
                    if b:
                        act.wait_ge(av_done, 3 * b)
                    src = c[0:TAIL, 0:HEADS * TAIL]
                    dst = [g_tail[:, i].rearrange("p h s -> p (h s)") for i in range(2)]
                else:
                    q = 3 * b + u[2] // 4
                    if q:
                        act.wait_ge(av_done, q)
                    src = c
                    dst = [sig[:, u[2] % 4, i, :] for i in range(2)]
                act.activation(dst[0], src, ACT.Sigmoid, scale=2 * K0 * D3 * SCORE_SCALE)
                act.activation(dst[1], src, ACT.Sigmoid, scale=2 * K1 * D3 * SCORE_SCALE).then_inc(sig_ready, 1)

            act.wait_ge(zero_out, 16 * (TILES * D // 1280))
            for b in range(B):
                act.wait_ge(scattered[b], 16 * NIN)
            for u in plan:
                kind = u[0]
                count_of[kind] = count_of.get(kind, 0) + 1
                if kind == "xT":
                    if u[1]:
                        full(act, ("v", u[1] - 1))
                    evacuate_T(u, xT, xT_ready)
                elif kind == "zT":
                    evacuate_T(u, yT, zT_ready)
                elif kind == "yT":
                    if u[1]:
                        full(act, ("logit", u[1] - 1))
                    evacuate_T(u, yT, yT_ready)
                elif kind == "q" or kind == "k":
                    m = 2 * u[1] + (kind == "k")
                    act.wait_ge(rotated, m + 1)
                    if m:
                        act.wait_ge(parts_out, 16 * m)
                    act.activation(parts[:, 0], rot, ACT.Copy).then_inc(hi_ready, 1)
                    act.wait_ge(rest_ready, m + 1)
                    act.activation(parts[:, 1], rot, ACT.Copy).then_inc(mid_ready, 1)
                elif kind == "v":
                    full(act, u)
                    s = slot(u)
                    if u[1]:
                        act.wait_ge(av_done, 3 * u[1])
                    for i, mix in enumerate((2 * MIX0, 2 * MIX1)):
                        for bank in range(2):
                            act.activation(v_mix5[:, i, 2 * bank:2 * bank + 2, :, 0:HD],
                                           s[:, 512 * bank:512 * bank + 2 * D].rearrange("p (t h d) -> p t h d", t=2, h=HEADS),
                                           ACT.Copy, scale=mix)
                        last = act.activation(v_mix5[0:TAIL, i, 4, :, 0:HD],
                                              s[0:TAIL, 1024:1024 + D].rearrange("p (h d) -> p h d", h=HEADS),
                                              ACT.Copy, scale=mix)
                    last.then_inc(v_ready, 1)
                    act.wait_ge(v_ready, u[1] + 1)
                    act.sem_inc(slot_free[free_before(u)[0]], 1)
                elif kind in ("tail", "head"):
                    n = nonlinear_of[u]
                    full(act, u)
                    if n >= 2:
                        act.wait_ge(sq_used, n - 1)
                    s = slot(u)
                    if kind == "tail":
                        act.activation(sq[0:TAIL, n % 2, 0:HEADS * TAIL], s[0:TAIL, 0:HEADS * TAIL], ACT.Square,
                                       scale=SCORE_SCALE).then_inc(sq_ready, 1)
                    else:
                        act.activation(sq[:, n % 2, :], s[:, RUN0:RUN0 + RUN], ACT.Square,
                                       scale=SCORE_SCALE).then_inc(sq_ready, 1)
                    sigmoids()
                    pending.append(u)
                elif kind == "flush":
                    sigmoids()
                elif kind == "av":
                    q = u[1]
                    act.wait_ge(av_done, q + 1)
                    if q >= 2:
                        full(act, ("oT", q - 2))
                    act.activation(o_sb[:, q % 2, 0:S0], o_ps[:, 0:S0], ACT.Copy)
                    act.activation(o_sb[:, q % 2, S0:KEEP], o_ps[:, 512:512 + KEEP - S0], ACT.Copy).then_inc(o_ready, 1)
            act.wait_ge(hot_ready, 1)
            act.activation(prob, cand, ACT.Exp).then_inc(hot_ready, 1)
            def copy_tT(i, par):
                act.wait_ge(tT_full, i + 1)
                act.activation(x_tT[0:C, par], slots[0][0:C, 0:2 * P].rearrange("p (c t) -> p c t", c=2),
                               ACT.Copy).then_inc(tT_ready, 1)

            def relu_a(i, par):
                act.wait_ge(hid_full, i + 1)
                act.activation(hid[:, par, 0:F // 2], slots[par][:, 512:512 + F // 2], ACT.Relu).then_inc(hid_a, 1)

            def copy_hT_a(i, par):
                act.wait_ge(hT_full, i + 1)
                act.activation(hidT[:, par, 0:3], o_ps[:, 0:3 * P].rearrange("p (k t) -> p k t", k=3),
                               ACT.Copy).then_inc(hT_a, 1)

            copy_tT(0, 0)
            copy_tT(1, 1)
            with act.Fori(0, TILES // 2 - 1) as j:
                for par in range(2):
                    relu_a(2 * j + par, par)
                    copy_tT(2 * j + par + 2, par)
                    copy_hT_a(2 * j + par, par)
            for par in range(2):
                relu_a(TILES - 2 + par, par)
                copy_hT_a(TILES - 2 + par, par)

        @block.vector
        def _(dve):
            v = nc.vector
            step = [0]

            def link(ins):
                ins.then_inc(vec_step, 1)
                step[0] += 1
                dve.wait_ge(vec_step, step[0])

            def rsqrt(y, t, a):
                link(v.tensor_scalar(y.bitcast(I32), a.bitcast(I32), -0.5, 1597463007.0, ALU.mult, ALU.add))
                for _ in range(4):
                    link(v.tensor_tensor(t, y, y, ALU.mult))
                    link(v.scalar_tensor_tensor(out=t, in0=t, scalar=-0.5, in1=a, op0=ALU.mult, op1=ALU.mult))
                    link(v.scalar_tensor_tensor(out=y, in0=t, scalar=1.5, in1=y, op0=ALU.add, op1=ALU.mult))

            v.memset(cnt[0:TIN], 0.0)
            v.memset(o_ps[:, :], 0.0)
            v.memset(v_mix5[:, 0, :, :, HD:HD + 1], 2 * MIX0)
            link(v.memset(v_mix5[:, 1, :, :, HD:HD + 1], 2 * MIX1))
            dve.wait_ge(row_in, 64)
            v.tensor_tensor(gw, gam_bc, w_bc, ALU.mult)
            link(v.scalar_tensor_tensor(out=junk, in0=bet_bc, scalar=1.0, in1=w_bc, op0=ALU.mult, op1=ALU.mult,
                                        accum_out=konst[0:TIN, 0:1]))
            link(v.tensor_tensor(konst[0:TIN, 0:1], konst[0:TIN, 0:1], konst[0:TIN, 1:2], ALU.add))

            def score_batch(b):
                dve.wait_ge(x_in[b], 16)
                tiles = range(NIN * b, NIN * (b + 1))
                for t in tiles:
                    link(v.bn_stats(stats[0:TIN, :], xn[:, t, 0:D]))
                    link(v.bn_aggr(mv[0:TIN, t, :], stats[0:TIN, :]))
                s = slice(NIN * b, NIN * (b + 1))
                link(v.tensor_scalar(var_e[0:TIN, s], mv[0:TIN, s, 1], LN_EPS, None, ALU.add))
                rsqrt(rs[0:TIN, s], rs_t[0:TIN, s], var_e[0:TIN, s])
                for t in tiles:
                    last = v.tensor_scalar(xn[:, t, D:2 * D], xn[:, t, 0:D], mv[0:TIN, t, 0:1], rs[0:TIN, t:t + 1],
                                           ALU.subtract, ALU.mult)
                link(last)
                for t in tiles:
                    last = v.scalar_tensor_tensor(out=junk, in0=xn[:, t, D:2 * D], scalar=1.0, in1=gw,
                                                  op0=ALU.mult, op1=ALU.mult, accum_out=score[0:TIN, t:t + 1])
                    link(last)
                link(v.tensor_scalar(score[0:TIN, s], score[0:TIN, s], konst[0:TIN, 0:1], None, ALU.add))
                if b == 0:
                    dve.wait_ge(const_set, 1)
                else:
                    full(dve, ("rank", b - 1))
                v.tensor_tensor(sdiag, ident[0:TIN, 0:TIN].unsqueeze(1).broadcast_to([TIN, NIN, TIN]),
                                score[0:TIN, s].unsqueeze(2).broadcast_to([TIN, NIN, TIN]), ALU.mult).then_inc(diag_ready, 1)

            def rank_batch(b):
                u = ("rank", b)
                full(dve, u)
                ps = slot(u)
                for t in range(NIN):
                    tt = NIN * b + t
                    s = score[0:TIN, tt:tt + 1]
                    c0, c1 = TIN * t, TIN * (t + 1)
                    if t:
                        link(v.tensor_scalar(cmp_junk[:, 0:c0], ps[0:TIN, 0:c0], s, None, ALU.is_ge, ALU.add,
                                             accum_out=cnt[0:TIN, tt, 0:1]))
                    if t < NIN - 1:
                        link(v.tensor_scalar(cmp_junk[:, c1:N], ps[0:TIN, c1:N], s, None, ALU.is_gt, ALU.add,
                                             accum_out=cnt[0:TIN, tt, 1:2]))
                    link(v.tensor_scalar(cmp_junk[:, c0:c1], ps[0:TIN, c0:c1], s, None, ALU.is_gt, ALU.add,
                                         accum_out=cnt[0:TIN, tt, 2:3]))
                    link(v.scalar_tensor_tensor(out=cmp_junk[:, c0:c1], in0=ps[0:TIN, c0:c1], scalar=s, in1=later[:, :],
                                                op0=ALU.is_equal, op1=ALU.mult, accum_out=cnt[0:TIN, tt, 3:4]))
                dve.sem_inc(slot_free[free_before(u)[0]], 1)
                s = slice(NIN * b, NIN * (b + 1))
                link(v.tensor_reduce(rs_t[0:TIN, s], cnt[0:TIN, s, :], AX.X, ALU.add))
                v.tensor_scalar(idx[0:TIN, s], rs_t[0:TIN, s], float(N * b), None, ALU.add).then_inc(idx_ready, 1)

            score_batch(0)
            for b in range(B):
                if b + 1 < B:
                    score_batch(b + 1)
                rank_batch(b)

            dve.wait_ge(w_in, 16 * 8)
            for u in plan:
                kind = u[0]
                if kind == "q" or kind == "k":
                    m = 2 * u[1] + (kind == "k")
                    full(dve, u)
                    s = slot(u)
                    if m:
                        dve.wait_ge(rotated, m)
                    wide = s[0:C, 0:1024].rearrange("p (a s) -> p a s", a=2)[:, :, 0:350]
                    rest_ = s[0:C, 1024:1374].rearrange("p (a s) -> p a s", a=2)
                    for table, dst in ((cos_sb, rot_c), (sin_sb, rot_s)):
                        v.tensor_tensor(dst[:, :, 0:350], wide, table[:, 0:350].unsqueeze(1).broadcast_to([C, 2, 350]), ALU.mult)
                        last = v.tensor_tensor(dst[:, :, 350:KEEP], rest_, table[:, 350:KEEP].unsqueeze(1).broadcast_to([C, 2, 175]), ALU.mult)
                    last.then_inc(rope_mul, 1)
                    dve.wait_ge(rope_mul, m + 1)
                    dve.sem_inc(slot_free[free_before(u)[0]], 1)
                elif kind in ("tail", "head"):
                    n = nonlinear_of[u]
                    if kind == "tail":
                        a, c = sq[0:TAIL, n % 2, 0:HEADS * TAIL], cub[0:TAIL, n % 2, 0:HEADS * TAIL]
                        s = slot(u)[0:TAIL, 0:HEADS * TAIL]
                    else:
                        a, c, s = sq[:, n % 2, :], cub[:, n % 2, :], slot(u)[:, RUN0:RUN0 + RUN]
                    dve.wait_ge(sq_ready, n + 1)
                    if n >= 2:
                        dve.wait_ge(sig_ready, n - 1)
                    link(v.scalar_tensor_tensor(out=c, in0=a, scalar=D2 / D3, in1=a, op0=ALU.add, op1=ALU.mult))
                    v.scalar_tensor_tensor(out=c, in0=c, scalar=D1 / D3, in1=a, op0=ALU.add, op1=ALU.mult).then_inc(sq_used, 1)
                    dve.wait_ge(sq_used, n + 1)
                    v.scalar_tensor_tensor(out=c, in0=c, scalar=1.0 / D3, in1=s, op0=ALU.add, op1=ALU.mult).then_inc(cub_ready, 1)
                    dve.wait_ge(cub_ready, n + 1)
                    dve.sem_inc(slot_free[free_before(u)[0]], 1)
                elif kind == "oT":
                    q = u[1]
                    full(dve, u)
                    if q % 3 == 0 and q:
                        full(dve, ("yT", q // 3 - 1))
                    o = slot(u)[0:TOK, 0:NT * P].rearrange("p (t h d) -> p t h d", t=NT, h=4)
                    link(v.tensor_scalar(den[0:TOK], o[:, :, :, HD], DEN_EPS, None, ALU.max))
                    link(v.reciprocal(den[0:TOK], den[0:TOK]))
                    g4 = q % 3
                    y4 = y_sb[:, :, 64 * g4:64 * g4 + 64].rearrange("p t (h d) -> p t h d", h=4)
                    for t in range(NT):
                        last = v.tensor_tensor(y4[:, t], o[:, t, :, 0:HD],
                                               den[0:TOK, t].unsqueeze(2).broadcast_to([TOK, 4, HD]), ALU.mult)
                    last.then_inc(y_ready, 1)
                    dve.wait_ge(y_ready, q + 1)
                    dve.sem_inc(slot_free[free_before(u)[0]], 1)
                elif kind == "proj":
                    b = u[1]
                    full(dve, u)
                    dve.wait_ge(h_loaded[b], 16)
                    s = slot(u)
                    for t in range(NT):
                        at = 512 * (t // 2) + D * (t % 2)
                        link(v.tensor_tensor(hres[:, NT * b + t, :], s[0:TOK, at:at + D], hres[:, NT * b + t, :], ALU.add))
                        link(v.bn_stats(stats[0:TOK, :], hres[:, NT * b + t, :]))
                        link(v.bn_aggr(mv2[0:TOK, NT * b + t, :], stats[0:TOK, :]))
                    dve.sem_inc(slot_free[free_before(u)[0]], 1)
                    s5 = slice(NT * b, NT * (b + 1))
                    link(v.tensor_scalar(var_e[0:TOK, 0:NT], mv2[0:TOK, s5, 1], LN_EPS, None, ALU.add))
                    rsqrt(rs[0:TOK, 0:NT], rs_t[0:TOK, 0:NT], var_e[0:TOK, 0:NT])
                    for t in range(NT):
                        tt = NT * b + t
                        last = v.tensor_scalar(z[:, tt, :], hres[:, tt, :], mv2[0:TOK, tt, 0:1], rs[0:TOK, t:t + 1],
                                               ALU.subtract, ALU.mult)
                    last.then_inc(z_ready, 1)
                elif kind == "logit":
                    b = u[1]
                    full(dve, u)
                    link(v.tensor_copy(logits[0:TOK, NT * b:NT * (b + 1), :],
                                       slot(u)[0:TOK, 0:NT * E].rearrange("p (t e) -> p t e", t=NT)))
                    dve.sem_inc(slot_free[free_before(u)[0]], 1)

            def wide8(a):
                return a.unsqueeze(2).broadcast_to([TOK, NTA, E])

            lg = logits[0:TOK]
            numbers = count_sb[0:TOK, 0:E].unsqueeze(1).broadcast_to([TOK, NTA, E])
            link(v.tensor_reduce(ind, lg, AX.X, ALU.max))
            v.tensor_tensor(cand, lg, wide8(ind), ALU.subtract).then_inc(hot_ready, 1)
            dve.wait_ge(hot_ready, 2)
            link(v.tensor_reduce(sums, prob, AX.X, ALU.add))
            link(v.reciprocal(sums, sums))
            link(v.tensor_tensor(prob, prob, wide8(sums), ALU.mult))

            def pick(top, hot):
                link(v.tensor_reduce(top, prob, AX.X, ALU.max))
                link(v.tensor_tensor(cand, prob, wide8(top), ALU.is_equal))
                link(v.scalar_tensor_tensor(out=cand, in0=cand, scalar=-float(E), in1=numbers, op0=ALU.mult, op1=ALU.add))
                link(v.tensor_reduce(ind, cand, AX.X, ALU.min))
                link(v.tensor_scalar(ind, ind, float(E), None, ALU.add))
                link(v.tensor_tensor(hot, numbers, wide8(ind), ALU.is_equal))

            pick(top1, hot1)
            link(v.scalar_tensor_tensor(out=prob, in0=hot1, scalar=-2.0, in1=prob, op0=ALU.mult, op1=ALU.add))
            pick(top2, hot2)
            v.tensor_tensor(both, hot1, hot2, ALU.add).then_inc(hot_ready, 1)
            link(v.tensor_tensor(sums, top1, top2, ALU.add))
            link(v.reciprocal(sums, sums))
            v.tensor_tensor(cw1, top1, sums, ALU.mult)
            link(v.tensor_tensor(cw2, top2, sums, ALU.mult))
            link(v.memset(carry, 1.0))
            link(v.memset(carry[:, :, 0], 0.0))
            dve.wait_ge(prefix_ready, 1)
            link(v.tensor_copy(totals, slots[0][0:TOK, 512:512 + NTA * E].rearrange("p (t e) -> p e t", e=E)))
            link(v.tensor_tensor_scan(run_tot.rearrange("p e t -> p (e t)"), carry.rearrange("p e t -> p (e t)"),
                                      totals.rearrange("p e t -> p (e t)"), 0.0, ALU.mult, ALU.add))
            link(v.tensor_scalar(n_int, run_tot[:, :, NTA - 1], float(P - 1), None, ALU.add))
            link(v.tensor_scalar(n_int, n_int, 7, None, ALU.arith_shift_right))
            link(v.tensor_copy(n_tiles, n_int))
            link(v.tensor_tensor_scan(ends, ones[0:TOK, 0:E], n_tiles, 0.0, ALU.mult, ALU.add))
            link(v.tensor_tensor(base, ends, n_tiles, ALU.subtract))
            link(v.tensor_tensor(run_tot, run_tot, totals, ALU.subtract))
            link(v.scalar_tensor_tensor(out=run_tot, in0=base.unsqueeze(2).broadcast_to([TOK, E, NTA]), scalar=float(P),
                                        in1=run_tot, op0=ALU.mult, op1=ALU.add))
            link(v.tensor_tensor(posf, slots[0][0:TOK, 0:NTA * E].rearrange("p (t e) -> p t e", e=E),
                                 run_tot.rearrange("p e t -> p t e"), ALU.add))
            for hot, pos in ((hot1, pos1), (hot2, pos2)):
                link(v.tensor_tensor(cand, posf, hot, ALU.mult))
                link(v.tensor_reduce(ind, cand, AX.X, ALU.add))
                link(v.tensor_copy(pos, ind))
            dve.sem_inc(pos_ready, 1)
            link(v.tensor_tensor(tile_cmp, count_sb[0:TOK, :].unsqueeze(2).broadcast_to([TOK, TILES, E]),
                                 ends.unsqueeze(1).broadcast_to([TOK, TILES, E]), ALU.is_ge))
            link(v.tensor_reduce(eid_f, tile_cmp, AX.X, ALU.add))
            link(v.tensor_scalar(eid_f, eid_f, float(E - 1), None, ALU.min))
            v.tensor_copy(eid, eid_f).then_inc(pos_ready, 1)
            dve.wait_ge(av_done, 3 * B)
            v.memset(x_tT[C:C + 1, :, 1, :], 1.0).then_inc(ones_row, 1)
            dve.wait_ge(b2_in, 16)
            dve.wait_ge(pos_ready, 2)
            dve.sem_inc(y_out_ready, 1)

            with dve.Fori(0, TILES // 2) as j:
                for par in range(2):
                    i = 2 * j + par
                    e = dve.value_load(eid[0:1, bass.ds(i, 1)], min_val=0, max_val=E - 1)
                    dve.wait_ge(hid_full, i + 1)
                    v.tensor_scalar(hid[:, par, F // 2:F], slots[par][:, 1024:1024 + F // 2], 0.0, None, ALU.max).then_inc(hid_b, 1)
                    dve.wait_ge(hT_full, i + 1)
                    v.tensor_copy(hidT[:, par, 3:6], o_ps[:, 512:512 + 3 * P].rearrange("p (k t) -> p k t", k=3)).then_inc(hT_b, 1)
                    dve.wait_ge(y_full, i + 1)
                    dve.wait_ge(y_out[par], 16 * (j + 1))
                    v.tensor_tensor(y_tile[:, par, :], slots[1][:, 0:D], b2_bc[:, bass.ds(e * D, D)], ALU.add).then_inc(y_out_ready, 1)

            dve.wait_ge(gathered, 16 * 2 * NTA)
            for b in range(B):
                for t in range(NT * b, NT * (b + 1)):
                    link(v.scalar_tensor_tensor(out=z[:, t, :], in0=y1_g[:, t, :], scalar=cw1[:, t:t + 1], in1=hres[:, t, :],
                                                op0=ALU.mult, op1=ALU.add))
                    last = v.scalar_tensor_tensor(out=z[:, t, :], in0=y2_g[:, t, :], scalar=cw2[:, t:t + 1], in1=z[:, t, :],
                                                  op0=ALU.mult, op1=ALU.add)
                    if t < NT * (b + 1) - 1:
                        link(last)
                last.then_inc(out_ready, 1)
                dve.wait_ge(out_ready, b + 1)

        @block.tensor
        def _(pe):
            def transposes(u, src, tile0):
                s = slot(u)
                for t in range(NT):
                    for c in range(2):
                        dst = s[0:C, 512 * c + TOK * t:512 * c + TOK * (t + 1)] if t < 4 else \
                            s[0:C, 1024 + TOK * c:1024 + TOK * (c + 1)]
                        last = pe.transpose(dst, src[:, tile0 + t, C * c:C * (c + 1)], ident[0:TOK, 0:TOK])
                last.then_inc(psum_full, 1)

            pe.wait_ge(const_set, 1)
            for u in plan:
                kind = u[0]
                if kind in SLOTTED:
                    take_slot(pe, u)
                    s = slot(u)
                if kind == "rank":
                    pe.wait_ge(diag_ready, u[1] + 1)
                    pe.matmul(s[0:TIN, 0:4 * TIN], ones[0:TIN, 0:TIN], sdiag[:, 0:4, :], start=True, stop=True)
                    flat = sdiag.rearrange("p t j -> p (t j)")
                    pe.matmul(s[0:TIN, 500:512], ones[0:TIN, 0:TIN], flat[:, 500:512], start=True, stop=True)
                    pe.matmul(s[0:TIN, 512:N], ones[0:TIN, 0:TIN], flat[:, 512:N], start=True, stop=True).then_inc(psum_full, 1)
                elif kind == "xT":
                    pe.wait_ge(x_loaded[u[1]], 16)
                    transposes(u, x_sorted, 0)
                elif kind in ("q", "k"):
                    pe.wait_ge(xT_ready, u[1] + 1)
                    pe.wait_ge(w_in, 16 * 8)
                    for two in range(2):
                        for lo, hi, at in ((0, 350, 512 * two), (350, KEEP, 1024 + 175 * two)):
                            for c in range(2):
                                last = pe.matmul(s[0:C, at:at + hi - lo], wqk_sb[:, int(kind == "k"), c, two, :],
                                                 xT[:, c, lo:hi], start=(c == 0), stop=(c == 1))
                    last.then_inc(psum_full, 1)
                elif kind == "v":
                    for t in range(NT):
                        n = min(P, KEEP - P * t)
                        at = 512 * (t // 2) + D * (t % 2)
                        for c in range(2):
                            last = pe.matmul(s[0:n, at:at + D], xT[:, c, P * t:P * t + n], wv_sb[:, c, :],
                                             start=(c == 0), stop=(c == 1))
                    last.then_inc(psum_full, 1)
                elif kind in ("tail", "head"):
                    b = u[1]
                    pe.wait_ge(stack_in[b % 2], 16 * 16 * (b // 2 + 1))
                    qs = stack(b % 2, 0).rearrange("p (h s) -> p h s", h=HEADS)
                    ks = stack(b % 2, 1).rearrange("p (h s) -> p h s", h=HEADS)
                    if kind == "tail":
                        for h in range(HEADS):
                            last = pe.matmul(s[0:TAIL, TAIL * h:TAIL * (h + 1)], ks[:, h, 512:KEEP], qs[:, h, 512:KEEP],
                                             start=True, stop=True)
                    else:
                        h = u[2]
                        for kt, q0, n, at in PIECES:
                            last = pe.matmul(s[:, RUN0 + at:RUN0 + at + n], ks[:, h, P * kt:P * (kt + 1)],
                                             qs[:, h, q0:q0 + n], start=True, stop=True)
                    last.then_inc(psum_full, 1)
                elif kind == "av":
                    q = u[1]
                    b, g4 = q // 3, q % 3
                    pe.wait_ge(v_ready, b + 1)
                    pe.wait_ge(sig_ready, nonlinear_of[("head", b, 4 * g4 + 3)] + 1)
                    if b:
                        pe.wait_ge(sig_ready, nonlinear_of[("tail", b)] + 1)
                    if q:
                        pe.wait_ge(o_ready, q)
                    for m in range(2):
                        for n, (kt, q0, width, at) in enumerate(PIECES):
                            o0 = 512 + q0 - S0 if q0 >= S0 else q0
                            first = m == 0 and (n == 0 or q0 < S0)
                            for hh in range(4):
                                h = 4 * g4 + hh
                                pe.matmul(o_ps[32 * hh:32 * hh + HD + 1, o0:o0 + width],
                                          v_mix5[:, m, kt, h, :], sig[:, hh, m, at:at + width],
                                          start=first, stop=(m == 1 and q0 < S0))
                    for m in range(2):
                        for hh in range(4):
                            h = 4 * g4 + hh
                            last = pe.matmul(o_ps[32 * hh:32 * hh + HD + 1, 512 + 512 - S0:512 + KEEP - S0],
                                             v_mix5[0:TAIL, m, 4, h, :], g_tail[:, m, h, :],
                                             start=False, stop=(m == 1))
                    last.then_inc(av_done, 1)
                elif kind == "oT":
                    q = u[1]
                    pe.wait_ge(o_ready, q + 1)
                    for t in range(NT):
                        last = pe.transpose(s[0:TOK, P * t:P * (t + 1)], o_sb[:, q % 2, TOK * t:TOK * (t + 1)], ident[:, :])
                    last.then_inc(psum_full, 1)
                elif kind == "yT":
                    pe.wait_ge(y_ready, 3 * (u[1] + 1))
                    transposes(u, y_sb, 0)
                elif kind == "proj":
                    pe.wait_ge(yT_ready, u[1] + 1)
                    for t in range(NT):
                        at = 512 * (t // 2) + D * (t % 2)
                        for c in range(2):
                            last = pe.matmul(s[0:TOK, at:at + D], yT[:, c, TOK * t:TOK * (t + 1)], wp_sb[:, c, :],
                                             start=(c == 0), stop=(c == 1))
                    last.then_inc(psum_full, 1)
                elif kind == "zT":
                    pe.wait_ge(z_ready, u[1] + 1)
                    transposes(u, z, NT * u[1])
                elif kind == "logit":
                    pe.wait_ge(zT_ready, u[1] + 1)
                    for t in range(NT):
                        for c in range(2):
                            last = pe.matmul(s[0:TOK, E * t:E * (t + 1)], yT[:, c, TOK * t:TOK * (t + 1)], wg_sb[:, c, :],
                                             start=(c == 0), stop=(c == 1))
                    last.then_inc(psum_full, 1)

            for sl in range(2):
                pe.wait_ge(slot_free[sl], (len(unit_of) + 1 - sl) // 2)
            pe.wait_ge(hot_ready, 3)
            flat = both.rearrange("p t e -> p (t e)")
            pe.matmul(slots[0][0:TOK, 0:NTA * E], before[:, :], flat, start=True, stop=True)
            pe.matmul(slots[0][0:TOK, 512:512 + NTA * E], ones[0:TOK, 0:TOK], flat, start=True, stop=True).then_inc(prefix_ready, 1)

            pe.wait_ge(pos_ready, 2)
            pe.wait_ge(w1_in, 48)
            pe.wait_ge(w2_in, 16 * E)
            pe.wait_ge(ones_row, 1)
            pe.wait_ge(o_ready, 3 * B)

            def transpose_in(par, i, j):
                pe.wait_ge(tile_in[par], 16 * (j + 1))
                pe.wait_ge(tT_ready, i)
                pe.transpose(slots[0][0:C, 0:P], x_tile[:, par, 0:C], ident[:, :])
                pe.transpose(slots[0][0:C, P:2 * P], x_tile[:, par, C:D], ident[:, :]).then_inc(tT_full, 1)

            def multiply_w1(par, i):
                e = pe.value_load(eid[0:1, bass.ds(i, 1)], min_val=0, max_val=E - 1)
                pe.wait_ge(tT_ready, i + 1)
                for half in range(2):
                    dst = slots[par][:, 512 * (half + 1):512 * (half + 1) + F // 2]
                    for c, k in ((0, C), (1, C + 1)):
                        last = pe.matmul(dst, x_tT[0:k, par, c, :],
                                         w1_sb[0:k, bass.ds(e * (2 * F) + (c * F + half * (F // 2)), F // 2)],
                                         start=(c == 0), stop=(c == 1))
                last.then_inc(hid_full, 1)

            def stage_out(par, i):
                e = pe.value_load(eid[0:1, bass.ds(i, 1)], min_val=0, max_val=E - 1)
                pe.wait_ge(hid_a, i + 1)
                pe.wait_ge(hid_b, i + 1)
                for k in range(6):
                    last = pe.transpose(o_ps[:, 512 * (k // 3) + P * (k % 3):512 * (k // 3) + P * (k % 3 + 1)],
                                        hid[:, par, P * k:P * (k + 1)], ident[:, :])
                last.then_inc(hT_full, 1)
                pe.wait_ge(hT_a, i + 1)
                pe.wait_ge(hT_b, i + 1)
                pe.wait_ge(y_out_ready, i + 1)
                for k in range(6):
                    last = pe.matmul(slots[1][:, 0:D], hidT[:, par, k, :], w2_sb[:, bass.ds(e * (6 * D) + k * D, D)],
                                     start=(k == 0), stop=(k == 5))
                last.then_inc(y_full, 1)

            transpose_in(0, 0, 0)
            multiply_w1(0, 0)
            transpose_in(1, 1, 0)
            with pe.Fori(0, TILES // 2 - 1) as j:
                multiply_w1(1, 2 * j + 1)
                transpose_in(0, 2 * j + 2, j + 1)
                stage_out(0, 2 * j)
                multiply_w1(0, 2 * j + 2)
                transpose_in(1, 2 * j + 3, j + 1)
                stage_out(1, 2 * j + 1)
            multiply_w1(1, TILES - 1)
            stage_out(0, TILES - 2)
            stage_out(1, TILES - 1)


def kernel(x, L0_tok_gamma, L0_tok_beta, L0_tok_w, L0_tok_b, L0_attn_Wq, L0_attn_Wk, L0_attn_Wv, L0_attn_Wproj,
           L0_ffn_Wg, L0_ffn_W1, L0_ffn_b1, L0_ffn_W2, L0_ffn_b2):
    import concourse.bacc as bacc
    from concourse.bass_utils import run_bass_kernel_spmd

    def chunks(w):
        return np.ascontiguousarray(np.asarray(w).reshape(D, 2, C).transpose(2, 1, 0))

    def rotary_chunks(w):
        return np.ascontiguousarray(np.asarray(w).reshape(HEADS, HALF, 2, 2, C).transpose(4, 3, 2, 1, 0)).reshape(C, 2, 2, C)

    freq = (np.float32(1.0) / np.float32(10000.0) ** (np.arange(HALF, dtype=np.float32) / np.float32(HALF))).astype(np.float32)
    angle = (np.repeat(freq, HEADS)[:, None] * np.arange(KEEP, dtype=np.float32)[None, :]).astype(np.float32)
    arrays = {
        "x": x, "gamma": L0_tok_gamma, "beta": L0_tok_beta, "w": L0_tok_w, "b_score": L0_tok_b,
        "wqT": rotary_chunks(L0_attn_Wq), "wkT": rotary_chunks(L0_attn_Wk),
        "wvT": chunks(L0_attn_Wv), "wpT": chunks(L0_attn_Wproj),
        "wg": L0_ffn_Wg, "w1": L0_ffn_W1, "b1": L0_ffn_b1, "w2": L0_ffn_W2, "b2": L0_ffn_b2,
        "rope_cos": np.cos(angle), "rope_sin": np.sin(angle), "count": np.arange(TILES, dtype=np.float32),
    }
    nc = bacc.Bacc("TRN2", target_bir_lowering=False, num_devices=1)
    arrays = {k: np.ascontiguousarray(a) for k, a in arrays.items()}
    args = [nc.dram_tensor(k, a.shape, mybir.dt.from_np(a.dtype), kind="ExternalInput").ap() for k, a in arrays.items()]
    out = nc.dram_tensor("out", (B, KEEP, D), F32, kind="ExternalOutput").ap()
    build_program(nc, *args, out)
    result = run_bass_kernel_spmd(nc, [arrays], core_ids=[0])
    return result.results[0]["out"]
```

```python
from contextlib import ExitStack

import numpy as np

import concourse.bass as bass
from concourse import mybir

F32 = mybir.dt.float32
BF16 = mybir.dt.bfloat16
I32 = mybir.dt.int32
U32 = mybir.dt.uint32
ALU = mybir.AluOpType
ACT = mybir.ActivationFunctionType
AX = mybir.AxisListType

B, N, D = 4, 750, 192
KEEP = int(N * 0.7)
HEADS, HD = 12, 16
E, F = 8, 768
TIN, NIN = 125, 6
TOK, NT = 105, 5
C = D // 2
PAIRS = HEADS // 2
HALF = HD // 2
P = 128
NTA = B * NT
ROWS = B * KEEP
SMALL = 690
TILES = (2 * ROWS + E * (P - 1)) // P
META_GROUPS = (slice(0, 8), slice(8, TILES))
ROW = D + 4
LN_EPS = 1e-5
DEN_EPS = 1e-6

S0 = 115
PIECES = [(0, S0, KEEP - S0, 0), (1, 128, KEEP - 128, 410), (0, 0, S0, 807),
          (2, 256, KEEP - 256, 922), (3, 384, KEEP - 384, 1191)]
RUN = 1332
RUN0 = 512 - (KEEP - S0)
TAIL = KEEP - 512

D1, D2, D3 = 0.10836966378404583, -0.0026960067293568426, 4.653028531935965e-05
ROOT = -float(min(np.roots([1.0, D2 / D3, D1 / D3, 1.0 / D3]), key=lambda z: abs(z.imag)).real)
QUAD1, QUAD0 = D2 / D3 - ROOT, 1.0 / (D3 * ROOT)
K0, K1 = 1.01124489655701, 1.274538823519078
MIX0 = 0.555126294782942
MIX1 = 1.0 - MIX0
SCORE_SCALE = 1.0 / HD ** 0.5

Q_BLOCKS = [0, 0, 0, 1, 1, 1, 2, 2]
K_BLOCKS = [0, 1, 2, 0, 1, 2, 0, 1]
MASKED = -1e6


ROUTER_AT = ((16, 17, 18, 19, 20, 21, 22, 23, 24, 25, 26, 27, 28, 29, 29, 30, 31, 32, 33),
             (16, 17, 17, 17, 18, 18, 18, 19, 20, 21, 22, 22, 23, 23, 24, 24, 24, 24, 24))


def build_plan():
    plan = [("rank", b) for b in range(B)]
    plan += [("xT", 0), ("q", 0), ("hi", 0), ("mid", 0), ("k", 0), ("hi", 1), ("mid", 1), ("v", 0), ("tail", 0)]
    after = {(b, h): [] for b in range(B) for h in range(HEADS)}

    def late(b, h):
        return after.get((b + h // HEADS, h % HEADS), ending)

    ending = []
    for b in range(B):
        if b:
            late(b, 2).append(("v", b))
            late(b, 3).append(("tail", b))
        for pair in range(HEADS // 2):
            late(b, 2 * pair + 3).append(("av", 6 * b + pair, 0))
            late(b, 2 * pair + 4).append(("av", 6 * b + pair, 1))
        for g in range(3):
            late(b, 4 * g + 6).append(("o", 3 * b + g))
            late(b, 4 * g + 7).append(("oT", 3 * b + g))
        if b + 1 < B:
            late(b, 2).append(("xT", b + 1))
            late(b, 3).append(("q", b + 1))
            late(b, 5).append(("hi", 2 * b + 2))
            late(b, 6).extend([("mid", 2 * b + 2), ("k", b + 1)])
            late(b, 8).append(("hi", 2 * b + 3))
            late(b, 9).append(("mid", 2 * b + 3))
        for h, u in zip(ROUTER_AT[b == B - 2],
                        [("yT", b), ("proj", b)] + [("z", b, t) for t in range(NT)] +
                        [("zT", b), ("logit", b), ("pick", b), ("pick2", b), ("count", b), ("place", b), ("note", b)] +
                        [("disp", b, t) for t in range(NT)], strict=True):
            late(b, h).append(u)
    for b in range(B):
        for h in range(HEADS):
            after[b, h].sort(key=lambda u: ("av", "o", "oT", "v", "xT").index(u[0]) if u[0] in ("av", "o", "oT", "v", "xT") else 9)
            plan += [("head", b, h)] + after[b, h]
    plan += [("flush",)] + ending
    return plan


SLOTTED = ("rank", "xT", "q", "k", "v", "tail", "head", "oT", "yT", "proj", "zT", "logit", "count")


def build_program(nc, x, gamma, beta, w, b_score, wqT, wkT, wvT, wpT, wg, w1, b1, w2, b2,
                  rope_cos, rope_sin, count, token_no, out):
    plan = build_plan()
    unit_of = {}
    for u in plan:
        if u[0] in SLOTTED:
            unit_of[u] = len(unit_of)
    nonlinear_of = {}
    for u in plan:
        if u[0] in ("tail", "head"):
            nonlinear_of[u] = len(nonlinear_of)

    ctx = ExitStack()
    with ctx:
        def sb(name, shape, dt=F32):
            return ctx.enter_context(nc.sbuf_tensor(name, shape, dt))

        def dram(name, shape, dt=F32):
            return nc.dram_tensor(name, shape, dt, kind="Internal").ap()

        def sem(name):
            return ctx.enter_context(nc.semaphore(name))

        sorted_d = dram("sorted_d", [B * N, 2 * D])
        parts_d = dram("parts_d", [B, 2, 6 * C, KEEP], BF16)
        disp_d = dram("disp_d", [TILES * P, ROW])
        acc_d = dram("acc_d", [ROWS + P, D])

        arena = sb("arena", [P, 21504])
        g_area = sb("g_area", [P, 8 * RUN])
        hres = sb("hres", [TOK, NTA, D])
        z = sb("z", [TOK, NTA, ROW])
        sq = sb("sq", [P, 2, RUN])
        quad = sb("quad", [P, RUN])
        cub = sb("cub", [P, 2, RUN])
        v_mix = sb("v_mix", [P, 2, NT, HEADS * (HD + 1)])
        v_mix5 = v_mix[:, :, :, :].rearrange("p m t (h d) -> p m t h d", h=HEADS)
        o_sb = sb("o_sb", [P, 2, KEEP])
        y_sb = sb("y_sb", [TOK, NT, D])
        yT = sb("yT", [C, 2, KEEP])
        wp_sb = sb("wp_sb", [C, 2, D])
        wg_sb = sb("wg_sb", [C, 2, E])
        ident = sb("ident", [P, P])
        before = sb("before", [TOK, TOK])
        ones = sb("ones", [P, P])
        count_sb = sb("count_sb", [P, TILES])
        small = sb("small", [P, SMALL])

        stack_w = HEADS * KEEP // 2
        def stack(par, qk):
            at = par * 12288 + qk * stack_w
            return arena[:, at:at + stack_w].bitcast(BF16)
        rot_c = arena[0:C, 6300:7350].rearrange("p (a s) -> p a s", a=2)
        rot_s = arena[0:C, 7350:8400].rearrange("p (a s) -> p a s", a=2)
        rot = arena[0:C, 8400:9450].rearrange("p (a s) -> p a s", a=2)
        parts = arena[0:C, 9450:11025].bitcast(BF16).rearrange("p (a b s) -> p a b s", a=3, b=2)
        xT = arena[0:C, 11025:12075].rearrange("p (c s) -> p c s", c=2)
        tri = arena[:, 12075:12139].bitcast(BF16)
        ident_b = arena[:, 12139:12203].bitcast(BF16)
        w1_sb = arena[:, 0:12288]
        cos_sb = arena[0:C, 18588:19113]
        sin_sb = arena[0:C, 19113:19638]
        wqk_sb = arena[0:C, 19638:20406].rearrange("p (q c t m) -> p q c t m", q=2, c=2, t=2)
        wv_sb = arena[0:C, 20406:20790].rearrange("p (c o) -> p c o", c=2)
        hs = HEADS * TAIL
        g_tail = arena[0:TAIL, 20790:20790 + 2 * hs].rearrange("p (m h s) -> p m h s", m=2, h=HEADS)
        sq_tail, cub_tail = arena[0:TAIL, 21102:21102 + hs], arena[0:TAIL, 21258:21258 + hs]
        idx = arena[:, 21414:21414 + B * NIN].bitcast(U32)
        w2_sb = arena[:, 12288:21504]

        xn = g_area[0:TIN, 0:24 * 384].rearrange("p (t d) -> p t d", t=B * NIN)
        pad_row = g_area[:, 9216:9216 + ROW]
        sig = g_area[:, :].rearrange("p (h m s) -> p h m s", h=4, m=2)
        b2_bc = g_area[:, 0:1536]
        b2_row = g_area[:, 1536:1536 + D]
        meta = g_area[:, 1728:1728 + 4 * TILES].rearrange("p (t w) -> p t w", t=TILES)
        weight, weight2 = g_area[:, 1888:1888 + TILES], g_area[:, 1928:1928 + TILES]
        dest = g_area[:, 1968:1968 + TILES].bitcast(U32)
        dest_now = g_area[:, 2008:2010].bitcast(U32)
        eid = g_area[:, 2040:2040 + TILES].bitcast(I32)
        x_tT = g_area[0:C + 1, 2112:2624].rearrange("p (r c t) -> p r c t", r=2, c=2)
        hidT = g_area[:, 2624:4160].rearrange("p (r k t) -> p r k t", r=2, k=6)
        w1_now = g_area[0:C + 1, 4160:4160 + 4 * F].rearrange("p (r c f) -> p r c f", r=2, c=2)
        y_tile = g_area[:, 7232:7232 + 2 * D].rearrange("p (r d) -> p r d", r=2)
        x_tile = g_area[:, 7616:7616 + 2 * D].rearrange("p (r d) -> p r d", r=2)

        used = {"front": 0, "small": 0}

        def tiny(where, parts_, *dims, dt=F32):
            area, size = {"front": (o_front, 2 * KEEP), "small": (small, SMALL)}[where]
            n, at = int(np.prod(dims)), used[where]
            used[where] += n
            assert used[where] <= size
            v = area[0:parts_, at:at + n]
            if dt is not F32:
                v = v.bitcast(dt)
            if len(dims) == 2:
                v = v.rearrange("p (a b) -> p a b", a=dims[0])
            if len(dims) == 3:
                v = v.rearrange("p (a b c) -> p a b c", a=dims[0], b=dims[1])
            return v

        o_front = o_sb[:, :, :].rearrange("p a s -> p (a s)")
        later = tiny("front", TIN, TIN)
        stats = tiny("front", P, NIN, 6)
        mv = tiny("front", P, B * NIN, 2)
        var_e, rs, rs_t, score = (tiny("front", P, B * NIN) for _ in range(4))
        cnt = tiny("front", P, B * NIN, 4)
        konst = tiny("front", P, 2)
        token_sb = tiny("front", P, NTA + 1)
        half_quad = tiny("small", P, 1)
        den = tiny("small", P, NT, 4)
        mv2 = tiny("small", P, NTA, 2)
        rs2 = tiny("small", P, NTA)
        var2, rs2_t = tiny("small", P, NT), tiny("small", P, NT)
        front = cub[0:TIN, 0, :]
        gw = front[:, 0:D]
        gam_bc = front[:, D:2 * D]
        bet_bc = front[:, 2 * D:3 * D]
        w_bc = front[:, 3 * D:4 * D]
        junk = front[:, 4 * D:5 * D]
        sdiag = cub[0:TIN, 1, 0:NIN * TIN].rearrange("p (t j) -> p t j", t=NIN)
        cmp_junk = sq[0:TIN, 0, 0:N]

        prob, cand, cand2, hot1, hot2, both = (tiny("small", TOK, NT, E) for _ in range(6))
        posf = cand
        stats2 = prob.rearrange("p t e -> p (t e)")[:, 0:NT * 6].rearrange("p (t s) -> p t s", t=NT)
        top1, top2, ind, sums = (tiny("small", TOK, NT) for _ in range(4))
        pos1, pos2 = tiny("small", TOK, NTA, dt=U32), tiny("small", TOK, NTA, dt=U32)
        totals, run_tot, carry = (tiny("small", P, E, NT) for _ in range(3))
        rows_e, chunks_e, last_tile, ends, base, n_new, c_new, tmp_e, old_e = (tiny("small", P, E) for _ in range(9))
        c_int = tiny("small", P, E, dt=I32)
        used_tiles = tiny("small", P, 1)
        eid_f, eid_add = tiny("small", P, TILES), totals.rearrange("p e t -> p (e t)")[:, 0:TILES]
        assert TILES <= E * NT

        slots = [ctx.enter_context(nc.psum_tensor(f"slot{i}", [P, 1536], F32)) for i in range(2)]
        o_ps = ctx.enter_context(nc.psum_tensor("o_ps", [P, 1024], F32))

        def slot(u):
            return slots[unit_of[u] % 2]

        x_in = [sem(f"x_in{b}") for b in range(B)]
        row_in, w_in, token_in, pad_set, pad_out = sem("row_in"), sem("w_in"), sem("token_in"), sem("pad_set"), sem("pad_out")
        const_set, vec_step = sem("const_set"), sem("vec_step")
        diag_ready, idx_ready = sem("diag_ready"), sem("idx_ready")
        scattered = [sem(f"scattered{b}") for b in range(B)]
        x_loaded, h_loaded = ([sem(f"{n}{b}") for b in range(B)] for n in ("x_loaded", "h_loaded"))
        psum_full, slot_free = sem("psum_full"), [sem("slot_free0"), sem("slot_free1")]
        xT_ready, rope_mul, rotated, hi_ready, rest_ready, mid_ready, parts_ready = (
            sem("xT_ready"), sem("rope_mul"), sem("rotated"), sem("hi_ready"), sem("rest_ready"),
            sem("mid_ready"), sem("parts_ready"))
        parts_out, stack_in = sem("parts_out"), [sem("stack_in0"), sem("stack_in1")]
        v_ready, sq_ready, cub_ready, sig_ready = (
            sem("v_ready"), sem("sq_ready"), sem("cub_ready"), sem("sig_ready"))
        lin_ready, quad_ready, quad_v, norm_ready = sem("lin_ready"), sem("quad_ready"), sem("quad_v"), sem("norm_ready")
        pool_step = sem("pool_step")
        av_done, o_ready, y_ready, yT_ready, z_ready, zT_ready = (
            sem("av_done"), sem("o_ready"), sem("y_ready"), sem("yT_ready"), sem("z_ready"), sem("zT_ready"))
        w1_in, w2_in, b2_in = sem("w1_in"), sem("w2_in"), sem("b2_in")
        shifted, prob_ready, hot_ready, pos_ready, eid_ready, dispatched, h_added, acc_in = (
            sem("shifted"), sem("prob_ready"), sem("hot_ready"), sem("pos_ready"), sem("eid_ready"),
            sem("dispatched"), sem("h_added"), sem("acc_in"))
        ones_row = sem("ones_row")
        tile_in = [sem(f"tile_in{i}") for i in range(2)]
        tT_full, tT_ready, w1_copied, hid_full, hid_copied, y_full, y_copied, y_out_ready = (
            sem("tT_full"), sem("tT_ready"), [sem("w1_copied0"), sem("w1_copied1")], sem("hid_full"),
            [sem("hid_copied0"), sem("hid_copied1")], sem("y_full"), sem("y_copied"), sem("y_out_ready"))
        meta_in = [sem(f"meta_in{i}") for i in range(2)]
        added = [sem(f"added{i}") for i in range(2)]
        dest_ready, dest_set, add_begun, out_done = sem("dest_ready"), sem("dest_set"), sem("add_begun"), sem("out_done")

        def wait_from_1(eng, semaphore, n):
            if not isinstance(n, int) or n > 0:
                eng.wait_ge(semaphore, n)

        def on_scalar(u):
            return u[0] == "head" and u[2] % 2 == 1

        def buffers(u):
            if u[0] == "tail":
                return sq_tail, cub_tail, slot(u)[0:TAIL, 0:HEADS * TAIL]
            return sq[:, u[2] % 2, :], cub[:, u[2] % 2, :], slot(u)[:, RUN0:RUN0 + RUN]

        def two_before(u):
            _, b, *h = u
            former = ("tail", b - 1) if not h else ("head", b, h[0] - 2) if h[0] >= 2 else ("head", b - 1, HEADS + h[0] - 2)
            return nonlinear_of.get(former, -1) + 1

        def free_before(u):
            n = unit_of[u]
            return n % 2, n // 2

        def take_slot(eng, u):
            s, k = free_before(u)
            if k:
                eng.wait_ge(slot_free[s], k)

        def full(eng, u):
            eng.wait_ge(psum_full, unit_of[u] + 1)

        block = ctx.enter_context(nc.Block())

        @block.sync
        def _(sp):
            sp.dma_start(token_sb, token_no).then_inc(token_in, 16)
            for b in range(B):
                sp.dma_start(xn[:, NIN * b:NIN * (b + 1), 0:D],
                             x[b].rearrange("(t p) d -> p t d", p=TIN)).then_inc(x_in[b], 16)
                if b == 0:
                    for dst, src in ((gam_bc, gamma), (bet_bc, beta), (w_bc, w)):
                        sp.dma_start(dst, src.rearrange("(a d) -> a d", a=1).broadcast_to([TIN, D])).then_inc(row_in, 16)
                    sp.dma_start(konst[0:TIN, 1:2], b_score.rearrange("(a d) -> a d", a=1).broadcast_to([TIN, 1])).then_inc(row_in, 16)
            for dst, src in ((wqk_sb[:, 0], wqT), (wqk_sb[:, 1], wkT), (wv_sb, wvT), (wp_sb[:, :, :], wpT),
                             (wg_sb[:, :, :], wg.rearrange("(c p) e -> p c e", c=2)), (cos_sb, rope_cos),
                             (sin_sb, rope_sin), (count_sb[:, :], count.rearrange("(a d) -> a d", a=1).broadcast_to([P, TILES]))):
                sp.dma_start(dst, src).then_inc(w_in, 16)
            sp.wait_ge(pad_set, 1)
            sp.dma_start(disp_d.rearrange("(t p) d -> p t d", p=P),
                         pad_row.unsqueeze(1).broadcast_to([P, TILES, ROW])).then_inc(pad_out, 16)
            sp.dma_start(acc_d[ROWS:ROWS + P, :], pad_row[:, 0:D]).then_inc(pad_out, 16)

            def load_sorted(b):
                sp.wait_ge(scattered[b], 16 * NIN)
                rows = sorted_d[N * b:N * b + KEEP, :].rearrange("(t p) d -> p t d", p=TOK)
                sp.dma_start(z[:, NT * b:NT * (b + 1), 0:D], rows[:, :, D:2 * D]).then_inc(x_loaded[b], 16)
                sp.dma_start(hres[:, NT * b:NT * (b + 1), :], rows[:, :, 0:D]).then_inc(h_loaded[b], 16)

            def stack_parts(m):
                b, qk = m // 2, m % 2
                sp.wait_ge(parts_ready, m + 1)
                sp.dma_start(parts_d[b, qk].rearrange("(a m) s -> m a s", a=6),
                             parts.rearrange("p a b s -> p (a b) s")).then_inc(parts_out, 16)
                sp.wait_ge(parts_out, 16 * (m + 1))
                if b >= 2 and qk == 0:
                    sp.wait_ge(psum_full, unit_of[("head", b - 2, HEADS - 1)] + 1)
                rows = parts_d[b, qk].rearrange("m s -> (m s)").rearrange("(r x) -> r x", r=3 * HD)
                st = stack(b % 2, qk)
                for i, part in enumerate((Q_BLOCKS, K_BLOCKS)[qk]):
                    sp.dma_start(st[HD * i:HD * (i + 1), :], rows[HD * part:HD * (part + 1), :]).then_inc(stack_in[b % 2], 16)

            load_sorted(0)
            stack_parts(0)
            stack_parts(1)
            def store_h(b):
                sp.wait_ge(h_added, b + 1)
                sp.dma_start(acc_d[KEEP * b:KEEP * (b + 1), :].rearrange("(t p) d -> p t d", p=TOK),
                             hres[:, NT * b:NT * (b + 1), :]).then_inc(acc_in, 16)

            for b in range(1, B):
                load_sorted(b)
                stack_parts(2 * b)
                stack_parts(2 * b + 1)
            for b in range(B - 2):
                store_h(b)
            w1_e = w1_sb.rearrange("p (e c f) -> p e c f", e=E, c=2)

            def load_w1(e):
                sp.dma_start(w1_e[0:C, e], w1[e].rearrange("(c p) f -> p c f", c=2)).then_inc(w1_in, 16)
                sp.dma_start(w1_e[C:C + 1, e, 1], b1[e:e + 1, :]).then_inc(w1_in, 16)

            sp.wait_ge(psum_full, unit_of[("v", B - 1)] + 1)
            for e in range(E - 1):
                load_w1(e)
            sp.wait_ge(psum_full, unit_of[("head", B - 1, HEADS - 1)] + 1)
            load_w1(E - 1)
            for e in range(E):
                if e == E - 1:
                    sp.wait_ge(av_done, PAIRS * B)
                sp.dma_start(w2_sb.rearrange("p (e k d) -> p e k d", e=E, k=6)[:, e],
                             w2[e].rearrange("(k p) d -> p k d", k=6)).then_inc(w2_in, 16)
            sp.dma_start(b2_bc, b2.rearrange("(a e) d -> a (e d)", a=1).broadcast_to([P, E * D])).then_inc(b2_in, 16)
            store_h(B - 2)
            store_h(B - 1)
            sp.wait_ge(dispatched, 16 * 2 * NTA)

            def load_tile(par, row):
                sp.dma_start(x_tile[:, par, :], disp_d[bass.ds(row, P), 0:D]).then_inc(tile_in[par], 16)

            load_tile(0, 0)
            load_tile(1, P)
            rows = disp_d.rearrange("(t p) d -> p t d", p=P)
            for group, tiles in enumerate(META_GROUPS):
                sp.dma_start(meta[:, tiles], rows[:, tiles, D:ROW]).then_inc(meta_in[group], 16)
            with sp.Fori(0, TILES // 2 - 1) as j:
                for par in range(2):
                    sp.wait_ge(tT_full, 2 * j + par + 1)
                    load_tile(par, (2 * j + par + 2) * P)
            for par in range(2):
                sp.wait_ge(added[par], 16 * (TILES // 2))
            sp.dma_start(out.rearrange("b s d -> (b s d)").rearrange("(p n) -> p n", p=P),
                         acc_d[0:ROWS, :].rearrange("r d -> (r d)").rearrange("(p n) -> p n", p=P)).then_inc(out_done, 16)
            sp.wait_ge(out_done, 16)

        @block.gpsimd
        def _(g):
            step = [0]

            def link(ins):
                ins.then_inc(pool_step, 1)
                step[0] += 1
                g.wait_ge(pool_step, step[0])

            link(g.memset(pad_row, 0.0))
            g.wait_ge(token_in, 16)
            g.tensor_copy(pad_row[:, D:D + 1], token_sb[:, NTA:NTA + 1]).then_inc(pad_set, 1)
            g.tensor_copy(z[:, :, D:D + 1], token_sb[0:TOK, 0:NTA].unsqueeze(2))
            g.memset(ones[:, :], 1.0)
            g.memset(ident[:, :], 0.0)
            g.memset(later, 1.0)
            g.memset(tri, 0.0)
            link(g.memset(before[:, :], 1.0))
            g.affine_select(out=ident[:, :], in_=ident[:, :], compare_op=ALU.not_equal, fill=1.0, base=0,
                            pattern=[[-1, P]], channel_multiplier=1)
            g.affine_select(out=tri, in_=tri, compare_op=ALU.is_ge, fill=MASKED, base=0,
                            pattern=[[1, P]], channel_multiplier=-1)
            g.affine_select(out=later, in_=later, compare_op=ALU.is_gt, fill=0.0, base=0,
                            pattern=[[-1, TIN]], channel_multiplier=1)
            link(g.affine_select(out=before[:, :], in_=before[:, :], compare_op=ALU.is_gt, fill=0.0, base=0,
                                 pattern=[[1, TOK]], channel_multiplier=-1))
            g.tensor_copy(ident_b, ident[:, :]).then_inc(const_set, 1)
            for b in range(B):
                g.wait_ge(idx_ready, b + 1)
                for t in range(NIN * b, NIN * (b + 1)):
                    g.indirect_dma_start(sorted_d, bass.IndirectOffsetOnAxis(idx[0:TIN, t:t + 1], 0),
                                         xn[:, t, :], None).then_inc(scattered[b], 16)

            def rotate(m):
                g.wait_ge(rope_mul, m + 1)
                if m:
                    g.wait_ge(parts_ready, m)
                g.tensor_tensor(rot[:, 0, :], rot_c[:, 0, :], rot_s[:, 1, :], ALU.subtract)
                g.tensor_tensor(rot[:, 1, :], rot_s[:, 0, :], rot_c[:, 1, :], ALU.add).then_inc(rotated, 1)

            def rest(m):
                g.wait_ge(hi_ready, m + 1)
                g.tensor_tensor(rot, rot, parts[:, 0], ALU.subtract).then_inc(rest_ready, 1)

            def low(m):
                g.wait_ge(mid_ready, m + 1)
                g.wait_ge(rest_ready, m + 1)
                if m:
                    g.wait_ge(parts_out, 16 * m)
                g.tensor_tensor(parts[:, 2], rot, parts[:, 1], ALU.subtract).then_inc(parts_ready, 1)

            for u in plan:
                if u[0] in ("q", "k"):
                    rotate(2 * u[1] + (u[0] == "k"))
                elif u[0] == "hi":
                    rest(u[1])
                elif u[0] == "mid":
                    low(u[1])
                elif u[0] == "z":
                    _, b, t = u
                    g.wait_ge(norm_ready, b + 1)
                    t += NT * b
                    g.tensor_scalar(z[:, t, 0:D], hres[:, t, :], mv2[0:TOK, t, 0:1], rs2[0:TOK, t:t + 1],
                                    ALU.subtract, ALU.mult).then_inc(z_ready, 1)
                elif u[0] == "disp":
                    _, b, t = u
                    if b == 0 and t == 0:
                        g.wait_ge(pad_out, 32)
                    g.wait_ge(pos_ready, b + 1)
                    g.wait_ge(z_ready, NT * (b + 1))
                    for pos in (pos1, pos2):
                        g.indirect_dma_start(disp_d, bass.IndirectOffsetOnAxis(pos[:, NT * b + t:NT * b + t + 1], 0),
                                             z[:, NT * b + t, :], None).then_inc(dispatched, 16)
            g.wait_ge(acc_in, 16 * B)

            for group in range(2):
                g.wait_ge(dest_ready, group + 1)

            def add_tile(par, i, former):
                g.tensor_copy(dest_now[:, par:par + 1], dest[:, bass.ds(i, 1)]).then_inc(dest_set, 1)
                g.wait_ge(dest_set, i + 1)
                g.wait_ge(y_out_ready, i + 1)
                if former is not None:
                    g.wait_ge(added[1 - par], former)
                g.sem_inc(add_begun, 1)
                g.indirect_dma_start(acc_d, bass.IndirectOffsetOnAxis(dest_now[:, par:par + 1], 0),
                                     y_tile[:, par, :], None, compute_op=ALU.add).then_inc(added[par], 16)

            add_tile(0, 0, None)
            add_tile(1, 1, 16)
            with g.Fori(1, TILES // 2) as j:
                add_tile(0, 2 * j, 16 * j)
                add_tile(1, 2 * j + 1, 16 * (j + 1))

        @block.scalar
        def _(act):
            def evacuate_T(u, dst, ready):
                full(act, u)
                s = slot(u)
                act.activation(dst[:, 0, 0:4 * TOK], s[0:C, 0:4 * TOK], ACT.Copy)
                act.activation(dst[:, 1, 0:4 * TOK], s[0:C, 512:512 + 4 * TOK], ACT.Copy)
                act.activation(dst[:, :, 4 * TOK:KEEP], s[0:C, 1024:1024 + 2 * TOK].rearrange("p (c s) -> p c s", c=2),
                               ACT.Copy).then_inc(ready, 1)
                act.wait_ge(ready, count_of[u[0]])
                act.sem_inc(slot_free[free_before(u)[0]], 1)

            count_of = {}
            pending = []

            def sigmoids():
                if not pending:
                    return
                u = pending.pop(0)
                n = nonlinear_of[u]
                act.wait_ge(cub_ready, n + 1)
                b = u[1]
                if u[0] == "tail":
                    if b:
                        act.wait_ge(av_done, PAIRS * b)
                    dst = [g_tail[:, i].rearrange("p h s -> p (h s)") for i in range(2)]
                else:
                    pair = PAIRS * b + u[2] // 2
                    if pair >= 2:
                        act.wait_ge(av_done, pair - 1)
                    dst = [sig[:, u[2] % 4, i, :] for i in range(2)]
                src = buffers(u)[1]
                act.activation(dst[0], src, ACT.Sigmoid, scale=2 * K0 * D3 * SCORE_SCALE)
                act.activation(dst[1], src, ACT.Sigmoid, scale=2 * K1 * D3 * SCORE_SCALE).then_inc(sig_ready, 1)

            act.wait_ge(pad_out, 32)
            for b in range(B):
                act.wait_ge(scattered[b], 16 * NIN)
            for u in plan:
                kind = u[0]
                count_of[kind] = count_of.get(kind, 0) + 1
                if kind == "xT":
                    if u[1]:
                        full(act, ("v", u[1] - 1))
                    evacuate_T(u, xT, xT_ready)
                elif kind == "zT":
                    evacuate_T(u, yT, zT_ready)
                elif kind == "yT":
                    if u[1]:
                        full(act, ("logit", u[1] - 1))
                    evacuate_T(u, yT, yT_ready)
                elif kind == "hi":
                    m = u[1]
                    act.wait_ge(rotated, m + 1)
                    if m:
                        act.wait_ge(parts_out, 16 * m)
                    act.activation(parts[:, 0], rot, ACT.Copy).then_inc(hi_ready, 1)
                elif kind == "mid":
                    act.wait_ge(rest_ready, u[1] + 1)
                    act.activation(parts[:, 1], rot, ACT.Copy).then_inc(mid_ready, 1)
                elif kind == "v":
                    full(act, u)
                    s = slot(u)
                    if u[1]:
                        act.wait_ge(av_done, PAIRS * u[1])
                    for i, mix in enumerate((2 * MIX0, 2 * MIX1)):
                        for bank in range(2):
                            act.activation(v_mix5[:, i, 2 * bank:2 * bank + 2, :, 0:HD],
                                           s[:, 512 * bank:512 * bank + 2 * D].rearrange("p (t h d) -> p t h d", t=2, h=HEADS),
                                           ACT.Copy, scale=mix)
                        last = act.activation(v_mix5[0:TAIL, i, 4, :, 0:HD],
                                              s[0:TAIL, 1024:1024 + D].rearrange("p (h d) -> p h d", h=HEADS),
                                              ACT.Copy, scale=mix)
                    last.then_inc(v_ready, 1)
                    act.wait_ge(v_ready, u[1] + 1)
                    act.sem_inc(slot_free[free_before(u)[0]], 1)
                elif kind in ("tail", "head"):
                    n = nonlinear_of[u]
                    full(act, u)
                    before_last = two_before(u)
                    if before_last:
                        act.wait_ge(cub_ready, before_last)
                    s = slot(u)
                    a, _, run = buffers(u)
                    act.activation(a, run, ACT.Square, scale=SCORE_SCALE).then_inc(sq_ready, 1)
                    if on_scalar(u):
                        act.wait_ge(sq_ready, n + 1)
                        act.activation(quad[:, :], a, ACT.Square, bias=half_quad[:, 0:1]).then_inc(quad_ready, 1)
                    sigmoids()
                    pending.append(u)
                elif kind == "flush":
                    sigmoids()
                elif kind == "pick":
                    act.wait_ge(shifted, u[1] + 1)
                    act.activation(prob, cand, ACT.Sigmoid)
                    act.activation(cand2, cand, ACT.Sigmoid, scale=-1.0).then_inc(prob_ready, 1)
                elif kind == "o":
                    q = u[1]
                    act.wait_ge(av_done, 2 * (q + 1))
                    if q >= 2:
                        full(act, ("oT", q - 2))
                    act.activation(o_sb[:, q % 2, 0:S0], o_ps[:, 0:S0], ACT.Copy)
                    act.activation(o_sb[:, q % 2, S0:KEEP], o_ps[:, 512:512 + KEEP - S0], ACT.Copy).then_inc(o_ready, 1)

            act.wait_ge(eid_ready, 1)
            act.wait_ge(w1_in, 16 * 2 * E)

            def copy_w1(par, i):
                e = act.value_load(eid[0:1, bass.ds(i, 1)], min_val=0, max_val=E - 1)
                wait_from_1(act, hid_full, i - 1)
                act.activation(w1_now[0:C, par, 0, :], w1_sb[0:C, bass.ds(e * (2 * F), F)], ACT.Copy).then_inc(w1_copied[0], 1)

            def copy_tT(par, i):
                act.wait_ge(tT_full, i + 1)
                wait_from_1(act, hid_full, i - 1)
                act.activation(x_tT[0:C, par], slots[par][0:C, 0:2 * P].rearrange("p (c t) -> p c t", c=2),
                               ACT.Copy).then_inc(tT_ready, 1)

            def relu_a(par, i):
                act.wait_ge(hid_full, i + 1)
                wait_from_1(act, y_full, i - 1)
                act.activation(hidT[:, par, 0:3], slots[par][:, 512:512 + 3 * P].rearrange("p (k t) -> p k t", k=3),
                               ACT.Relu).then_inc(hid_copied[0], 1)

            def tile_round(par, i):
                copy_tT(par, i + 2)
                relu_a(1 - par, i + 1)
                copy_w1(par, i + 2)

            for par in range(2):
                copy_w1(par, par)
                copy_tT(par, par)
            relu_a(0, 0)
            tile_round(0, 0)
            tile_round(1, 1)
            with act.Fori(1, TILES // 2 - 1) as j:
                for par in range(2):
                    tile_round(par, 2 * j + par)
            relu_a(1, TILES - 1)

        @block.vector
        def _(dve):
            v = nc.vector
            step = [0]

            def link(ins):
                ins.then_inc(vec_step, 1)
                step[0] += 1
                dve.wait_ge(vec_step, step[0])

            def rsqrt(y, t, a):
                link(v.tensor_scalar(y.bitcast(I32), a.bitcast(I32), -0.5, 1597463007.0, ALU.mult, ALU.add))
                for _ in range(3):
                    link(v.tensor_tensor(t, y, y, ALU.mult))
                    link(v.scalar_tensor_tensor(out=t, in0=t, scalar=-0.5, in1=a, op0=ALU.mult, op1=ALU.mult))
                    link(v.scalar_tensor_tensor(out=y, in0=t, scalar=1.5, in1=y, op0=ALU.add, op1=ALU.mult))

            v.memset(cnt[0:TIN], 0.0)
            v.memset(half_quad, QUAD1 / 2)
            v.memset(o_ps[:, :], 0.0)
            v.memset(v_mix5[:, 0, :, :, HD:HD + 1], 2 * MIX0)
            link(v.memset(v_mix5[:, 1, :, :, HD:HD + 1], 2 * MIX1))
            dve.wait_ge(row_in, 64)
            v.tensor_tensor(gw, gam_bc, w_bc, ALU.mult)
            link(v.scalar_tensor_tensor(out=junk, in0=bet_bc, scalar=1.0, in1=w_bc, op0=ALU.mult, op1=ALU.mult,
                                        accum_out=konst[0:TIN, 0:1]))
            link(v.tensor_tensor(konst[0:TIN, 0:1], konst[0:TIN, 0:1], konst[0:TIN, 1:2], ALU.add))

            def score_batch(b):
                dve.wait_ge(x_in[b], 16)
                tiles = range(NIN * b, NIN * (b + 1))
                for t in tiles:
                    last = v.bn_stats(stats[0:TIN, t % NIN, :], xn[:, t, 0:D])
                link(last)
                for t in tiles:
                    last = v.bn_aggr(mv[0:TIN, t, :], stats[0:TIN, t % NIN, :])
                link(last)
                s = slice(NIN * b, NIN * (b + 1))
                link(v.tensor_scalar(var_e[0:TIN, s], mv[0:TIN, s, 1], LN_EPS, None, ALU.add))
                rsqrt(rs[0:TIN, s], rs_t[0:TIN, s], var_e[0:TIN, s])
                for t in tiles:
                    last = v.tensor_scalar(xn[:, t, D:2 * D], xn[:, t, 0:D], mv[0:TIN, t, 0:1], rs[0:TIN, t:t + 1],
                                           ALU.subtract, ALU.mult)
                link(last)
                for t in tiles:
                    last = v.scalar_tensor_tensor(out=junk, in0=xn[:, t, D:2 * D], scalar=1.0, in1=gw,
                                                  op0=ALU.mult, op1=ALU.mult, accum_out=score[0:TIN, t:t + 1])
                    link(last)
                link(v.tensor_scalar(score[0:TIN, s], score[0:TIN, s], konst[0:TIN, 0:1], None, ALU.add))
                if b == 0:
                    dve.wait_ge(const_set, 1)
                else:
                    full(dve, ("rank", b - 1))
                v.tensor_tensor(sdiag, ident[0:TIN, 0:TIN].unsqueeze(1).broadcast_to([TIN, NIN, TIN]),
                                score[0:TIN, s].unsqueeze(2).broadcast_to([TIN, NIN, TIN]), ALU.mult).then_inc(diag_ready, 1)

            def rank_batch(b):
                u = ("rank", b)
                full(dve, u)
                ps = slot(u)
                for t in range(NIN):
                    tt = NIN * b + t
                    s = score[0:TIN, tt:tt + 1]
                    c0, c1 = TIN * t, TIN * (t + 1)
                    if t:
                        link(v.tensor_scalar(cmp_junk[:, 0:c0], ps[0:TIN, 0:c0], s, None, ALU.is_ge, ALU.add,
                                             accum_out=cnt[0:TIN, tt, 0:1]))
                    if t < NIN - 1:
                        link(v.tensor_scalar(cmp_junk[:, c1:N], ps[0:TIN, c1:N], s, None, ALU.is_gt, ALU.add,
                                             accum_out=cnt[0:TIN, tt, 1:2]))
                    link(v.tensor_scalar(cmp_junk[:, c0:c1], ps[0:TIN, c0:c1], s, None, ALU.is_gt, ALU.add,
                                         accum_out=cnt[0:TIN, tt, 2:3]))
                    link(v.scalar_tensor_tensor(out=cmp_junk[:, c0:c1], in0=ps[0:TIN, c0:c1], scalar=s, in1=later,
                                                op0=ALU.is_equal, op1=ALU.mult, accum_out=cnt[0:TIN, tt, 3:4]))
                dve.sem_inc(slot_free[free_before(u)[0]], 1)
                s = slice(NIN * b, NIN * (b + 1))
                link(v.tensor_reduce(rs_t[0:TIN, s], cnt[0:TIN, s, :], AX.X, ALU.add))
                v.tensor_scalar(idx[0:TIN, s], rs_t[0:TIN, s], float(N * b), None, ALU.add).then_inc(idx_ready, 1)

            score_batch(0)
            for b in range(B):
                if b + 1 < B:
                    score_batch(b + 1)
                rank_batch(b)

            def wide8(a):
                return a.unsqueeze(2).broadcast_to([TOK, NT, E])

            numbers = count_sb[0:TOK, 0:E].unsqueeze(1).broadcast_to([TOK, NT, E])

            def pick(top, hot):
                link(v.tensor_reduce(top, prob, AX.X, ALU.max))
                link(v.tensor_tensor(cand, prob, wide8(top), ALU.is_equal))
                link(v.scalar_tensor_tensor(out=cand, in0=cand, scalar=-float(E), in1=numbers, op0=ALU.mult, op1=ALU.add))
                link(v.tensor_reduce(ind, cand, AX.X, ALU.min))
                link(v.tensor_scalar(ind, ind, float(E), None, ALU.add))
                link(v.tensor_tensor(hot, numbers, wide8(ind), ALU.is_equal))

            def choose_first(b):
                dve.wait_ge(prob_ready, b + 1)
                link(v.reciprocal(cand2, cand2))
                link(v.tensor_tensor(prob, prob, cand2, ALU.mult))
                link(v.tensor_reduce(sums, prob, AX.X, ALU.add))
                link(v.reciprocal(sums, sums))
                link(v.tensor_tensor(prob, prob, wide8(sums), ALU.mult))
                pick(top1, hot1)
                v.tensor_copy(z[:, NT * b:NT * (b + 1), D + 1], ind)

            def choose_second(b):
                tt = slice(NT * b, NT * (b + 1))
                link(v.scalar_tensor_tensor(out=prob, in0=hot1, scalar=-2.0, in1=prob, op0=ALU.mult, op1=ALU.add))
                pick(top2, hot2)
                v.tensor_tensor(both, hot1, hot2, ALU.add).then_inc(hot_ready, 1)
                link(v.tensor_tensor(sums, top1, top2, ALU.add))
                link(v.reciprocal(sums, sums))
                v.tensor_tensor(z[:, tt, D + 2], top1, sums, ALU.mult)
                link(v.tensor_tensor(z[:, tt, D + 3], top2, sums, ALU.mult))

            def count_rows(u):
                full(dve, u)
                ps = slot(u)
                link(v.tensor_copy(totals, ps[:, 512:512 + NT * E].rearrange("p (t e) -> p e t", e=E)))
                link(v.tensor_tensor_scan(run_tot.rearrange("p e t -> p (e t)"), carry.rearrange("p e t -> p (e t)"),
                                          totals.rearrange("p e t -> p (e t)"), 0.0, ALU.mult, ALU.add))
                link(v.tensor_tensor(n_new, rows_e, run_tot[:, :, NT - 1], ALU.add))
                link(v.tensor_scalar(c_int, n_new, float(P - 1), None, ALU.add))
                link(v.tensor_scalar(c_int, c_int, 7, None, ALU.arith_shift_right))
                link(v.tensor_copy(c_new, c_int))
                link(v.tensor_tensor(tmp_e, c_new, chunks_e, ALU.subtract))
                link(v.tensor_tensor_scan(ends, ones[:, 0:E], tmp_e, used_tiles, ALU.mult, ALU.add))
                link(v.tensor_tensor(base, ends, tmp_e, ALU.subtract))
                link(v.tensor_tensor(run_tot, run_tot, totals, ALU.subtract))
                link(v.tensor_tensor(run_tot, run_tot, rows_e.unsqueeze(2).broadcast_to([P, E, NT]), ALU.add))
                link(v.tensor_tensor(posf, ps[0:TOK, 0:NT * E].rearrange("p (t e) -> p t e", e=E),
                                     run_tot[0:TOK].rearrange("p e t -> p t e"), ALU.add))
                dve.sem_inc(slot_free[free_before(u)[0]], 1)

            def per_e(a):
                return a[0:TOK].unsqueeze(1).broadcast_to([TOK, NT, E])

            def place_rows(b):
                link(v.tensor_scalar(old_e, chunks_e, float(P), None, ALU.mult))
                link(v.tensor_tensor(cand2, posf, per_e(old_e), ALU.is_lt))
                link(v.tensor_tensor(old_e, last_tile, base, ALU.subtract))
                link(v.tensor_scalar(old_e, old_e, 1.0, None, ALU.add))
                link(v.tensor_tensor(cand2, cand2, per_e(old_e), ALU.mult))
                link(v.tensor_tensor(old_e, base, chunks_e, ALU.subtract))
                link(v.tensor_tensor(cand2, cand2, per_e(old_e), ALU.add))
                link(v.scalar_tensor_tensor(out=posf, in0=cand2, scalar=float(P), in1=posf, op0=ALU.mult, op1=ALU.add))
                tt = slice(NT * b, NT * (b + 1))
                for hot, pos in ((hot1, pos1), (hot2, pos2)):
                    link(v.tensor_tensor(cand2, posf, hot, ALU.mult))
                    link(v.tensor_reduce(ind, cand2, AX.X, ALU.add))
                    link(v.tensor_copy(pos[:, tt], ind))
                dve.sem_inc(pos_ready, 1)

            def note_tiles():
                link(v.tensor_scalar(tmp_e, tmp_e, 0.0, None, ALU.is_gt))
                link(v.tensor_tensor(old_e, ends, last_tile, ALU.subtract))
                link(v.scalar_tensor_tensor(out=old_e, in0=old_e, scalar=-1.0, in1=tmp_e, op0=ALU.add, op1=ALU.mult))
                v.tensor_tensor(last_tile, last_tile, old_e, ALU.add)
                v.tensor_copy(rows_e, n_new)
                v.tensor_copy(chunks_e, c_new)
                v.tensor_copy(used_tiles, ends[:, E - 1:E])
                link(v.tensor_scalar(eid_add, count_sb[:, :], ends[:, 0:1], None, ALU.is_ge))
                for e in range(1, E):
                    link(v.scalar_tensor_tensor(out=eid_add, in0=count_sb[:, :], scalar=ends[:, e:e + 1], in1=eid_add,
                                                op0=ALU.is_ge, op1=ALU.add))
                link(v.scalar_tensor_tensor(out=eid_add, in0=eid_add, scalar=float(E), in1=eid_add, op0=ALU.is_lt, op1=ALU.mult))
                link(v.tensor_tensor(eid_f, eid_f, eid_add, ALU.add))

            for a in (rows_e, chunks_e, last_tile, used_tiles, eid_f):
                v.memset(a, 0.0)
            link(v.memset(carry, 1.0))
            link(v.memset(carry[:, :, 0:1], 0.0))

            quads = {True: 0, False: 0}

            dve.wait_ge(w_in, 16 * 8)
            for u in plan:
                kind = u[0]
                if kind in ("q", "k"):
                    m = 2 * u[1] + (kind == "k")
                    full(dve, u)
                    s = slot(u)
                    if m:
                        dve.wait_ge(rotated, m)
                    wide = s[0:C, 0:1024].rearrange("p (a s) -> p a s", a=2)[:, :, 0:350]
                    rest_ = s[0:C, 1024:1374].rearrange("p (a s) -> p a s", a=2)
                    for table, dst in ((cos_sb, rot_c), (sin_sb, rot_s)):
                        v.tensor_tensor(dst[:, :, 0:350], wide, table[:, 0:350].unsqueeze(1).broadcast_to([C, 2, 350]), ALU.mult)
                        last = v.tensor_tensor(dst[:, :, 350:KEEP], rest_, table[:, 350:KEEP].unsqueeze(1).broadcast_to([C, 2, 175]), ALU.mult)
                    last.then_inc(rope_mul, 1)
                    dve.wait_ge(rope_mul, m + 1)
                    dve.sem_inc(slot_free[free_before(u)[0]], 1)
                elif kind in ("tail", "head"):
                    n = nonlinear_of[u]
                    a, c, run = buffers(u)
                    dve.wait_ge(sq_ready, n + 1)
                    before_last = two_before(u)
                    if before_last:
                        dve.wait_ge(sig_ready, before_last)
                    v.scalar_tensor_tensor(out=c, in0=a, scalar=ROOT, in1=run, op0=ALU.add, op1=ALU.mult).then_inc(lin_ready, 1)
                    if on_scalar(u):
                        factor, const, done = quad[:, :], QUAD0 - QUAD1 * QUAD1 / 4, quad_ready
                    else:
                        v.scalar_tensor_tensor(out=a, in0=a, scalar=QUAD1, in1=a, op0=ALU.add, op1=ALU.mult).then_inc(quad_v, 1)
                        factor, const, done = a, QUAD0, quad_v
                    dve.wait_ge(lin_ready, n + 1)
                    dve.sem_inc(slot_free[free_before(u)[0]], 1)
                    quads[on_scalar(u)] += 1
                    dve.wait_ge(done, quads[on_scalar(u)])
                    v.scalar_tensor_tensor(out=c, in0=factor, scalar=const, in1=c, op0=ALU.add, op1=ALU.mult).then_inc(cub_ready, 1)
                elif kind == "oT":
                    q = u[1]
                    full(dve, u)
                    if q % 3 == 0 and q:
                        full(dve, ("yT", q // 3 - 1))
                    o = slot(u)[0:TOK, 0:NT * P].rearrange("p (t h d) -> p t h d", t=NT, h=4)
                    link(v.tensor_scalar(den[0:TOK], o[:, :, :, HD], DEN_EPS, None, ALU.max))
                    link(v.reciprocal(den[0:TOK], den[0:TOK]))
                    g4 = q % 3
                    y4 = y_sb[:, :, 64 * g4:64 * g4 + 64].rearrange("p t (h d) -> p t h d", h=4)
                    for t in range(NT):
                        last = v.tensor_tensor(y4[:, t], o[:, t, :, 0:HD],
                                               den[0:TOK, t].unsqueeze(2).broadcast_to([TOK, 4, HD]), ALU.mult)
                    last.then_inc(y_ready, 1)
                    dve.wait_ge(y_ready, q + 1)
                    dve.sem_inc(slot_free[free_before(u)[0]], 1)
                elif kind == "proj":
                    b = u[1]
                    full(dve, u)
                    dve.wait_ge(h_loaded[b], 16)
                    s = slot(u)
                    for t in range(NT):
                        at = 512 * (t // 2) + D * (t % 2)
                        last = v.tensor_tensor(hres[:, NT * b + t, :], s[0:TOK, at:at + D], hres[:, NT * b + t, :], ALU.add)
                    link(last)
                    dve.sem_inc(slot_free[free_before(u)[0]], 1)
                    dve.sem_inc(h_added, 1)
                    for t in range(NT):
                        last = v.bn_stats(stats2[:, t, :], hres[:, NT * b + t, :])
                    link(last)
                    for t in range(NT):
                        last = v.bn_aggr(mv2[0:TOK, NT * b + t, :], stats2[:, t, :])
                    link(last)
                    s5 = slice(NT * b, NT * (b + 1))
                    link(v.tensor_scalar(var2[0:TOK], mv2[0:TOK, s5, 1], LN_EPS, None, ALU.add))
                    rsqrt(rs2[0:TOK, s5], rs2_t[0:TOK], var2[0:TOK])
                    dve.sem_inc(norm_ready, 1)
                elif kind == "logit":
                    full(dve, u)
                    raw = slot(u)[0:TOK, 0:NT * E].rearrange("p (t e) -> p t e", t=NT)
                    link(v.tensor_reduce(ind, raw, AX.X, ALU.max))
                    if u[1]:
                        dve.wait_ge(hot_ready, u[1])
                    v.tensor_tensor(cand, raw, wide8(ind), ALU.subtract).then_inc(shifted, 1)
                    dve.wait_ge(shifted, u[1] + 1)
                    dve.sem_inc(slot_free[free_before(u)[0]], 1)
                elif kind == "pick":
                    choose_first(u[1])
                elif kind == "pick2":
                    choose_second(u[1])
                elif kind == "count":
                    count_rows(u)
                elif kind == "place":
                    place_rows(u[1])
                elif kind == "note":
                    note_tiles()

            dve.wait_ge(av_done, PAIRS * B)
            v.tensor_copy(eid, eid_f).then_inc(eid_ready, 1)
            v.memset(x_tT[C:C + 1, :, 1, :], 1.0).then_inc(ones_row, 1)
            dve.wait_ge(b2_in, 16)
            dve.wait_ge(eid_ready, 1)
            dve.wait_ge(w1_in, 16 * 2 * E)

            def copy_w1(par, i):
                e = dve.value_load(eid[0:1, bass.ds(i, 1)], min_val=0, max_val=E - 1)
                wait_from_1(dve, hid_full, i - 1)
                v.tensor_copy(w1_now[:, par, 1, :], w1_sb[0:C + 1, bass.ds(e * (2 * F) + F, F)]).then_inc(w1_copied[1], 1)

            def relu_b(par, i):
                dve.wait_ge(hid_full, i + 1)
                wait_from_1(dve, y_full, i - 1)
                v.tensor_scalar(hidT[:, par, 3:6], slots[par][:, 1024:1024 + 3 * P].rearrange("p (k t) -> p k t", k=3),
                                0.0, None, ALU.max).then_inc(hid_copied[1], 1)

            def row_weights(group):
                t = META_GROUPS[group]
                dve.wait_ge(meta_in[group], 16)
                first, mine = meta[:, t, 1], eid_f[:, t]
                v.tensor_copy(dest[:, t], meta[:, t, 0]).then_inc(dest_ready, 1)
                link(v.tensor_tensor(weight[:, t], first, mine, ALU.is_equal))
                link(v.tensor_tensor(weight[:, t], weight[:, t], meta[:, t, 2], ALU.mult))
                link(v.tensor_tensor(weight2[:, t], first, mine, ALU.not_equal))
                link(v.tensor_tensor(weight2[:, t], weight2[:, t], meta[:, t, 3], ALU.mult))
                link(v.tensor_tensor(weight[:, t], weight[:, t], weight2[:, t], ALU.add))

            def weigh_result(par, i, j):
                e = dve.value_load(eid[0:1, bass.ds(i, 1)], min_val=0, max_val=E - 1)
                dve.wait_ge(y_full, i + 1)
                v.tensor_tensor(b2_row, o_ps[:, 512 * par:512 * par + D], b2_bc[:, bass.ds(e * D, D)], ALU.add).then_inc(y_copied, 1)
                dve.wait_ge(y_copied, i + 1)
                wait_from_1(dve, added[par], 16 * j)
                v.tensor_scalar(y_tile[:, par, :], b2_row, weight[:, bass.ds(i, 1)], None, ALU.mult).then_inc(y_out_ready, 1)
                dve.wait_ge(y_out_ready, i + 1)

            def tile_round(par, i, j):
                relu_b(1 - par, i + 1)
                copy_w1(par, i + 2)
                weigh_result(par, i, j)

            copy_w1(0, 0)
            copy_w1(1, 1)
            relu_b(0, 0)
            row_weights(0)
            tile_round(0, 0, 0)
            row_weights(1)
            tile_round(1, 1, 0)
            with dve.Fori(1, TILES // 2 - 1) as j:
                for par in range(2):
                    tile_round(par, 2 * j + par, j)
            relu_b(1, TILES - 1)
            weigh_result(0, TILES - 2, TILES // 2 - 1)
            weigh_result(1, TILES - 1, TILES // 2 - 1)

        @block.tensor
        def _(pe):
            def transposes(u, src, tile0):
                s = slot(u)
                for t in range(NT):
                    for c in range(2):
                        dst = s[0:C, 512 * c + TOK * t:512 * c + TOK * (t + 1)] if t < 4 else \
                            s[0:C, 1024 + TOK * c:1024 + TOK * (c + 1)]
                        last = pe.transpose(dst, src[:, tile0 + t, C * c:C * (c + 1)], ident[0:TOK, 0:TOK])
                last.then_inc(psum_full, 1)

            pe.wait_ge(const_set, 1)
            for u in plan:
                kind = u[0]
                if kind in SLOTTED:
                    take_slot(pe, u)
                    s = slot(u)
                if kind == "rank":
                    pe.wait_ge(diag_ready, u[1] + 1)
                    pe.matmul(s[0:TIN, 0:4 * TIN], ones[0:TIN, 0:TIN], sdiag[:, 0:4, :], start=True, stop=True)
                    flat = sdiag.rearrange("p t j -> p (t j)")
                    pe.matmul(s[0:TIN, 500:512], ones[0:TIN, 0:TIN], flat[:, 500:512], start=True, stop=True)
                    pe.matmul(s[0:TIN, 512:N], ones[0:TIN, 0:TIN], flat[:, 512:N], start=True, stop=True).then_inc(psum_full, 1)
                elif kind == "xT":
                    pe.wait_ge(x_loaded[u[1]], 16)
                    transposes(u, z, NT * u[1])
                elif kind in ("q", "k"):
                    pe.wait_ge(xT_ready, u[1] + 1)
                    pe.wait_ge(w_in, 16 * 8)
                    for two in range(2):
                        for lo, hi, at in ((0, 350, 512 * two), (350, KEEP, 1024 + 175 * two)):
                            for c in range(2):
                                last = pe.matmul(s[0:C, at:at + hi - lo], wqk_sb[:, int(kind == "k"), c, two, :],
                                                 xT[:, c, lo:hi], start=(c == 0), stop=(c == 1))
                    last.then_inc(psum_full, 1)
                elif kind == "v":
                    for t in range(NT):
                        n = min(P, KEEP - P * t)
                        at = 512 * (t // 2) + D * (t % 2)
                        for c in range(2):
                            last = pe.matmul(s[0:n, at:at + D], xT[:, c, P * t:P * t + n], wv_sb[:, c, :],
                                             start=(c == 0), stop=(c == 1))
                    last.then_inc(psum_full, 1)
                elif kind in ("tail", "head"):
                    b = u[1]
                    pe.wait_ge(stack_in[b % 2], 16 * 16 * (b // 2 + 1))
                    qs = stack(b % 2, 0).rearrange("p (h s) -> p h s", h=HEADS)
                    ks = stack(b % 2, 1).rearrange("p (h s) -> p h s", h=HEADS)
                    if kind == "tail":
                        pe.matmul(s[0:TAIL, 0:HEADS * TAIL], ident_b[0:TAIL, 0:TAIL],
                                  tri[0:TAIL, 0:TAIL].unsqueeze(1).broadcast_to([TAIL, HEADS, TAIL]),
                                  start=True, stop=False)
                        for h in range(HEADS):
                            last = pe.matmul(s[0:TAIL, TAIL * h:TAIL * (h + 1)], ks[:, h, 512:KEEP], qs[:, h, 512:KEEP],
                                             start=False, stop=(h == HEADS - 1))
                    else:
                        h = u[2]
                        for kt, q0, n, at in PIECES:
                            c0 = q0 - P * kt
                            m = min(P - c0, n)
                            o0 = RUN0 + at
                            key = ks[:, h, P * kt:P * (kt + 1)]
                            pe.matmul(s[:, o0:o0 + m], ident_b, tri[:, c0:c0 + m], start=True, stop=False)
                            last = pe.matmul(s[:, o0:o0 + m], key, qs[:, h, q0:q0 + m], start=False, stop=True)
                            if m < n:
                                last = pe.matmul(s[:, o0 + m:o0 + n], key, qs[:, h, q0 + m:q0 + n], start=True, stop=True)
                    last.then_inc(psum_full, 1)
                elif kind == "av":
                    _, pair, m = u
                    b, h0 = pair // PAIRS, 2 * (pair % PAIRS)
                    if m == 0:
                        pe.wait_ge(v_ready, b + 1)
                        pe.wait_ge(sig_ready, nonlinear_of[("head", b, h0 + 1)] + 1)
                        if pair >= 2:
                            pe.wait_ge(o_ready, pair // 2)
                    for n, (kt, q0, width, at) in enumerate(PIECES):
                        o0 = 512 + q0 - S0 if q0 >= S0 else q0
                        for h in (h0, h0 + 1):
                            row = 32 * (h % 4)
                            pe.matmul(o_ps[row:row + HD + 1, o0:o0 + width], v_mix5[:, m, kt, h, :], sig[:, h % 4, m, at:at + width],
                                      start=(m == 0 and (n == 0 or q0 < S0)), stop=(m == 1 and q0 < S0))
                    if m == 1:
                        pe.wait_ge(sig_ready, nonlinear_of[("tail", b)] + 1)
                        for i in range(2):
                            for h in (h0, h0 + 1):
                                row = 32 * (h % 4)
                                last = pe.matmul(o_ps[row:row + HD + 1, 512 + 512 - S0:512 + KEEP - S0],
                                                 v_mix5[0:TAIL, i, 4, h, :], g_tail[:, i, h, :], start=False, stop=(i == 1))
                        last.then_inc(av_done, 1)
                elif kind == "oT":
                    q = u[1]
                    pe.wait_ge(o_ready, q + 1)
                    for t in range(NT):
                        last = pe.transpose(s[0:TOK, P * t:P * (t + 1)], o_sb[:, q % 2, TOK * t:TOK * (t + 1)], ident[:, :])
                    last.then_inc(psum_full, 1)
                elif kind == "yT":
                    pe.wait_ge(y_ready, 3 * (u[1] + 1))
                    transposes(u, y_sb, 0)
                elif kind == "proj":
                    pe.wait_ge(yT_ready, u[1] + 1)
                    for t in range(NT):
                        at = 512 * (t // 2) + D * (t % 2)
                        for c in range(2):
                            last = pe.matmul(s[0:TOK, at:at + D], yT[:, c, TOK * t:TOK * (t + 1)], wp_sb[:, c, :],
                                             start=(c == 0), stop=(c == 1))
                    last.then_inc(psum_full, 1)
                elif kind == "zT":
                    pe.wait_ge(z_ready, NT * (u[1] + 1))
                    transposes(u, z, NT * u[1])
                elif kind == "count":
                    pe.wait_ge(hot_ready, u[1] + 1)
                    flat = both.rearrange("p t e -> p (t e)")
                    pe.matmul(s[0:TOK, 0:NT * E], before[:, :], flat, start=True, stop=True)
                    pe.matmul(s[:, 512:512 + NT * E], ones[0:TOK, :], flat, start=True, stop=True).then_inc(psum_full, 1)
                elif kind == "logit":
                    pe.wait_ge(zT_ready, u[1] + 1)
                    for t in range(NT):
                        for c in range(2):
                            last = pe.matmul(s[0:TOK, E * t:E * (t + 1)], yT[:, c, TOK * t:TOK * (t + 1)], wg_sb[:, c, :],
                                             start=(c == 0), stop=(c == 1))
                    last.then_inc(psum_full, 1)

            for sl in range(2):
                pe.wait_ge(slot_free[sl], (len(unit_of) + 1 - sl) // 2)
            pe.wait_ge(eid_ready, 1)
            pe.wait_ge(w1_in, 16 * 2 * E)
            pe.wait_ge(w2_in, 16 * E)
            pe.wait_ge(ones_row, 1)
            pe.wait_ge(o_ready, 3 * B)

            def transpose_in(par, i, j):
                pe.wait_ge(tile_in[par], 16 * (j + 1))
                wait_from_1(pe, tT_ready, i - 1)
                pe.transpose(slots[par][0:C, 0:P], x_tile[:, par, 0:C], ident[:, :])
                pe.transpose(slots[par][0:C, P:2 * P], x_tile[:, par, C:D], ident[:, :]).then_inc(tT_full, 1)

            def multiply_w1(par, i):
                pe.wait_ge(tT_ready, i + 1)
                for half in range(2):
                    pe.wait_ge(w1_copied[half], i + 1)
                    wait_from_1(pe, hid_copied[half], i - 1)
                for f in range(F // P):
                    at = 512 * (1 + f // 3) + P * (f % 3)
                    for c, k in ((0, C), (1, C + 1)):
                        last = pe.matmul(slots[par][:, at:at + P], w1_now[0:k, par, c, P * f:P * (f + 1)], x_tT[0:k, par, c, :],
                                         start=(c == 0), stop=(c == 1))
                last.then_inc(hid_full, 1)

            def multiply_w2(par, i):
                e = pe.value_load(eid[0:1, bass.ds(i, 1)], min_val=0, max_val=E - 1)
                for half in range(2):
                    pe.wait_ge(hid_copied[half], i + 1)
                wait_from_1(pe, y_copied, i - 1)
                for k in range(F // P):
                    last = pe.matmul(o_ps[:, 512 * par:512 * par + D], hidT[:, par, k, :],
                                     w2_sb[:, bass.ds(e * (6 * D) + k * D, D)], start=(k == 0), stop=(k == F // P - 1))
                last.then_inc(y_full, 1)

            def tile_round(par, i, j):
                transpose_in(par, i + 2, j + 1)
                multiply_w1(1 - par, i + 1)
                multiply_w2(par, i)

            transpose_in(0, 0, 0)
            transpose_in(1, 1, 0)
            multiply_w1(0, 0)
            tile_round(0, 0, 0)
            tile_round(1, 1, 0)
            with pe.Fori(1, TILES // 2 - 1) as j:
                for par in range(2):
                    tile_round(par, 2 * j + par, j)
            multiply_w1(1, TILES - 1)
            multiply_w2(0, TILES - 2)
            multiply_w2(1, TILES - 1)


def kernel(x, L0_tok_gamma, L0_tok_beta, L0_tok_w, L0_tok_b, L0_attn_Wq, L0_attn_Wk, L0_attn_Wv, L0_attn_Wproj,
           L0_ffn_Wg, L0_ffn_W1, L0_ffn_b1, L0_ffn_W2, L0_ffn_b2):
    import concourse.bacc as bacc
    from concourse.bass_utils import run_bass_kernel_spmd

    def chunks(w):
        return np.ascontiguousarray(np.asarray(w).reshape(D, 2, C).transpose(2, 1, 0))

    def rotary_chunks(w):
        return np.ascontiguousarray(np.asarray(w).reshape(HEADS, HALF, 2, 2, C).transpose(4, 3, 2, 1, 0)).reshape(C, 2, 2, C)

    freq = (np.float32(1.0) / np.float32(10000.0) ** (np.arange(HALF, dtype=np.float32) / np.float32(HALF))).astype(np.float32)
    angle = (np.repeat(freq, HEADS)[:, None] * np.arange(KEEP, dtype=np.float32)[None, :]).astype(np.float32)
    arrays = {
        "x": x, "gamma": L0_tok_gamma, "beta": L0_tok_beta, "w": L0_tok_w, "b_score": L0_tok_b,
        "wqT": rotary_chunks(L0_attn_Wq), "wkT": rotary_chunks(L0_attn_Wk),
        "wvT": chunks(L0_attn_Wv), "wpT": chunks(L0_attn_Wproj),
        "wg": L0_ffn_Wg, "w1": L0_ffn_W1, "b1": L0_ffn_b1, "w2": L0_ffn_W2, "b2": L0_ffn_b2,
        "rope_cos": np.cos(angle), "rope_sin": np.sin(angle), "count": np.arange(TILES, dtype=np.float32),
        "token_no": np.concatenate([np.arange(P)[:, None] + TOK * np.arange(NTA)[None, :], ROWS + np.arange(P)[:, None]],
                                   axis=1).astype(np.float32),
    }
    nc = bacc.Bacc("TRN2", target_bir_lowering=False, num_devices=1)
    arrays = {k: np.ascontiguousarray(a) for k, a in arrays.items()}
    args = [nc.dram_tensor(k, a.shape, mybir.dt.from_np(a.dtype), kind="ExternalInput").ap() for k, a in arrays.items()]
    out = nc.dram_tensor("out", (B, KEEP, D), F32, kind="ExternalOutput").ap()
    build_program(nc, *args, out)
    result = run_bass_kernel_spmd(nc, [arrays], core_ids=[0])
    return result.results[0]["out"]
```

```python
from contextlib import ExitStack

import numpy as np

import concourse.bass as bass
from concourse import mybir

F32 = mybir.dt.float32
BF16 = mybir.dt.bfloat16
I32 = mybir.dt.int32
U32 = mybir.dt.uint32
ALU = mybir.AluOpType
ACT = mybir.ActivationFunctionType
AX = mybir.AxisListType

B, N, D = 4, 750, 192
KEEP = int(N * 0.7)
HEADS, HD = 12, 16
E, F = 8, 768
TIN, NIN = 125, 6
TOK, NT = 105, 5
C = D // 2
PAIRS = HEADS // 2
GROUPS = ((0, B - 1), (B - 1, B))
HALF = HD // 2
P = 128
NTA = B * NT
ROWS = B * KEEP
SMALL = 690
TILES = (2 * ROWS + E * (P - 1)) // P
META_GROUPS = (slice(0, 8), slice(8, TILES))
ROW = D + 4
LN_EPS = 1e-5
DEN_EPS = 1e-6

S0 = 115
PIECES = [(0, S0, KEEP - S0, 0), (1, 128, KEEP - 128, 410), (0, 0, S0, 807),
          (2, 256, KEEP - 256, 922), (3, 384, KEEP - 384, 1191)]
RUN = 1332
RUN0 = 512 - (KEEP - S0)
TAIL = KEEP - 512

D1, D2, D3 = 0.10836966378404583, -0.0026960067293568426, 4.653028531935965e-05
ROOT = -float(min(np.roots([1.0, D2 / D3, D1 / D3, 1.0 / D3]), key=lambda z: abs(z.imag)).real)
QUAD1, QUAD0 = D2 / D3 - ROOT, 1.0 / (D3 * ROOT)
K0, K1 = 1.01124489655701, 1.274538823519078
MIX0 = 0.555126294782942
MIX1 = 1.0 - MIX0
SCORE_SCALE = 1.0 / HD ** 0.5

Q_BLOCKS = [0, 0, 0, 1, 1, 1, 2, 2]
K_BLOCKS = [0, 1, 2, 0, 1, 2, 0, 1]
W1_LATE = (4,)
MASKED = -1e6


ROTARY_AT = (3, 4, 5, 5, 7, 8)
ROUTER_AT = ((18, 20, 21, 22, 23), (16, 18, 19, 20, 21))
PLACES_AT = (22, 23, 24, 24, 24)


def build_plan():
    plan = [("score", 0), ("rank", 0), ("scatter", 0), ("score", 1), ("score", 2), ("rank", 1), ("scatter", 1),
            ("xT", 0), ("q", 0), ("hi", 0), ("mid", 0), ("score", 3), ("k", 0), ("hi", 1), ("mid", 1),
            ("rank", 2), ("scatter", 2), ("rank", 3), ("scatter", 3), ("v", 0), ("tail", 0)]
    after = {(b, h): [] for b in range(B) for h in range(HEADS)}

    def late(b, h):
        return after.get((b + h // HEADS, h % HEADS), ending)

    ending = []
    for b in range(B):
        if b:
            late(b, 2).append(("v", b))
            late(b, 2).append(("tail", b))
        for pair in range(HEADS // 2):
            late(b, 2 * pair + 3).append(("av", 6 * b + pair, 0))
            late(b, 2 * pair + 4).append(("av", 6 * b + pair, 1))
        for g in range(3):
            late(b, 4 * g + 6).append(("o", 3 * b + g))
            late(b, 4 * g + 7).append(("oT", 3 * b + g))
        if b + 1 < B:
            late(b, 2).append(("xT", b + 1))
            for h, u in zip(ROTARY_AT, (("q", b + 1), ("hi", 2 * b + 2), ("mid", 2 * b + 2),
                                        ("k", b + 1), ("hi", 2 * b + 3), ("mid", 2 * b + 3)), strict=True):
                late(b, h).append(u)
        for h, u in zip(ROUTER_AT[b == B - 2], ("yT", "proj", "z", "zT", "logit"), strict=True):
            late(b, h).append((u, b))
        if b >= B - 2:
            g = b - (B - 2)
            for h, u in zip(PLACES_AT, ("pick", "pick2", "count", "place", "note"), strict=True):
                late(b, h).append((u, g))
            for t in range(NT * GROUPS[g][0], NT * GROUPS[g][1]):
                late(b, 24).append(("disp", g, t))
    for b in range(B):
        for h in range(HEADS):
            after[b, h].sort(key=lambda u: ("av", "o", "oT", "v", "xT").index(u[0]) if u[0] in ("av", "o", "oT", "v", "xT") else 9)
            plan += [("head", b, h)] + after[b, h]
    stages = [("yT", B - 1), ("count", 0), ("place", 0), ("proj", B - 1), ("note", 0)]
    ending.sort(key=lambda u: -1 if u[0] in ("av", "o", "oT") else
                stages.index(u) if u in stages else len(stages) + (u[0] != "disp" or u[1] != 0))
    plan += [("flush",)] + ending
    return plan


SLOTTED = ("rank", "xT", "q", "k", "v", "tail", "head", "oT", "yT", "proj", "zT", "logit", "count")


def build_program(nc, x, gamma, beta, w, b_score, wqT, wkT, wvT, wpT, wg, w1, b1, w2, b2,
                  rope_cos, rope_sin, count, token_no, out):
    plan = build_plan()
    unit_of = {}
    for u in plan:
        if u[0] in SLOTTED:
            unit_of[u] = len(unit_of)
    nonlinear_of = {}
    for u in plan:
        if u[0] in ("tail", "head"):
            nonlinear_of[u] = len(nonlinear_of)

    ctx = ExitStack()
    with ctx:
        def sb(name, shape, dt=F32):
            return ctx.enter_context(nc.sbuf_tensor(name, shape, dt))

        def dram(name, shape, dt=F32):
            return nc.dram_tensor(name, shape, dt, kind="Internal").ap()

        def sem(name):
            return ctx.enter_context(nc.semaphore(name))

        sorted_d = dram("sorted_d", [B * N, 2 * D])
        parts_d = dram("parts_d", [B, 2, 6 * C, KEEP], BF16)
        disp_d = dram("disp_d", [TILES * P, ROW])
        acc_d = dram("acc_d", [ROWS + P, D])

        arena = sb("arena", [P, 21504])
        g_area = sb("g_area", [P, 8 * RUN])
        hres = sb("hres", [TOK, NTA, D])
        z = sb("z", [TOK, NTA, ROW])
        sq = sb("sq", [P, 2, RUN])
        quad = sb("quad", [P, RUN])
        cub = sb("cub", [P, 2, RUN])
        v_mix = sb("v_mix", [P, 2, NT, HEADS * (HD + 1)])
        v_mix5 = v_mix[:, :, :, :].rearrange("p m t (h d) -> p m t h d", h=HEADS)
        o_sb = sb("o_sb", [P, 2, KEEP])
        y_sb = sb("y_sb", [TOK, NT, D])
        yT = sb("yT", [C, 2, KEEP])
        wp_sb = sb("wp_sb", [C, 2, D])
        wg_sb = sb("wg_sb", [C, 2, E])
        ident = sb("ident", [P, P])
        before = sb("before", [TOK, TOK])
        ones = sb("ones", [P, P])
        count_sb = sb("count_sb", [P, TILES])
        small = sb("small", [P, SMALL])

        stack_w = HEADS * KEEP // 2
        def stack(par, qk):
            at = par * 12288 + qk * stack_w
            return arena[:, at:at + stack_w].bitcast(BF16)
        rot_c = arena[0:C, 6300:7350].rearrange("p (a s) -> p a s", a=2)
        rot_s = arena[0:C, 7350:8400].rearrange("p (a s) -> p a s", a=2)
        rot = arena[0:C, 8400:9450].rearrange("p (a s) -> p a s", a=2)
        parts = arena[0:C, 9450:11025].bitcast(BF16).rearrange("p (a b s) -> p a b s", a=3, b=2)
        xT = arena[0:C, 11025:12075].rearrange("p (c s) -> p c s", c=2)
        tri = arena[:, 12075:12139].bitcast(BF16)
        ident_b = arena[:, 12139:12203].bitcast(BF16)
        w1_sb = arena[:, 0:12288]
        cos_sb = arena[0:C, 18588:19113]
        sin_sb = arena[0:C, 19113:19638]
        wqk_sb = arena[0:C, 19638:20406].rearrange("p (q c t m) -> p q c t m", q=2, c=2, t=2)
        wv_sb = arena[0:C, 20406:20790].rearrange("p (c o) -> p c o", c=2)
        hs = HEADS * TAIL
        g_tail = arena[0:TAIL, 20790:20790 + 2 * hs].rearrange("p (m h s) -> p m h s", m=2, h=HEADS)
        sq_tail, cub_tail = arena[0:TAIL, 21102:21102 + hs], arena[0:TAIL, 21258:21258 + hs]
        idx = arena[:, 21414:21414 + B * NIN].bitcast(U32)
        w2_sb = arena[:, 12288:21504]

        xn = g_area[0:TIN, 0:24 * 384].rearrange("p (t d) -> p t d", t=B * NIN)
        pad_row = g_area[:, 9216:9216 + ROW]
        sig = g_area[:, :].rearrange("p (h m s) -> p h m s", h=4, m=2)
        b2_bc = g_area[:, 0:1536]
        b2_row = g_area[:, 1536:1536 + D]
        meta = g_area[:, 1728:1728 + 4 * TILES].rearrange("p (t w) -> p t w", t=TILES)
        weight, weight2 = g_area[:, 1888:1888 + TILES], g_area[:, 1928:1928 + TILES]
        dest = g_area[:, 1968:1968 + TILES].bitcast(U32)
        dest_now = g_area[:, 2008:2010].bitcast(U32)
        eid = g_area[:, 2040:2040 + TILES].bitcast(I32)
        x_tT = g_area[0:C + 1, 2112:2624].rearrange("p (r c t) -> p r c t", r=2, c=2)
        hidT = g_area[:, 2624:4160].rearrange("p (r k t) -> p r k t", r=2, k=6)
        w1_now = g_area[0:C + 1, 4160:4160 + 4 * F].rearrange("p (r c f) -> p r c f", r=2, c=2)
        y_tile = g_area[:, 7232:7232 + 2 * D].rearrange("p (r d) -> p r d", r=2)
        x_tile = g_area[:, 7616:7616 + 2 * D].rearrange("p (r d) -> p r d", r=2)

        used = {"front": 0, "small": 0, "qk": 0}

        def tiny(where, parts_, *dims, dt=F32):
            area, size = {"front": (o_front, 2 * KEEP), "small": (small, SMALL), "qk": (arena[:, 6300:], 1380)}[where]
            n, at = int(np.prod(dims)), used[where]
            used[where] += n
            assert used[where] <= size
            v = area[0:parts_, at:at + n]
            if dt is not F32:
                v = v.bitcast(dt)
            if len(dims) == 2:
                v = v.rearrange("p (a b) -> p a b", a=dims[0])
            if len(dims) == 3:
                v = v.rearrange("p (a b c) -> p a b c", a=dims[0], b=dims[1])
            return v

        o_front = o_sb[:, :, :].rearrange("p a s -> p (a s)")
        later = tiny("front", TIN, TIN)
        stats = tiny("front", P, NIN, 6)
        mv = tiny("front", P, B * NIN, 2)
        var_e, rs, rs_t, shift, score = (tiny("front", P, B * NIN) for _ in range(5))
        cnt = tiny("front", P, B * NIN, 4)
        konst = tiny("front", P, 2)
        shift2 = tiny("small", P, NTA)
        token_sb = tiny("front", P, NTA + 1)
        half_quad = tiny("small", P, 1)
        den = tiny("small", P, NT, 4)
        mv2 = tiny("small", P, NTA, 2)
        rs2 = tiny("small", P, NTA)
        var2, rs2_t = tiny("small", P, NT), tiny("small", P, NT)
        front = cub[0:TIN, 0, :]
        gw = front[:, 0:D]
        gam_bc = front[:, D:2 * D]
        bet_bc = front[:, 2 * D:3 * D]
        w_bc = front[:, 3 * D:4 * D]
        junk = quad[0:TIN, 0:NIN * D].rearrange("p (t d) -> p t d", t=NIN)
        sdiag = cub[0:TIN, 1, 0:NIN * TIN].rearrange("p (t j) -> p t j", t=NIN)
        cmp_junk = sq[0:TIN, :, :].rearrange("p a s -> p (a s)")[:, 0:NIN * (N + TIN + 1) // 2].bitcast(BF16).rearrange(
            "p (t j) -> p t j", t=NIN)

        pos1, pos2 = tiny("small", TOK, NTA, dt=U32), tiny("small", TOK, NTA, dt=U32)
        rows_e, chunks_e, last_tile, ends, base, n_new, c_new, tmp_e, old_e = (tiny("small", P, E) for _ in range(9))
        c_int = tiny("small", P, E, dt=I32)
        used_tiles = tiny("small", P, 1)
        eid_f = tiny("small", P, TILES)

        class Router:

            def __init__(self, n):
                self.n = n
                self.cand = tiny("small", TOK, n, E)
                self.prob, self.cand2, self.hot1, self.hot2, self.both = (tiny("qk", TOK, n, E) for _ in range(5))
                self.top1, self.top2, self.ind, self.sums = (tiny("qk", TOK, n) for _ in range(4))
                self.totals, self.run_tot, self.carry = (tiny("qk", P, E, n) for _ in range(3))
                self.eid_add = self.totals.rearrange("p e t -> p (e t)")[:, 0:TILES]

        routers = [Router(NT * (end - start)) for start, end in GROUPS]
        assert TILES <= E * NT
        assert W1_LATE[0] * 2 * F <= 6300 and 6300 + used["qk"] <= (W1_LATE[-1] + 1) * 2 * F
        logit_max = tiny("small", TOK, NT)
        stats2 = tiny("small", TOK, NT, 6)

        slots = [ctx.enter_context(nc.psum_tensor(f"slot{i}", [P, 1536], F32)) for i in range(2)]
        o_ps = ctx.enter_context(nc.psum_tensor("o_ps", [P, 1024], F32))

        def slot(u):
            return slots[unit_of[u] % 2]

        x_in = [sem(f"x_in{b}") for b in range(B)]
        row_in, w_in, token_in, pad_set, pad_out = sem("row_in"), sem("w_in"), sem("token_in"), sem("pad_set"), sem("pad_out")
        const_set, vec_step = sem("const_set"), sem("vec_step")
        diag_ready, idx_ready = sem("diag_ready"), sem("idx_ready")
        scattered = [sem(f"scattered{b}") for b in range(B)]
        x_loaded, h_loaded = ([sem(f"{n}{b}") for b in range(B)] for n in ("x_loaded", "h_loaded"))
        rs_ready, xn_ready = sem("rs_ready"), sem("xn_ready")
        psum_full, slot_free = sem("psum_full"), [sem("slot_free0"), sem("slot_free1")]
        xT_ready, rope_mul, rotated, hi_ready, rest_ready, mid_ready, parts_ready = (
            sem("xT_ready"), sem("rope_mul"), sem("rotated"), sem("hi_ready"), sem("rest_ready"),
            sem("mid_ready"), sem("parts_ready"))
        parts_out, stack_in = sem("parts_out"), [sem("stack_in0"), sem("stack_in1")]
        v_ready, sq_ready, cub_ready, sig_ready = (
            sem("v_ready"), sem("sq_ready"), sem("cub_ready"), sem("sig_ready"))
        lin_ready, quad_ready, quad_v, norm_ready = sem("lin_ready"), sem("quad_ready"), sem("quad_v"), sem("norm_ready")
        pool_step = sem("pool_step")
        av_done, o_ready, y_ready, yT_ready, z_ready, zT_ready = (
            sem("av_done"), sem("o_ready"), sem("y_ready"), sem("yT_ready"), sem("z_ready"), sem("zT_ready"))
        w1_in, w2_in, b2_in = sem("w1_in"), sem("w2_in"), sem("b2_in")
        shifted, prob_ready, hot_ready, pos_ready, eid_ready, dispatched, h_added, acc_in = (
            sem("shifted"), sem("prob_ready"), sem("hot_ready"), sem("pos_ready"), sem("eid_ready"),
            sem("dispatched"), sem("h_added"), sem("acc_in"))
        noted = sem("noted")
        ones_row = sem("ones_row")
        tile_in = [sem(f"tile_in{i}") for i in range(2)]
        tT_full, tT_ready, w1_copied, hid_full, hid_copied, y_full, y_copied, y_out_ready = (
            sem("tT_full"), sem("tT_ready"), [sem("w1_copied0"), sem("w1_copied1")], sem("hid_full"),
            [sem("hid_copied0"), sem("hid_copied1")], sem("y_full"), sem("y_copied"), sem("y_out_ready"))
        meta_in = [sem(f"meta_in{i}") for i in range(2)]
        added = [sem(f"added{i}") for i in range(2)]
        dest_ready, dest_set, add_begun, out_done = sem("dest_ready"), sem("dest_set"), sem("add_begun"), sem("out_done")

        def wait_from_1(eng, semaphore, n):
            if not isinstance(n, int) or n > 0:
                eng.wait_ge(semaphore, n)

        def on_scalar(u):
            return u[0] == "head" and u[2] % 2 == 1

        def buffers(u):
            if u[0] == "tail":
                return sq_tail, cub_tail, slot(u)[0:TAIL, 0:HEADS * TAIL]
            return sq[:, u[2] % 2, :], cub[:, u[2] % 2, :], slot(u)[:, RUN0:RUN0 + RUN]

        def two_before(u):
            _, b, *h = u
            former = ("tail", b - 1) if not h else ("head", b, h[0] - 2) if h[0] >= 2 else ("head", b - 1, HEADS + h[0] - 2)
            return nonlinear_of.get(former, -1) + 1

        def free_before(u):
            n = unit_of[u]
            return n % 2, n // 2

        def take_slot(eng, u):
            s, k = free_before(u)
            if k:
                eng.wait_ge(slot_free[s], k)

        def full(eng, u):
            eng.wait_ge(psum_full, unit_of[u] + 1)

        block = ctx.enter_context(nc.Block())

        @block.sync
        def _(sp):
            sp.dma_start(token_sb, token_no).then_inc(token_in, 16)
            for b in range(B):
                sp.dma_start(xn[:, NIN * b:NIN * (b + 1), 0:D],
                             x[b].rearrange("(t p) d -> p t d", p=TIN)).then_inc(x_in[b], 16)
                if b == 0:
                    for dst, src in ((gam_bc, gamma), (bet_bc, beta), (w_bc, w)):
                        sp.dma_start(dst, src.rearrange("(a d) -> a d", a=1).broadcast_to([TIN, D])).then_inc(row_in, 16)
                    sp.dma_start(konst[0:TIN, 1:2], b_score.rearrange("(a d) -> a d", a=1).broadcast_to([TIN, 1])).then_inc(row_in, 16)
            for dst, src in ((wqk_sb[:, 0], wqT), (wqk_sb[:, 1], wkT), (wv_sb, wvT), (wp_sb[:, :, :], wpT),
                             (wg_sb[:, :, :], wg.rearrange("(c p) e -> p c e", c=2)), (cos_sb, rope_cos),
                             (sin_sb, rope_sin), (count_sb[:, :], count.rearrange("(a d) -> a d", a=1).broadcast_to([P, TILES]))):
                sp.dma_start(dst, src).then_inc(w_in, 16)
            sp.wait_ge(pad_set, 1)
            sp.dma_start(disp_d.rearrange("(t p) d -> p t d", p=P),
                         pad_row.unsqueeze(1).broadcast_to([P, TILES, ROW])).then_inc(pad_out, 16)
            sp.dma_start(acc_d[ROWS:ROWS + P, :], pad_row[:, 0:D]).then_inc(pad_out, 16)

            def load_sorted(b):
                sp.wait_ge(scattered[b], 16 * NIN)
                rows = sorted_d[N * b:N * b + KEEP, :].rearrange("(t p) d -> p t d", p=TOK)
                sp.dma_start(z[:, NT * b:NT * (b + 1), 0:D], rows[:, :, D:2 * D]).then_inc(x_loaded[b], 16)
                sp.dma_start(hres[:, NT * b:NT * (b + 1), :], rows[:, :, 0:D]).then_inc(h_loaded[b], 16)

            def stack_parts(m):
                b, qk = m // 2, m % 2
                sp.wait_ge(parts_ready, m + 1)
                sp.dma_start(parts_d[b, qk].rearrange("(a m) s -> m a s", a=6),
                             parts.rearrange("p a b s -> p (a b) s")).then_inc(parts_out, 16)
                sp.wait_ge(parts_out, 16 * (m + 1))
                if b >= 2 and qk == 0:
                    sp.wait_ge(psum_full, unit_of[("head", b - 2, HEADS - 1)] + 1)
                rows = parts_d[b, qk].rearrange("m s -> (m s)").rearrange("(r x) -> r x", r=3 * HD)
                st = stack(b % 2, qk)
                for i, part in enumerate((Q_BLOCKS, K_BLOCKS)[qk]):
                    sp.dma_start(st[HD * i:HD * (i + 1), :], rows[HD * part:HD * (part + 1), :]).then_inc(stack_in[b % 2], 16)

            load_sorted(0)
            stack_parts(0)
            stack_parts(1)
            def store_h(b):
                sp.wait_ge(h_added, b + 1)
                sp.dma_start(acc_d[KEEP * b:KEEP * (b + 1), :].rearrange("(t p) d -> p t d", p=TOK),
                             hres[:, NT * b:NT * (b + 1), :]).then_inc(acc_in, 16)

            for b in range(1, B):
                load_sorted(b)
                stack_parts(2 * b)
                stack_parts(2 * b + 1)
            for b in range(B - 2):
                store_h(b)
            w1_e = w1_sb.rearrange("p (e c f) -> p e c f", e=E, c=2)

            def load_w1(e):
                sp.dma_start(w1_e[0:C, e], w1[e].rearrange("(c p) f -> p c f", c=2)).then_inc(w1_in, 16)
                sp.dma_start(w1_e[C:C + 1, e, 1], b1[e:e + 1, :]).then_inc(w1_in, 16)

            sp.wait_ge(psum_full, unit_of[("v", B - 1)] + 1)
            for e in range(E - 1):
                if e not in W1_LATE:
                    load_w1(e)
            sp.wait_ge(psum_full, unit_of[("head", B - 1, HEADS - 1)] + 1)
            load_w1(E - 1)
            for e in range(E):
                if e == E - 1:
                    sp.wait_ge(av_done, PAIRS * B)
                sp.dma_start(w2_sb.rearrange("p (e k d) -> p e k d", e=E, k=6)[:, e],
                             w2[e].rearrange("(k p) d -> p k d", k=6)).then_inc(w2_in, 16)
            sp.dma_start(b2_bc, b2.rearrange("(a e) d -> a (e d)", a=1).broadcast_to([P, E * D])).then_inc(b2_in, 16)
            store_h(B - 2)
            store_h(B - 1)
            sp.wait_ge(noted, len(GROUPS))
            for e in W1_LATE:
                load_w1(e)
            sp.wait_ge(dispatched, 16 * 2 * NTA)

            def load_tile(par, row):
                sp.dma_start(x_tile[:, par, :], disp_d[bass.ds(row, P), 0:D]).then_inc(tile_in[par], 16)

            load_tile(0, 0)
            load_tile(1, P)
            rows = disp_d.rearrange("(t p) d -> p t d", p=P)
            for group, tiles in enumerate(META_GROUPS):
                sp.dma_start(meta[:, tiles], rows[:, tiles, D:ROW]).then_inc(meta_in[group], 16)
            with sp.Fori(0, TILES // 2 - 1) as j:
                for par in range(2):
                    sp.wait_ge(tT_full, 2 * j + par + 1)
                    load_tile(par, (2 * j + par + 2) * P)
            for par in range(2):
                sp.wait_ge(added[par], 16 * (TILES // 2))
            sp.dma_start(out.rearrange("b s d -> (b s d)").rearrange("(p n) -> p n", p=P),
                         acc_d[0:ROWS, :].rearrange("r d -> (r d)").rearrange("(p n) -> p n", p=P)).then_inc(out_done, 16)
            sp.wait_ge(out_done, 16)

        @block.gpsimd
        def _(g):
            step = [0]

            def link(ins):
                ins.then_inc(pool_step, 1)
                step[0] += 1
                g.wait_ge(pool_step, step[0])

            link(g.memset(pad_row, 0.0))
            g.wait_ge(token_in, 16)
            g.tensor_copy(pad_row[:, D:D + 1], token_sb[:, NTA:NTA + 1]).then_inc(pad_set, 1)
            g.tensor_copy(z[:, :, D:D + 1], token_sb[0:TOK, 0:NTA].unsqueeze(2))
            g.memset(ones[:, :], 1.0)
            g.memset(ident[:, :], 0.0)
            g.memset(later, 1.0)
            g.memset(tri, 0.0)
            link(g.memset(before[:, :], 1.0))
            g.affine_select(out=ident[:, :], in_=ident[:, :], compare_op=ALU.not_equal, fill=1.0, base=0,
                            pattern=[[-1, P]], channel_multiplier=1)
            g.affine_select(out=tri, in_=tri, compare_op=ALU.is_ge, fill=MASKED, base=0,
                            pattern=[[1, P]], channel_multiplier=-1)
            g.affine_select(out=later, in_=later, compare_op=ALU.is_gt, fill=0.0, base=0,
                            pattern=[[-1, TIN]], channel_multiplier=1)
            link(g.affine_select(out=before[:, :], in_=before[:, :], compare_op=ALU.is_gt, fill=0.0, base=0,
                                 pattern=[[1, TOK]], channel_multiplier=-1))
            g.tensor_copy(ident_b, ident[:, :]).then_inc(const_set, 1)

            def scatter(b):
                g.wait_ge(idx_ready, b + 1)
                g.wait_ge(xn_ready, b + 1)
                for t in range(NIN * b, NIN * (b + 1)):
                    g.indirect_dma_start(sorted_d, bass.IndirectOffsetOnAxis(idx[0:TIN, t:t + 1], 0),
                                         xn[:, t, :], None).then_inc(scattered[b], 16)

            def rotate(m):
                g.wait_ge(rope_mul, m + 1)
                g.tensor_tensor(rot[:, 0, :], rot_c[:, 0, :], rot_s[:, 1, :], ALU.subtract)
                g.tensor_tensor(rot[:, 1, :], rot_s[:, 0, :], rot_c[:, 1, :], ALU.add).then_inc(rotated, 1)

            def less_high(m):
                g.wait_ge(hi_ready, m + 1)
                g.tensor_tensor(rot, rot, parts[:, 0], ALU.subtract).then_inc(rest_ready, 1)

            def low_part(m):
                g.wait_ge(mid_ready, m + 1)
                g.wait_ge(rest_ready, m + 1)
                g.tensor_tensor(parts[:, 2], rot, parts[:, 1], ALU.subtract).then_inc(parts_ready, 1)
                g.wait_ge(parts_ready, m + 1)

            for u in plan:
                if u[0] == "scatter":
                    scatter(u[1])
                elif u[0] in ("q", "k"):
                    rotate(2 * u[1] + (u[0] == "k"))
                elif u[0] == "hi":
                    less_high(u[1])
                elif u[0] == "mid":
                    low_part(u[1])
                elif u[0] == "disp":
                    _, group, t = u
                    if t == 0:
                        g.wait_ge(pad_out, 32)
                    g.wait_ge(pos_ready, group + 1)
                    g.wait_ge(z_ready, GROUPS[group][1])
                    for pos in (pos1, pos2):
                        g.indirect_dma_start(disp_d, bass.IndirectOffsetOnAxis(pos[:, t:t + 1], 0),
                                             z[:, t, :], None).then_inc(dispatched, 16)
            g.wait_ge(acc_in, 16 * B)

            for group in range(2):
                g.wait_ge(dest_ready, group + 1)

            def add_tile(par, i, former):
                g.tensor_copy(dest_now[:, par:par + 1], dest[:, bass.ds(i, 1)]).then_inc(dest_set, 1)
                g.wait_ge(dest_set, i + 1)
                g.wait_ge(y_out_ready, i + 1)
                if former is not None:
                    g.wait_ge(added[1 - par], former)
                g.sem_inc(add_begun, 1)
                g.indirect_dma_start(acc_d, bass.IndirectOffsetOnAxis(dest_now[:, par:par + 1], 0),
                                     y_tile[:, par, :], None, compute_op=ALU.add).then_inc(added[par], 16)

            add_tile(0, 0, None)
            add_tile(1, 1, 16)
            with g.Fori(1, TILES // 2) as j:
                add_tile(0, 2 * j, 16 * j)
                add_tile(1, 2 * j + 1, 16 * (j + 1))

        @block.scalar
        def _(act):
            def evacuate_T(u, dst, ready):
                full(act, u)
                s = slot(u)
                act.activation(dst[:, 0, 0:4 * TOK], s[0:C, 0:4 * TOK], ACT.Copy)
                act.activation(dst[:, 1, 0:4 * TOK], s[0:C, 512:512 + 4 * TOK], ACT.Copy)
                act.activation(dst[:, :, 4 * TOK:KEEP], s[0:C, 1024:1024 + 2 * TOK].rearrange("p (c s) -> p c s", c=2),
                               ACT.Copy).then_inc(ready, 1)
                act.wait_ge(ready, count_of[u[0]])
                act.sem_inc(slot_free[free_before(u)[0]], 1)

            count_of = {}
            pending = []

            def sigmoids():
                if not pending:
                    return
                u = pending.pop(0)
                n = nonlinear_of[u]
                if n == 0:
                    act.wait_ge(pad_out, 32)
                    for b in range(B):
                        act.wait_ge(scattered[b], 16 * NIN)
                act.wait_ge(cub_ready, n + 1)
                b = u[1]
                if u[0] == "tail":
                    if b:
                        act.wait_ge(av_done, PAIRS * b)
                    dst = [g_tail[:, i].rearrange("p h s -> p (h s)") for i in range(2)]
                else:
                    pair = PAIRS * b + u[2] // 2
                    if pair >= 2:
                        act.wait_ge(av_done, pair - 1)
                    dst = [sig[:, u[2] % 4, i, :] for i in range(2)]
                src = buffers(u)[1]
                act.activation(dst[0], src, ACT.Sigmoid, scale=2 * K0 * D3 * SCORE_SCALE)
                act.activation(dst[1], src, ACT.Sigmoid, scale=2 * K1 * D3 * SCORE_SCALE).then_inc(sig_ready, 1)

            for u in plan:
                kind = u[0]
                count_of[kind] = count_of.get(kind, 0) + 1
                if kind == "score":
                    act.wait_ge(rs_ready, u[1] + 1)
                    for t in range(NIN * u[1], NIN * (u[1] + 1)):
                        last = act.activation(xn[:, t, D:2 * D], xn[:, t, 0:D], ACT.Identity, bias=shift[0:TIN, t:t + 1],
                                              scale=rs[0:TIN, t:t + 1])
                    last.then_inc(xn_ready, 1)
                elif kind == "xT":
                    if u[1]:
                        full(act, ("v", u[1] - 1))
                    evacuate_T(u, xT, xT_ready)
                elif kind == "zT":
                    evacuate_T(u, yT, zT_ready)
                elif kind == "yT":
                    if u[1]:
                        full(act, ("logit", u[1] - 1))
                    evacuate_T(u, yT, yT_ready)
                elif kind == "hi":
                    m = u[1]
                    act.wait_ge(rotated, m + 1)
                    if m:
                        act.wait_ge(parts_out, 16 * m)
                    act.activation(parts[:, 0], rot, ACT.Copy).then_inc(hi_ready, 1)
                elif kind == "mid":
                    act.wait_ge(rest_ready, u[1] + 1)
                    act.activation(parts[:, 1], rot, ACT.Copy).then_inc(mid_ready, 1)
                elif kind == "v":
                    full(act, u)
                    s = slot(u)
                    if u[1]:
                        act.wait_ge(av_done, PAIRS * u[1])
                    for i, mix in enumerate((2 * MIX0, 2 * MIX1)):
                        for bank in range(2):
                            act.activation(v_mix5[:, i, 2 * bank:2 * bank + 2, :, 0:HD],
                                           s[:, 512 * bank:512 * bank + 2 * D].rearrange("p (t h d) -> p t h d", t=2, h=HEADS),
                                           ACT.Copy, scale=mix)
                        last = act.activation(v_mix5[0:TAIL, i, 4, :, 0:HD],
                                              s[0:TAIL, 1024:1024 + D].rearrange("p (h d) -> p h d", h=HEADS),
                                              ACT.Copy, scale=mix)
                    last.then_inc(v_ready, 1)
                    act.wait_ge(v_ready, u[1] + 1)
                    act.sem_inc(slot_free[free_before(u)[0]], 1)
                elif kind in ("tail", "head"):
                    n = nonlinear_of[u]
                    if n == 0:
                        act.wait_ge(idx_ready, B)
                    full(act, u)
                    before_last = two_before(u)
                    if before_last:
                        act.wait_ge(cub_ready, before_last)
                    s = slot(u)
                    a, _, run = buffers(u)
                    act.activation(a, run, ACT.Square, scale=SCORE_SCALE).then_inc(sq_ready, 1)
                    if on_scalar(u):
                        act.wait_ge(sq_ready, n + 1)
                        act.activation(quad[:, :], a, ACT.Square, bias=half_quad[:, 0:1]).then_inc(quad_ready, 1)
                    sigmoids()
                    pending.append(u)
                elif kind == "flush":
                    sigmoids()
                elif kind == "z":
                    act.wait_ge(norm_ready, u[1] + 1)
                    for t in range(NT * u[1], NT * (u[1] + 1)):
                        last = act.activation(z[:, t, 0:D], hres[:, t, :], ACT.Identity, bias=shift2[0:TOK, t:t + 1],
                                              scale=rs2[0:TOK, t:t + 1])
                    last.then_inc(z_ready, 1)
                elif kind == "pick":
                    ro = routers[u[1]]
                    act.wait_ge(shifted, GROUPS[u[1]][1])
                    act.wait_ge(parts_ready, 2 * B)
                    act.activation(ro.prob, ro.cand, ACT.Sigmoid)
                    act.activation(ro.cand2, ro.cand, ACT.Sigmoid, scale=-1.0).then_inc(prob_ready, 1)
                elif kind == "o":
                    q = u[1]
                    act.wait_ge(av_done, 2 * (q + 1))
                    if q >= 2:
                        full(act, ("oT", q - 2))
                    act.activation(o_sb[:, q % 2, 0:S0], o_ps[:, 0:S0], ACT.Copy)
                    act.activation(o_sb[:, q % 2, S0:KEEP], o_ps[:, 512:512 + KEEP - S0], ACT.Copy).then_inc(o_ready, 1)

            act.wait_ge(eid_ready, 1)
            act.wait_ge(w1_in, 16 * 2 * E)

            def copy_w1(par, i):
                e = act.value_load(eid[0:1, bass.ds(i, 1)], min_val=0, max_val=E - 1)
                wait_from_1(act, hid_full, i - 1)
                act.activation(w1_now[0:C, par, 0, :], w1_sb[0:C, bass.ds(e * (2 * F), F)], ACT.Copy).then_inc(w1_copied[0], 1)

            def copy_tT(par, i):
                act.wait_ge(tT_full, i + 1)
                wait_from_1(act, hid_full, i - 1)
                act.activation(x_tT[0:C, par], slots[par][0:C, 0:2 * P].rearrange("p (c t) -> p c t", c=2),
                               ACT.Copy).then_inc(tT_ready, 1)

            def relu_a(par, i):
                act.wait_ge(hid_full, i + 1)
                wait_from_1(act, y_full, i - 1)
                act.activation(hidT[:, par, 0:3], slots[par][:, 512:512 + 3 * P].rearrange("p (k t) -> p k t", k=3),
                               ACT.Relu).then_inc(hid_copied[0], 1)

            def tile_round(par, i):
                copy_tT(par, i + 2)
                relu_a(1 - par, i + 1)
                copy_w1(par, i + 2)

            for par in range(2):
                copy_w1(par, par)
                copy_tT(par, par)
            relu_a(0, 0)
            tile_round(0, 0)
            tile_round(1, 1)
            with act.Fori(1, TILES // 2 - 1) as j:
                for par in range(2):
                    tile_round(par, 2 * j + par)
            relu_a(1, TILES - 1)

        @block.vector
        def _(dve):
            v = nc.vector
            step = [0]

            def link(ins):
                ins.then_inc(vec_step, 1)
                step[0] += 1
                dve.wait_ge(vec_step, step[0])

            def rsqrt(y, t, a):
                link(v.tensor_scalar(y.bitcast(I32), a.bitcast(I32), -0.5, 1597463007.0, ALU.mult, ALU.add))
                for _ in range(3):
                    link(v.tensor_tensor(t, y, y, ALU.mult))
                    link(v.scalar_tensor_tensor(out=t, in0=t, scalar=-0.5, in1=a, op0=ALU.mult, op1=ALU.mult))
                    link(v.scalar_tensor_tensor(out=y, in0=t, scalar=1.5, in1=y, op0=ALU.add, op1=ALU.mult))

            v.memset(cnt[0:TIN], 0.0)
            v.memset(half_quad, QUAD1 / 2)
            v.memset(o_ps[:, :], 0.0)
            v.memset(v_mix5[:, 0, :, :, HD:HD + 1], 2 * MIX0)
            link(v.memset(v_mix5[:, 1, :, :, HD:HD + 1], 2 * MIX1))
            dve.wait_ge(row_in, 64)
            v.tensor_tensor(gw, gam_bc, w_bc, ALU.mult)
            link(v.scalar_tensor_tensor(out=junk[:, 0], in0=bet_bc, scalar=1.0, in1=w_bc, op0=ALU.mult, op1=ALU.mult,
                                        accum_out=konst[0:TIN, 0:1]))
            link(v.tensor_tensor(konst[0:TIN, 0:1], konst[0:TIN, 0:1], konst[0:TIN, 1:2], ALU.add))

            def score_batch(b):
                dve.wait_ge(x_in[b], 16)
                tiles = range(NIN * b, NIN * (b + 1))
                for t in tiles:
                    last = v.bn_stats(stats[0:TIN, t % NIN, :], xn[:, t, 0:D])
                link(last)
                for t in tiles:
                    last = v.bn_aggr(mv[0:TIN, t, :], stats[0:TIN, t % NIN, :])
                link(last)
                s = slice(NIN * b, NIN * (b + 1))
                link(v.tensor_scalar(var_e[0:TIN, s], mv[0:TIN, s, 1], LN_EPS, None, ALU.add))
                rsqrt(rs[0:TIN, s], rs_t[0:TIN, s], var_e[0:TIN, s])
                link(v.scalar_tensor_tensor(out=shift[0:TIN, s], in0=mv[0:TIN, s, 0], scalar=-1.0, in1=rs[0:TIN, s],
                                            op0=ALU.mult, op1=ALU.mult))
                dve.sem_inc(rs_ready, 1)
                for t in tiles:
                    last = v.scalar_tensor_tensor(out=junk[:, t % NIN], in0=xn[:, t, 0:D], scalar=mv[0:TIN, t, 0:1], in1=gw,
                                                  op0=ALU.subtract, op1=ALU.mult, accum_out=score[0:TIN, t:t + 1])
                link(last)
                link(v.tensor_tensor(score[0:TIN, s], score[0:TIN, s], rs[0:TIN, s], ALU.mult))
                link(v.tensor_scalar(score[0:TIN, s], score[0:TIN, s], konst[0:TIN, 0:1], None, ALU.add))
                if b == 0:
                    dve.wait_ge(const_set, 1)
                else:
                    full(dve, ("rank", b - 1))
                v.tensor_tensor(sdiag, ident[0:TIN, 0:TIN].unsqueeze(1).broadcast_to([TIN, NIN, TIN]),
                                score[0:TIN, s].unsqueeze(2).broadcast_to([TIN, NIN, TIN]), ALU.mult).then_inc(diag_ready, 1)

            def rank_batch(b):
                u = ("rank", b)
                full(dve, u)
                ps = slot(u)
                for t in range(NIN):
                    tt = NIN * b + t
                    s = score[0:TIN, tt:tt + 1]
                    c0, c1 = TIN * t, TIN * (t + 1)
                    out = cmp_junk[:, t]
                    if t:
                        v.tensor_scalar(out[:, 0:c0], ps[0:TIN, 0:c0], s, None, ALU.is_ge, ALU.add, accum_out=cnt[0:TIN, tt, 0:1])
                    if t < NIN - 1:
                        v.tensor_scalar(out[:, c1:N], ps[0:TIN, c1:N], s, None, ALU.is_gt, ALU.add, accum_out=cnt[0:TIN, tt, 1:2])
                    v.tensor_scalar(out[:, c0:c1], ps[0:TIN, c0:c1], s, None, ALU.is_gt, ALU.add, accum_out=cnt[0:TIN, tt, 2:3])
                    last = v.scalar_tensor_tensor(out=out[:, N:N + TIN], in0=ps[0:TIN, c0:c1], scalar=s, in1=later,
                                                  op0=ALU.is_equal, op1=ALU.mult, accum_out=cnt[0:TIN, tt, 3:4])
                link(last)
                dve.sem_inc(slot_free[free_before(u)[0]], 1)
                s = slice(NIN * b, NIN * (b + 1))
                link(v.tensor_reduce(rs_t[0:TIN, s], cnt[0:TIN, s, :], AX.X, ALU.add))
                v.tensor_scalar(idx[0:TIN, s], rs_t[0:TIN, s], float(N * b), None, ALU.add).then_inc(idx_ready, 1)

            def wide8(a):
                return a.unsqueeze(2).broadcast_to([TOK, a.shape[1], E])

            def numbers(ro):
                return count_sb[0:TOK, 0:E].unsqueeze(1).broadcast_to([TOK, ro.n, E])

            def tiles_of(g):
                return slice(NT * GROUPS[g][0], NT * GROUPS[g][1])

            def pick(ro, top, hot):
                link(v.tensor_reduce(top, ro.prob, AX.X, ALU.max))
                link(v.tensor_tensor(ro.cand, ro.prob, wide8(top), ALU.is_equal))
                link(v.scalar_tensor_tensor(out=ro.cand, in0=ro.cand, scalar=-float(E), in1=numbers(ro), op0=ALU.mult, op1=ALU.add))
                link(v.tensor_reduce(ro.ind, ro.cand, AX.X, ALU.min))
                link(v.tensor_scalar(ro.ind, ro.ind, float(E), None, ALU.add))
                link(v.tensor_tensor(hot, numbers(ro), wide8(ro.ind), ALU.is_equal))

            def choose_first(g):
                ro = routers[g]
                dve.wait_ge(prob_ready, g + 1)
                link(v.reciprocal(ro.cand2, ro.cand2))
                link(v.tensor_tensor(ro.prob, ro.prob, ro.cand2, ALU.mult))
                link(v.tensor_reduce(ro.sums, ro.prob, AX.X, ALU.add))
                link(v.reciprocal(ro.sums, ro.sums))
                link(v.tensor_tensor(ro.prob, ro.prob, wide8(ro.sums), ALU.mult))
                pick(ro, ro.top1, ro.hot1)
                v.tensor_copy(z[:, tiles_of(g), D + 1], ro.ind)

            def choose_second(g):
                ro = routers[g]
                tt = tiles_of(g)
                link(v.scalar_tensor_tensor(out=ro.prob, in0=ro.hot1, scalar=-2.0, in1=ro.prob, op0=ALU.mult, op1=ALU.add))
                pick(ro, ro.top2, ro.hot2)
                v.tensor_tensor(ro.both, ro.hot1, ro.hot2, ALU.add).then_inc(hot_ready, 1)
                link(v.tensor_tensor(ro.sums, ro.top1, ro.top2, ALU.add))
                link(v.reciprocal(ro.sums, ro.sums))
                v.tensor_tensor(z[:, tt, D + 2], ro.top1, ro.sums, ALU.mult)
                link(v.tensor_tensor(z[:, tt, D + 3], ro.top2, ro.sums, ALU.mult))

            def count_rows(u):
                ro = routers[u[1]]
                full(dve, u)
                ps = slot(u)
                link(v.memset(ro.carry, 1.0))
                link(v.memset(ro.carry[:, :, 0:1], 0.0))
                link(v.tensor_copy(ro.totals, ps[:, 512:512 + ro.n * E].rearrange("p (t e) -> p e t", e=E)))
                link(v.tensor_tensor_scan(ro.run_tot.rearrange("p e t -> p (e t)"), ro.carry.rearrange("p e t -> p (e t)"),
                                          ro.totals.rearrange("p e t -> p (e t)"), 0.0, ALU.mult, ALU.add))
                link(v.tensor_tensor(n_new, rows_e, ro.run_tot[:, :, ro.n - 1], ALU.add))
                link(v.tensor_scalar(c_int, n_new, float(P - 1), None, ALU.add))
                link(v.tensor_scalar(c_int, c_int, 7, None, ALU.arith_shift_right))
                link(v.tensor_copy(c_new, c_int))
                link(v.tensor_tensor(tmp_e, c_new, chunks_e, ALU.subtract))
                link(v.tensor_tensor_scan(ends, ones[:, 0:E], tmp_e, used_tiles, ALU.mult, ALU.add))
                link(v.tensor_tensor(base, ends, tmp_e, ALU.subtract))
                link(v.tensor_tensor(ro.run_tot, ro.run_tot, ro.totals, ALU.subtract))
                link(v.tensor_tensor(ro.run_tot, ro.run_tot, rows_e.unsqueeze(2).broadcast_to([P, E, ro.n]), ALU.add))
                link(v.tensor_tensor(ro.cand, ps[0:TOK, 0:ro.n * E].rearrange("p (t e) -> p t e", e=E),
                                     ro.run_tot[0:TOK].rearrange("p e t -> p t e"), ALU.add))
                dve.sem_inc(slot_free[free_before(u)[0]], 1)

            def per_e(ro, a):
                return a[0:TOK].unsqueeze(1).broadcast_to([TOK, ro.n, E])

            def place_rows(g):
                ro = routers[g]
                link(v.tensor_scalar(old_e, chunks_e, float(P), None, ALU.mult))
                link(v.tensor_tensor(ro.cand2, ro.cand, per_e(ro, old_e), ALU.is_lt))
                link(v.tensor_tensor(old_e, last_tile, base, ALU.subtract))
                link(v.tensor_scalar(old_e, old_e, 1.0, None, ALU.add))
                link(v.tensor_tensor(ro.cand2, ro.cand2, per_e(ro, old_e), ALU.mult))
                link(v.tensor_tensor(old_e, base, chunks_e, ALU.subtract))
                link(v.tensor_tensor(ro.cand2, ro.cand2, per_e(ro, old_e), ALU.add))
                link(v.scalar_tensor_tensor(out=ro.cand, in0=ro.cand2, scalar=float(P), in1=ro.cand, op0=ALU.mult, op1=ALU.add))
                tt = tiles_of(g)
                for hot, pos in ((ro.hot1, pos1), (ro.hot2, pos2)):
                    link(v.tensor_tensor(ro.cand2, ro.cand, hot, ALU.mult))
                    link(v.tensor_reduce(ro.ind, ro.cand2, AX.X, ALU.add))
                    link(v.tensor_copy(pos[:, tt], ro.ind))
                dve.sem_inc(pos_ready, 1)

            def note_tiles(g):
                ro = routers[g]
                link(v.tensor_scalar(tmp_e, tmp_e, 0.0, None, ALU.is_gt))
                link(v.tensor_tensor(old_e, ends, last_tile, ALU.subtract))
                link(v.scalar_tensor_tensor(out=old_e, in0=old_e, scalar=-1.0, in1=tmp_e, op0=ALU.add, op1=ALU.mult))
                v.tensor_tensor(last_tile, last_tile, old_e, ALU.add)
                v.tensor_copy(rows_e, n_new)
                v.tensor_copy(chunks_e, c_new)
                v.tensor_copy(used_tiles, ends[:, E - 1:E])
                link(v.tensor_scalar(ro.eid_add, count_sb[:, :], ends[:, 0:1], None, ALU.is_ge))
                for e in range(1, E):
                    link(v.scalar_tensor_tensor(out=ro.eid_add, in0=count_sb[:, :], scalar=ends[:, e:e + 1], in1=ro.eid_add,
                                                op0=ALU.is_ge, op1=ALU.add))
                link(v.scalar_tensor_tensor(out=ro.eid_add, in0=ro.eid_add, scalar=float(E), in1=ro.eid_add, op0=ALU.is_lt, op1=ALU.mult))
                link(v.tensor_tensor(eid_f, eid_f, ro.eid_add, ALU.add))
                dve.sem_inc(noted, 1)

            for a in (rows_e, chunks_e, last_tile, used_tiles, eid_f):
                v.memset(a, 0.0)

            quads = {True: 0, False: 0}

            for u in plan:
                kind = u[0]
                if kind == "score":
                    score_batch(u[1])
                elif kind == "rank":
                    rank_batch(u[1])
                elif kind in ("q", "k"):
                    dve.wait_ge(w_in, 16 * 8)
                    m = 2 * u[1] + (kind == "k")
                    full(dve, u)
                    s = slot(u)
                    if m:
                        dve.wait_ge(rotated, m)
                    wide = s[0:C, 0:1024].rearrange("p (a s) -> p a s", a=2)[:, :, 0:350]
                    rest_ = s[0:C, 1024:1374].rearrange("p (a s) -> p a s", a=2)
                    for table, dst in ((cos_sb, rot_c), (sin_sb, rot_s)):
                        v.tensor_tensor(dst[:, :, 0:350], wide, table[:, 0:350].unsqueeze(1).broadcast_to([C, 2, 350]), ALU.mult)
                        last = v.tensor_tensor(dst[:, :, 350:KEEP], rest_, table[:, 350:KEEP].unsqueeze(1).broadcast_to([C, 2, 175]), ALU.mult)
                    last.then_inc(rope_mul, 1)
                    dve.wait_ge(rope_mul, m + 1)
                    dve.sem_inc(slot_free[free_before(u)[0]], 1)
                elif kind in ("tail", "head"):
                    n = nonlinear_of[u]
                    a, c, run = buffers(u)
                    dve.wait_ge(sq_ready, n + 1)
                    before_last = two_before(u)
                    if before_last:
                        dve.wait_ge(sig_ready, before_last)
                    v.scalar_tensor_tensor(out=c, in0=a, scalar=ROOT, in1=run, op0=ALU.add, op1=ALU.mult).then_inc(lin_ready, 1)
                    if on_scalar(u):
                        factor, const, done = quad[:, :], QUAD0 - QUAD1 * QUAD1 / 4, quad_ready
                    else:
                        v.scalar_tensor_tensor(out=a, in0=a, scalar=QUAD1, in1=a, op0=ALU.add, op1=ALU.mult).then_inc(quad_v, 1)
                        factor, const, done = a, QUAD0, quad_v
                    dve.wait_ge(lin_ready, n + 1)
                    dve.sem_inc(slot_free[free_before(u)[0]], 1)
                    quads[on_scalar(u)] += 1
                    dve.wait_ge(done, quads[on_scalar(u)])
                    v.scalar_tensor_tensor(out=c, in0=factor, scalar=const, in1=c, op0=ALU.add, op1=ALU.mult).then_inc(cub_ready, 1)
                elif kind == "oT":
                    q = u[1]
                    full(dve, u)
                    if q % 3 == 0 and q:
                        full(dve, ("yT", q // 3 - 1))
                    o = slot(u)[0:TOK, 0:NT * P].rearrange("p (t h d) -> p t h d", t=NT, h=4)
                    link(v.tensor_scalar(den[0:TOK], o[:, :, :, HD], DEN_EPS, None, ALU.max))
                    link(v.reciprocal(den[0:TOK], den[0:TOK]))
                    g4 = q % 3
                    y4 = y_sb[:, :, 64 * g4:64 * g4 + 64].rearrange("p t (h d) -> p t h d", h=4)
                    for t in range(NT):
                        last = v.tensor_tensor(y4[:, t], o[:, t, :, 0:HD],
                                               den[0:TOK, t].unsqueeze(2).broadcast_to([TOK, 4, HD]), ALU.mult)
                    last.then_inc(y_ready, 1)
                    dve.wait_ge(y_ready, q + 1)
                    dve.sem_inc(slot_free[free_before(u)[0]], 1)
                elif kind == "proj":
                    b = u[1]
                    full(dve, u)
                    dve.wait_ge(h_loaded[b], 16)
                    s = slot(u)
                    for t in range(NT):
                        at = 512 * (t // 2) + D * (t % 2)
                        last = v.tensor_tensor(hres[:, NT * b + t, :], s[0:TOK, at:at + D], hres[:, NT * b + t, :], ALU.add)
                    link(last)
                    dve.sem_inc(slot_free[free_before(u)[0]], 1)
                    dve.sem_inc(h_added, 1)
                    for t in range(NT):
                        last = v.bn_stats(stats2[:, t, :], hres[:, NT * b + t, :])
                    link(last)
                    for t in range(NT):
                        last = v.bn_aggr(mv2[0:TOK, NT * b + t, :], stats2[:, t, :])
                    link(last)
                    s5 = slice(NT * b, NT * (b + 1))
                    link(v.tensor_scalar(var2[0:TOK], mv2[0:TOK, s5, 1], LN_EPS, None, ALU.add))
                    rsqrt(rs2[0:TOK, s5], rs2_t[0:TOK], var2[0:TOK])
                    link(v.scalar_tensor_tensor(out=shift2[0:TOK, s5], in0=mv2[0:TOK, s5, 0], scalar=-1.0, in1=rs2[0:TOK, s5],
                                                op0=ALU.mult, op1=ALU.mult))
                    dve.sem_inc(norm_ready, 1)
                elif kind == "logit":
                    full(dve, u)
                    raw = slot(u)[0:TOK, 0:NT * E].rearrange("p (t e) -> p t e", t=NT)
                    link(v.tensor_reduce(logit_max, raw, AX.X, ALU.max))
                    g = int(u[1] >= GROUPS[1][0])
                    t0 = NT * (u[1] - GROUPS[g][0])
                    v.tensor_tensor(routers[g].cand[:, t0:t0 + NT], raw, logit_max.unsqueeze(2).broadcast_to([TOK, NT, E]),
                                    ALU.subtract).then_inc(shifted, 1)
                    dve.wait_ge(shifted, u[1] + 1)
                    dve.sem_inc(slot_free[free_before(u)[0]], 1)
                elif kind == "pick":
                    choose_first(u[1])
                elif kind == "pick2":
                    choose_second(u[1])
                elif kind == "count":
                    count_rows(u)
                elif kind == "place":
                    place_rows(u[1])
                elif kind == "note":
                    note_tiles(u[1])

            dve.wait_ge(av_done, PAIRS * B)
            v.tensor_copy(eid, eid_f).then_inc(eid_ready, 1)
            v.memset(x_tT[C:C + 1, :, 1, :], 1.0).then_inc(ones_row, 1)
            dve.wait_ge(b2_in, 16)
            dve.wait_ge(eid_ready, 1)
            dve.wait_ge(w1_in, 16 * 2 * E)

            def copy_w1(par, i):
                e = dve.value_load(eid[0:1, bass.ds(i, 1)], min_val=0, max_val=E - 1)
                wait_from_1(dve, hid_full, i - 1)
                v.tensor_copy(w1_now[:, par, 1, :], w1_sb[0:C + 1, bass.ds(e * (2 * F) + F, F)]).then_inc(w1_copied[1], 1)

            def relu_b(par, i):
                dve.wait_ge(hid_full, i + 1)
                wait_from_1(dve, y_full, i - 1)
                v.tensor_scalar(hidT[:, par, 3:6], slots[par][:, 1024:1024 + 3 * P].rearrange("p (k t) -> p k t", k=3),
                                0.0, None, ALU.max).then_inc(hid_copied[1], 1)

            def row_weights(group):
                t = META_GROUPS[group]
                dve.wait_ge(meta_in[group], 16)
                first, mine = meta[:, t, 1], eid_f[:, t]
                v.tensor_copy(dest[:, t], meta[:, t, 0]).then_inc(dest_ready, 1)
                link(v.tensor_tensor(weight[:, t], first, mine, ALU.is_equal))
                link(v.tensor_tensor(weight[:, t], weight[:, t], meta[:, t, 2], ALU.mult))
                link(v.tensor_tensor(weight2[:, t], first, mine, ALU.not_equal))
                link(v.tensor_tensor(weight2[:, t], weight2[:, t], meta[:, t, 3], ALU.mult))
                link(v.tensor_tensor(weight[:, t], weight[:, t], weight2[:, t], ALU.add))

            def weigh_result(par, i, j):
                e = dve.value_load(eid[0:1, bass.ds(i, 1)], min_val=0, max_val=E - 1)
                dve.wait_ge(y_full, i + 1)
                v.tensor_tensor(b2_row, o_ps[:, 512 * par:512 * par + D], b2_bc[:, bass.ds(e * D, D)], ALU.add).then_inc(y_copied, 1)
                dve.wait_ge(y_copied, i + 1)
                wait_from_1(dve, added[par], 16 * j)
                v.tensor_scalar(y_tile[:, par, :], b2_row, weight[:, bass.ds(i, 1)], None, ALU.mult).then_inc(y_out_ready, 1)
                dve.wait_ge(y_out_ready, i + 1)

            def tile_round(par, i, j):
                relu_b(1 - par, i + 1)
                copy_w1(par, i + 2)
                weigh_result(par, i, j)

            copy_w1(0, 0)
            copy_w1(1, 1)
            relu_b(0, 0)
            row_weights(0)
            tile_round(0, 0, 0)
            row_weights(1)
            tile_round(1, 1, 0)
            with dve.Fori(1, TILES // 2 - 1) as j:
                for par in range(2):
                    tile_round(par, 2 * j + par, j)
            relu_b(1, TILES - 1)
            weigh_result(0, TILES - 2, TILES // 2 - 1)
            weigh_result(1, TILES - 1, TILES // 2 - 1)

        @block.tensor
        def _(pe):
            def transposes(u, src, tile0):
                s = slot(u)
                for t in range(NT):
                    for c in range(2):
                        dst = s[0:C, 512 * c + TOK * t:512 * c + TOK * (t + 1)] if t < 4 else \
                            s[0:C, 1024 + TOK * c:1024 + TOK * (c + 1)]
                        last = pe.transpose(dst, src[:, tile0 + t, C * c:C * (c + 1)], ident[0:TOK, 0:TOK])
                last.then_inc(psum_full, 1)

            pe.wait_ge(const_set, 1)
            for u in plan:
                kind = u[0]
                if kind in SLOTTED:
                    take_slot(pe, u)
                    s = slot(u)
                if kind == "rank":
                    pe.wait_ge(diag_ready, u[1] + 1)
                    pe.matmul(s[0:TIN, 0:4 * TIN], ones[0:TIN, 0:TIN], sdiag[:, 0:4, :], start=True, stop=True)
                    flat = sdiag.rearrange("p t j -> p (t j)")
                    pe.matmul(s[0:TIN, 500:512], ones[0:TIN, 0:TIN], flat[:, 500:512], start=True, stop=True)
                    pe.matmul(s[0:TIN, 512:N], ones[0:TIN, 0:TIN], flat[:, 512:N], start=True, stop=True).then_inc(psum_full, 1)
                elif kind == "xT":
                    pe.wait_ge(x_loaded[u[1]], 16)
                    transposes(u, z, NT * u[1])
                elif kind in ("q", "k"):
                    pe.wait_ge(xT_ready, u[1] + 1)
                    pe.wait_ge(w_in, 16 * 8)
                    for two in range(2):
                        for lo, hi, at in ((0, 350, 512 * two), (350, KEEP, 1024 + 175 * two)):
                            for c in range(2):
                                last = pe.matmul(s[0:C, at:at + hi - lo], wqk_sb[:, int(kind == "k"), c, two, :],
                                                 xT[:, c, lo:hi], start=(c == 0), stop=(c == 1))
                    last.then_inc(psum_full, 1)
                elif kind == "v":
                    for t in range(NT):
                        n = min(P, KEEP - P * t)
                        at = 512 * (t // 2) + D * (t % 2)
                        for c in range(2):
                            last = pe.matmul(s[0:n, at:at + D], xT[:, c, P * t:P * t + n], wv_sb[:, c, :],
                                             start=(c == 0), stop=(c == 1))
                    last.then_inc(psum_full, 1)
                elif kind in ("tail", "head"):
                    b = u[1]
                    pe.wait_ge(stack_in[b % 2], 16 * 16 * (b // 2 + 1))
                    qs = stack(b % 2, 0).rearrange("p (h s) -> p h s", h=HEADS)
                    ks = stack(b % 2, 1).rearrange("p (h s) -> p h s", h=HEADS)
                    if kind == "tail":
                        pe.matmul(s[0:TAIL, 0:HEADS * TAIL], ident_b[0:TAIL, 0:TAIL],
                                  tri[0:TAIL, 0:TAIL].unsqueeze(1).broadcast_to([TAIL, HEADS, TAIL]),
                                  start=True, stop=False)
                        for h in range(HEADS):
                            last = pe.matmul(s[0:TAIL, TAIL * h:TAIL * (h + 1)], ks[:, h, 512:KEEP], qs[:, h, 512:KEEP],
                                             start=False, stop=(h == HEADS - 1))
                    else:
                        h = u[2]
                        for kt, q0, n, at in PIECES:
                            c0 = q0 - P * kt
                            m = min(P - c0, n)
                            o0 = RUN0 + at
                            key = ks[:, h, P * kt:P * (kt + 1)]
                            pe.matmul(s[:, o0:o0 + m], ident_b, tri[:, c0:c0 + m], start=True, stop=False)
                            last = pe.matmul(s[:, o0:o0 + m], key, qs[:, h, q0:q0 + m], start=False, stop=True)
                            if m < n:
                                last = pe.matmul(s[:, o0 + m:o0 + n], key, qs[:, h, q0 + m:q0 + n], start=True, stop=True)
                    last.then_inc(psum_full, 1)
                elif kind == "av":
                    _, pair, m = u
                    b, h0 = pair // PAIRS, 2 * (pair % PAIRS)
                    if m == 0:
                        pe.wait_ge(v_ready, b + 1)
                        pe.wait_ge(sig_ready, nonlinear_of[("head", b, h0 + 1)] + 1)
                        if pair >= 2:
                            pe.wait_ge(o_ready, pair // 2)
                    for n, (kt, q0, width, at) in enumerate(PIECES):
                        o0 = 512 + q0 - S0 if q0 >= S0 else q0
                        for h in (h0, h0 + 1):
                            row = 32 * (h % 4)
                            pe.matmul(o_ps[row:row + HD + 1, o0:o0 + width], v_mix5[:, m, kt, h, :], sig[:, h % 4, m, at:at + width],
                                      start=(m == 0 and (n == 0 or q0 < S0)), stop=(m == 1 and q0 < S0))
                    if m == 1:
                        pe.wait_ge(sig_ready, nonlinear_of[("tail", b)] + 1)
                        for i in range(2):
                            for h in (h0, h0 + 1):
                                row = 32 * (h % 4)
                                last = pe.matmul(o_ps[row:row + HD + 1, 512 + 512 - S0:512 + KEEP - S0],
                                                 v_mix5[0:TAIL, i, 4, h, :], g_tail[:, i, h, :], start=False, stop=(i == 1))
                        last.then_inc(av_done, 1)
                elif kind == "oT":
                    q = u[1]
                    pe.wait_ge(o_ready, q + 1)
                    for t in range(NT):
                        last = pe.transpose(s[0:TOK, P * t:P * (t + 1)], o_sb[:, q % 2, TOK * t:TOK * (t + 1)], ident[:, :])
                    last.then_inc(psum_full, 1)
                elif kind == "yT":
                    pe.wait_ge(y_ready, 3 * (u[1] + 1))
                    transposes(u, y_sb, 0)
                elif kind == "proj":
                    pe.wait_ge(yT_ready, u[1] + 1)
                    for t in range(NT):
                        at = 512 * (t // 2) + D * (t % 2)
                        for c in range(2):
                            last = pe.matmul(s[0:TOK, at:at + D], yT[:, c, TOK * t:TOK * (t + 1)], wp_sb[:, c, :],
                                             start=(c == 0), stop=(c == 1))
                    last.then_inc(psum_full, 1)
                elif kind == "zT":
                    pe.wait_ge(z_ready, u[1] + 1)
                    transposes(u, z, NT * u[1])
                elif kind == "count":
                    pe.wait_ge(hot_ready, u[1] + 1)
                    flat = routers[u[1]].both.rearrange("p t e -> p (t e)")
                    n = routers[u[1]].n * E
                    pe.matmul(s[0:TOK, 0:n], before[:, :], flat, start=True, stop=True)
                    pe.matmul(s[:, 512:512 + n], ones[0:TOK, :], flat, start=True, stop=True).then_inc(psum_full, 1)
                elif kind == "logit":
                    pe.wait_ge(zT_ready, u[1] + 1)
                    for t in range(NT):
                        for c in range(2):
                            last = pe.matmul(s[0:TOK, E * t:E * (t + 1)], yT[:, c, TOK * t:TOK * (t + 1)], wg_sb[:, c, :],
                                             start=(c == 0), stop=(c == 1))
                    last.then_inc(psum_full, 1)

            for sl in range(2):
                pe.wait_ge(slot_free[sl], (len(unit_of) + 1 - sl) // 2)
            pe.wait_ge(eid_ready, 1)
            pe.wait_ge(w1_in, 16 * 2 * E)
            pe.wait_ge(w2_in, 16 * E)
            pe.wait_ge(ones_row, 1)
            pe.wait_ge(o_ready, 3 * B)

            def transpose_in(par, i, j):
                pe.wait_ge(tile_in[par], 16 * (j + 1))
                wait_from_1(pe, tT_ready, i - 1)
                pe.transpose(slots[par][0:C, 0:P], x_tile[:, par, 0:C], ident[:, :])
                pe.transpose(slots[par][0:C, P:2 * P], x_tile[:, par, C:D], ident[:, :]).then_inc(tT_full, 1)

            def multiply_w1(par, i):
                pe.wait_ge(tT_ready, i + 1)
                for half in range(2):
                    pe.wait_ge(w1_copied[half], i + 1)
                    wait_from_1(pe, hid_copied[half], i - 1)
                for f in range(F // P):
                    at = 512 * (1 + f // 3) + P * (f % 3)
                    for c, k in ((0, C), (1, C + 1)):
                        last = pe.matmul(slots[par][:, at:at + P], w1_now[0:k, par, c, P * f:P * (f + 1)], x_tT[0:k, par, c, :],
                                         start=(c == 0), stop=(c == 1))
                last.then_inc(hid_full, 1)

            def multiply_w2(par, i):
                e = pe.value_load(eid[0:1, bass.ds(i, 1)], min_val=0, max_val=E - 1)
                for half in range(2):
                    pe.wait_ge(hid_copied[half], i + 1)
                wait_from_1(pe, y_copied, i - 1)
                for k in range(F // P):
                    last = pe.matmul(o_ps[:, 512 * par:512 * par + D], hidT[:, par, k, :],
                                     w2_sb[:, bass.ds(e * (6 * D) + k * D, D)], start=(k == 0), stop=(k == F // P - 1))
                last.then_inc(y_full, 1)

            def tile_round(par, i, j):
                transpose_in(par, i + 2, j + 1)
                multiply_w1(1 - par, i + 1)
                multiply_w2(par, i)

            transpose_in(0, 0, 0)
            transpose_in(1, 1, 0)
            multiply_w1(0, 0)
            tile_round(0, 0, 0)
            tile_round(1, 1, 0)
            with pe.Fori(1, TILES // 2 - 1) as j:
                for par in range(2):
                    tile_round(par, 2 * j + par, j)
            multiply_w1(1, TILES - 1)
            multiply_w2(0, TILES - 2)
            multiply_w2(1, TILES - 1)


def kernel(x, L0_tok_gamma, L0_tok_beta, L0_tok_w, L0_tok_b, L0_attn_Wq, L0_attn_Wk, L0_attn_Wv, L0_attn_Wproj,
           L0_ffn_Wg, L0_ffn_W1, L0_ffn_b1, L0_ffn_W2, L0_ffn_b2):
    import concourse.bacc as bacc
    from concourse.bass_utils import run_bass_kernel_spmd

    def chunks(w):
        return np.ascontiguousarray(np.asarray(w).reshape(D, 2, C).transpose(2, 1, 0))

    def rotary_chunks(w):
        return np.ascontiguousarray(np.asarray(w).reshape(HEADS, HALF, 2, 2, C).transpose(4, 3, 2, 1, 0)).reshape(C, 2, 2, C)

    freq = (np.float32(1.0) / np.float32(10000.0) ** (np.arange(HALF, dtype=np.float32) / np.float32(HALF))).astype(np.float32)
    angle = (np.repeat(freq, HEADS)[:, None] * np.arange(KEEP, dtype=np.float32)[None, :]).astype(np.float32)
    arrays = {
        "x": x, "gamma": L0_tok_gamma, "beta": L0_tok_beta, "w": L0_tok_w, "b_score": L0_tok_b,
        "wqT": rotary_chunks(L0_attn_Wq), "wkT": rotary_chunks(L0_attn_Wk),
        "wvT": chunks(L0_attn_Wv), "wpT": chunks(L0_attn_Wproj),
        "wg": L0_ffn_Wg, "w1": L0_ffn_W1, "b1": L0_ffn_b1, "w2": L0_ffn_W2, "b2": L0_ffn_b2,
        "rope_cos": np.cos(angle), "rope_sin": np.sin(angle), "count": np.arange(TILES, dtype=np.float32),
        "token_no": np.concatenate([np.arange(P)[:, None] + TOK * np.arange(NTA)[None, :], ROWS + np.arange(P)[:, None]],
                                   axis=1).astype(np.float32),
    }
    nc = bacc.Bacc("TRN2", target_bir_lowering=False, num_devices=1)
    arrays = {k: np.ascontiguousarray(a) for k, a in arrays.items()}
    args = [nc.dram_tensor(k, a.shape, mybir.dt.from_np(a.dtype), kind="ExternalInput").ap() for k, a in arrays.items()]
    out = nc.dram_tensor("out", (B, KEEP, D), F32, kind="ExternalOutput").ap()
    build_program(nc, *args, out)
    result = run_bass_kernel_spmd(nc, [arrays], core_ids=[0])
    return result.results[0]["out"]
```
